# Optimizing a Trainium2 kernel written in Bass

```python
import numpy as np
import jax
import jax.numpy as jnp

def _softmax(x, axis=-1):
    return jax.nn.softmax(x, axis=axis)

def _gelu(x):
    return jax.nn.gelu(x, approximate=True)

def _silu(x):
    return jax.nn.silu(x)

def _sigmoid(x):
    return jax.nn.sigmoid(x)

def _layernorm(x, axis=-1, eps=1e-05):
    m = jnp.mean(x, axis=axis, keepdims=True)
    v = jnp.var(x, axis=axis, keepdims=True)
    return (x - m) / jnp.sqrt(v + eps)

def _scatter_add(tgt, idx, src, axis=0):
    return tgt.at[idx].add(src)

def _segment_sum(src, seg, n):
    return jax.ops.segment_sum(src, seg, n)
kernel_name = 'mk_recurrent_d2_jaxref_r8_ea4c8f'

def setup_inputs(seed: int=0):
    np.random.seed(seed)
    _w = jnp.asarray

    def _L0_attn_setup():
        import jax, jax.numpy as jnp
        import numpy as np
        B, S, D_IN, D, H = (2, 256, 128, 128, 16)
        HD = D // H
        key = jax.random.key(seed)
        k1, k2, k3 = jax.random.split(key, 3)
        lim_qkv = float(np.sqrt(6.0 / (D_IN + 3 * D)))
        lim_o = float(np.sqrt(6.0 / (D + D)))
        return {'x': jax.random.normal(k1, (B, S, D_IN), dtype=jnp.float32), 'w_qkv': jax.random.uniform(k2, (3 * D, D_IN), dtype=jnp.float32, minval=-lim_qkv, maxval=lim_qkv), 'b_qkv': jnp.zeros((3 * D,), dtype=jnp.float32), 'w_o': jax.random.uniform(k3, (D, D), dtype=jnp.float32, minval=-lim_o, maxval=lim_o), 'b_o': jnp.zeros((D,), dtype=jnp.float32)}
    _L0_attn_in = _L0_attn_setup()

    def _L0_ffn_setup():
        import jax, jax.numpy as jnp
        import numpy as np
        LN_EPS = 1e-05

        def layer_norm(x, g, b):
            mu = jnp.mean(x, axis=-1, keepdims=True)
            var = jnp.var(x, axis=-1, keepdims=True)
            return (x - mu) / jnp.sqrt(var + LN_EPS) * g + b

        def balanced_assignment(scores):
            T, E = scores.shape
            C = T // E
            taken = jnp.zeros((T,), dtype=bool)
            parts = []
            for e in range(E):
                s = jnp.where(taken, -jnp.inf, scores[:, e])
                _, idx = jax.lax.top_k(s, C)
                parts.append(idx)
                taken = taken.at[idx].set(True)
            return jnp.concatenate(parts)
        key = jax.random.key(seed)
        ks = jax.random.split(key, 4)
        B, S, D, F, E = (4, 256, 128, 512, 8)
        return {'x': jax.random.normal(ks[0], (B, S, D), dtype=jnp.float32), 'centroids': jax.random.normal(ks[1], (E, D), dtype=jnp.float32) * 0.1, 'ln_g': jnp.ones((D,), dtype=jnp.float32), 'ln_b': jnp.zeros((D,), dtype=jnp.float32), 'w1': jax.random.normal(ks[2], (E, D, F), dtype=jnp.float32) * 0.02, 'b1': jnp.zeros((E, F), dtype=jnp.float32), 'w2': jax.random.normal(ks[3], (E, F, D), dtype=jnp.float32) * 0.02, 'b2': jnp.zeros((E, D), dtype=jnp.float32)}
    _L0_ffn_in = _L0_ffn_setup()

    def _L1_attn_setup():
        import jax, jax.numpy as jnp
        import numpy as np
        HEADS = 16
        key = jax.random.key(seed)
        k1, k2, k3, k4 = jax.random.split(key, 4)
        C, T, E = (8, 512, 128)
        D = E // HEADS
        x = jax.random.normal(k1, (C, T, E), dtype=jnp.float32)
        Wq = jax.random.normal(k2, (D, D), dtype=jnp.float32) * (1.0 / np.sqrt(D))
        Wk = jax.random.normal(k3, (D, D), dtype=jnp.float32) * (1.0 / np.sqrt(D))
        Wv = jax.random.normal(k4, (D, D), dtype=jnp.float32) * (1.0 / np.sqrt(D))
        return {'x': x, 'Wq': Wq, 'Wk': Wk, 'Wv': Wv}
    _L1_attn_in = _L1_attn_setup()

    def _L1_ffn_setup():
        import jax, jax.numpy as jnp
        import numpy as np
        E = 8
        D = 128
        H = 256
        TOP_K = 2
        key = jax.random.key(seed)
        k_x, k_g, k_w1, k_w2 = jax.random.split(key, 4)
        B, S = (4, 256)
        inp = {'input': jax.random.normal(k_x, (B, S, D), dtype=jnp.float32), 'Wg': jax.random.normal(k_g, (D, E), dtype=jnp.float32) * 0.02, 'W1': jax.random.normal(k_w1, (E, D, H), dtype=jnp.float32) * 0.02, 'b1': jnp.zeros((E, H), dtype=jnp.float32), 'W2': jax.random.normal(k_w2, (E, H, D), dtype=jnp.float32) * 0.02, 'b2': jnp.zeros((E, D), dtype=jnp.float32)}
        return inp
    _L1_ffn_in = _L1_ffn_setup()
    _d = {'L0_attn_x': _L0_attn_in['x'], 'L0_attn_w_qkv': _L0_attn_in['w_qkv'], 'L0_attn_b_qkv': _L0_attn_in['b_qkv'], 'L0_attn_w_o': _L0_attn_in['w_o'], 'L0_attn_b_o': _L0_attn_in['b_o'], 'L0_ffn_centroids': _L0_ffn_in['centroids'], 'L0_ffn_ln_g': _L0_ffn_in['ln_g'], 'L0_ffn_ln_b': _L0_ffn_in['ln_b'], 'L0_ffn_w1': _L0_ffn_in['w1'], 'L0_ffn_b1': _L0_ffn_in['b1'], 'L0_ffn_w2': _L0_ffn_in['w2'], 'L0_ffn_b2': _L0_ffn_in['b2'], 'L1_attn_Wq': _L1_attn_in['Wq'], 'L1_attn_Wk': _L1_attn_in['Wk'], 'L1_attn_Wv': _L1_attn_in['Wv'], 'L1_ffn_Wg': _L1_ffn_in['Wg'], 'L1_ffn_W1': _L1_ffn_in['W1'], 'L1_ffn_b1': _L1_ffn_in['b1'], 'L1_ffn_W2': _L1_ffn_in['W2'], 'L1_ffn_b2': _L1_ffn_in['b2']}
    _x0 = _d['L0_attn_x']
    _d['L0_attn_x'] = jax.random.normal(jax.random.fold_in(jax.random.key(seed), 1), (16, 256, 128), dtype=_x0.dtype)
    del _x0
    return _d

def reference(L0_attn_x, L0_attn_w_qkv, L0_attn_b_qkv, L0_attn_w_o, L0_attn_b_o, L0_ffn_centroids, L0_ffn_ln_g, L0_ffn_ln_b, L0_ffn_w1, L0_ffn_b1, L0_ffn_w2, L0_ffn_b2, L1_attn_Wq, L1_attn_Wk, L1_attn_Wv, L1_ffn_Wg, L1_ffn_W1, L1_ffn_b1, L1_ffn_W2, L1_ffn_b2):

    def _L0_attn_ref(x, w_qkv, b_qkv, w_o, b_o):
        import jax, jax.numpy as jnp
        import numpy as np
        B, S, D_IN, D, H = (2, 256, 128, 128, 16)
        HD = D // H
        b, s, _ = x.shape
        qkv = jnp.einsum('bsd,ed->bse', x, w_qkv) + b_qkv
        qkv = qkv.reshape(b, s, H, 3 * HD).transpose(0, 2, 1, 3)
        q, k, v = jnp.split(qkv, 3, axis=-1)
        scale = 1.0 / jnp.sqrt(jnp.asarray(HD, dtype=q.dtype))
        logits = jnp.einsum('bhqd,bhkd->bhqk', q, k) * scale
        attn = jax.nn.softmax(logits, axis=-1)
        vals = jnp.einsum('bhqk,bhkd->bhqd', attn, v)
        vals = vals.transpose(0, 2, 1, 3).reshape(b, s, D)
        return jnp.einsum('bsd,ed->bse', vals, w_o) + b_o

    def _L0_ffn_ref(x, centroids, ln_g, ln_b, w1, b1, w2, b2):
        import jax, jax.numpy as jnp
        import numpy as np
        LN_EPS = 1e-05

        def layer_norm(x, g, b):
            mu = jnp.mean(x, axis=-1, keepdims=True)
            var = jnp.var(x, axis=-1, keepdims=True)
            return (x - mu) / jnp.sqrt(var + LN_EPS) * g + b

        def balanced_assignment(scores):
            T, E = scores.shape
            C = T // E
            taken = jnp.zeros((T,), dtype=bool)
            parts = []
            for e in range(E):
                s = jnp.where(taken, -jnp.inf, scores[:, e])
                _, idx = jax.lax.top_k(s, C)
                parts.append(idx)
                taken = taken.at[idx].set(True)
            return jnp.concatenate(parts)
        D = x.shape[-1]
        feat = x.reshape(-1, D)
        T = feat.shape[0]
        E = centroids.shape[0]
        C = T // E
        norm = layer_norm(feat, ln_g, ln_b)
        scores = jax.lax.stop_gradient(norm @ centroids.T)
        sort_by_expert = balanced_assignment(scores)
        routed = feat[sort_by_expert].reshape(E, C, D)
        h = layer_norm(routed, ln_g, ln_b)
        h = jax.nn.gelu(jnp.einsum('ecd,edf->ecf', h, w1) + b1[:, None, :])
        h = jnp.einsum('ecf,efd->ecd', h, w2) + b2[:, None, :]
        out = routed + h
        inv = jnp.zeros((T,), dtype=jnp.int32).at[sort_by_expert].set(jnp.arange(T, dtype=jnp.int32))
        return out.reshape(T, D)[inv].reshape(x.shape)

    def _L1_attn_ref(x, Wq, Wk, Wv):
        import jax, jax.numpy as jnp
        import numpy as np
        HEADS = 16
        C, T, E = x.shape
        H = HEADS
        D = E // H
        xr = x.reshape(C, T, H, D)
        q = jnp.einsum('cthd,ed->cthe', xr, Wq)
        k = jnp.einsum('cthd,ed->cthe', xr, Wk)
        v = jnp.einsum('cthd,ed->cthe', xr, Wv)
        diag_scores = jnp.einsum('cthd,cthd->cth', q, k) / jnp.sqrt(jnp.asarray(E, x.dtype))
        probs = jax.nn.softmax(diag_scores, axis=0)
        vsum = v.sum(axis=1)
        attn = probs[..., None] * vsum[:, None, :, :]
        return attn.reshape(C, T, E)

    def _L1_ffn_ref(input, Wg, W1, b1, W2, b2):
        import jax, jax.numpy as jnp
        import numpy as np
        E = 8
        D = 128
        H = 256
        TOP_K = 2
        logits = jnp.einsum('bsd,de->bse', input, Wg)
        probs = jax.nn.softmax(logits, axis=-1)
        top_vals, top_idx = jax.lax.top_k(probs, TOP_K)
        top_vals = top_vals / jnp.sum(top_vals, axis=-1, keepdims=True)
        onehot = jax.nn.one_hot(top_idx, E, dtype=input.dtype)
        mask = jnp.sum(onehot, axis=2)
        scores = jnp.sum(onehot * top_vals[..., None], axis=2)
        xm = input[None] * jnp.moveaxis(mask, -1, 0)[..., None]
        h = jnp.einsum('ebsd,edh->ebsh', xm, W1) + b1[:, None, None, :]
        h = jax.nn.relu(h)
        y = jnp.einsum('ebsh,ehd->ebsd', h, W2) + b2[:, None, None, :]
        out = jnp.sum(y * jnp.moveaxis(scores, -1, 0)[..., None], axis=0)
        return out
    x = L0_attn_x
    xn = _layernorm(x, axis=-1)
    s = _L0_attn_ref(xn, L0_attn_w_qkv, L0_attn_b_qkv, L0_attn_w_o, L0_attn_b_o)
    g = _silu(_L0_ffn_ref(xn, L0_ffn_centroids, L0_ffn_ln_g, L0_ffn_ln_b, L0_ffn_w1, L0_ffn_b1, L0_ffn_w2, L0_ffn_b2))
    x = x + s * g
    xn = _layernorm(x, axis=-1)
    s = _L1_attn_ref(xn, L1_attn_Wq, L1_attn_Wk, L1_attn_Wv)
    g = _silu(_L1_ffn_ref(xn, L1_ffn_Wg, L1_ffn_W1, L1_ffn_b1, L1_ffn_W2, L1_ffn_b2))
    x = x + s * g
    return x

_drawn_inputs = setup_inputs


def setup_inputs(seed=0):
    import zlib

    import numpy as np

    out = dict(_drawn_inputs(seed))
    spreads = {'L0_attn_b_qkv': (0.0, 0.1),
     'L0_attn_b_o': (0.0, 0.1),
     'L0_ffn_ln_g': (1.0, 0.6),
     'L0_ffn_ln_b': (0.0, 0.8),
     'L0_ffn_b1': (0.0, 0.8),
     'L0_ffn_b2': (0.0, 0.696),
     'L1_ffn_b1': (0.0, 0.79),
     'L1_ffn_b2': (0.0, 0.1)}
    factors = {'L0_ffn_centroids': 4.742,
     'L0_ffn_w1': 8.0,
     'L0_ffn_w2': 7.854,
     'L1_attn_Wq': 4.07,
     'L1_attn_Wk': 3.657,
     'L1_ffn_W1': 2.857}
    for name, (base, spread) in spreads.items():
        noise = np.random.default_rng([zlib.crc32(name.encode()), seed]).standard_normal(out[name].shape)
        drawn = base * np.exp(spread * noise) if base else spread * noise
        out[name] = jnp.asarray(drawn.astype(out[name].dtype))
    for name, factor in factors.items():
        out[name] = (out[name] * factor).astype(out[name].dtype)
    return out
```

```python
from contextlib import ExitStack

import numpy as np

import concourse.bass as bass
from concourse import mybir

F32, BF16, F16 = mybir.dt.float32, mybir.dt.bfloat16, mybir.dt.float16
I32, U32, U16 = mybir.dt.int32, mybir.dt.uint32, mybir.dt.uint16
ALU, ACT, AX = mybir.AluOpType, mybir.ActivationFunctionType, mybir.AxisListType

P = 128
B, S, D = 16, 256, 128
H, HD = 16, 8
TOK = B * S
NT = TOK // P
GT = 4
GN = GT * P
NG = NT // GT
E0, F0 = 8, 512
CAP = TOK // E0
E1, H1 = 8, 256
EPS = 1e-5
REP = 16
ROUNDS = 4
HALF = 65536.0
STEPS = [float(REP ** (ROUNDS - 1 - r)) for r in range(ROUNDS)]
DONE = [sum(STEPS[:r]) for r in range(ROUNDS + 1)]
SLOTS_Q = (0, 0, 0, 1, 1, 2)
SLOTS_K = (0, 1, 2, 0, 1, 0)
KROWS = 96
MROW = 96
STACK = 2


def host_constants():
    p = np.arange(P)
    j = (p % REP).astype(np.float64)
    cols = [j * STEPS[0] * HALF] + [(j * STEPS[r] - DONE[r]) * HALF for r in range(1, ROUNDS)]
    cols += [j * STEPS[0]] + [j * STEPS[r] - DONE[r] for r in range(1, ROUNDS)]
    first = (p % REP == 0)[:, None]
    earlier = first & (p[:, None] // REP < p[None, :] // REP)
    low = np.tril(np.ones((E1, E1)), -1)[None].repeat(P, 0)
    return {
        "c_ident": np.eye(P, dtype=np.float32),
        "c_block": (p[:, None] // HD == p[None, :] // HD).astype(np.float32),
        "c_thr": np.stack(cols, 1).astype(np.float32),
        "c_pick": (p[:, None] % REP == np.arange(REP)[None]).astype(np.float16),
        "c_nge": (-1.0 * first * np.ones((1, P))).astype(np.float16),
        "c_neq": (1.0 * first - 1.0 * earlier).astype(np.float16),
        "c_tri": (p[:, None] < p[None, :]).astype(np.float16),
        "c_low": low.reshape(P, E1 * E1).astype(np.float32),
    }


class Chain:

    def __init__(self, engine, sem):
        self.engine, self.sem, self.base, self.n = engine, sem, 0, 0

    def link(self, ins):
        ins.then_inc(self.sem, 1)
        self.n += 1
        self.engine.wait_ge(self.sem, self.base + self.n)

    def loop(self, i, per):
        self.start, self.per, self.base = self.n, per, i * per

    def end(self, rounds):
        assert self.n - self.start == self.per, f"{self.n - self.start} links in a round"
        self.base, self.n = 0, self.start + self.per * rounds


def flat(ap):
    return ap.rearrange("p a n -> p (a n)")


def two_layers(nc, a, out):
    with ExitStack() as ctx:
        def sb(name, shape, dt=F32):
            return ctx.enter_context(nc.sbuf_tensor(name, shape, dt))

        def sem(name):
            return ctx.enter_context(nc.semaphore(name))

        bank = [ctx.enter_context(nc.psum_tensor(f"bank{i}", [P, 512], F32)) for i in range(8)]

        ident, block_mask = sb("ident", [P, P]), sb("block_mask", [P, P])
        ident_b, ident_h = sb("ident_b", [P, P], BF16), sb("ident_h", [P, P], F16)
        thr = sb("thr", [P, 2 * ROUNDS])
        pick, nge = sb("pick", [P, REP], F16), sb("nge", [P, P], F16)
        neq, tri = sb("neq", [P, P], F16), sb("tri", [P, P], F16)
        low = sb("low", [P, E1, E1])
        ones_h, ones_f = sb("ones_h", [P, GN], F16), sb("ones_f", [P, P])
        w_q, w_k, w_v, w_o = (sb(n, [P, P]) for n in ("w_q", "w_k", "w_v", "w_o"))
        b_qk, b_v, b_o = sb("b_qk", [P, 2]), sb("b_v", [P, P]), sb("b_o", [P, P])
        cent, ln_gb = sb("cent", [P, E0]), sb("ln_gb", [P, 2])
        x_all = sb("x_all", [P, NT, D])
        xn_all = sb("xn_all", [P, NT, D])
        s_all = sb("s_all", [P, NT, D])
        v_all = sb("v_all", [P, NT, D])
        arena = sb("arena", [P, 12288])
        STACKS_END = STACK * 2 * H * S // 2
        stacks = arena[:, 0:STACKS_END].bitcast(BF16).rearrange("p (s w h t) -> p s w h t", s=STACK, w=2, h=H)
        keys = sb("keys", [P, 2, E0 - 1, GN], U16)
        stat6, mean, var = sb("stat6", [P, NT, 6]), sb("mean", [P, NT]), sb("var", [P, NT])
        tmp_s, rstd, rstd2, zscale = (sb(n, [P, NT]) for n in ("tmp_s", "rstd", "rstd2", "zscale"))
        half_neg = sb("half_neg", [P, NT])
        xst, zst = sb("xst", [P, 2, GT, D]), sb("zst", [P, 2, GT, D])
        parts_sb = sb("parts_sb", [P, 2 * 3 * 2 * 512], BF16)
        pool_tile = sb("pool_tile", [P, 8, 512])
        xT, zT = pool_tile[:, 0:2, :], pool_tile[:, 2:4, :]
        qkf = pool_tile[:, 4:8, :].rearrange("p (a w) n -> p a w n", a=2)
        probs = pool_tile
        parts = parts_sb[:, :].rearrange("p (a i w n) -> p a i w n", a=2, i=3, w=2)
        sT = s_all[0:E0, :, :].rearrange("p t d -> p (t d)")
        v_b = sb("v_b", [P, 2, 2, H, 32])
        o_b = sb("o_b", [P, 2, 4, S])
        vals, vT = sb("vals", [P, 2, P]), sb("vT", [P, 2, P])
        rec = sb("rec", [P, 2, H])
        mx = sb("mx", [P, H, 2])
        nm = sb("nm", [P, P], BF16)
        nmT = sb("nmT", [P, P], BF16)
        khi, key2 = sb("khi", [P, GN]), sb("key2", [P, GN])
        junk, ge, eq, pre = (sb(n, [P, GN], F16) for n in ("junk", "ge", "eq", "pre"))
        avail, eid = sb("avail", [P, GN], F16), sb("eid", [P, GN], F16)
        cnt = sb("cnt", [P, 3], F16)
        junk16 = sb("junk16", [P, REP])
        st = sb("st", [P, 6])
        T, L, BASE, DIG, QUOTA = (st[:, i:i + 1] for i in range(5))
        eidT = sb("eidT", [P, NT])
        hot = sb("hot", [P, E0, NT], F16)
        key_f, key_h = khi[:, 0:S], khi[:, S:2 * S].bitcast(U16).rearrange("p (w f) -> p w f", w=2)
        tot, posa = khi[:, 0:E0 * NT], khi[:, E0 * NT:2 * E0 * NT]
        pos_f, pos = sb("pos_f", [P, NT]), sb("pos", [P, NT], I32)

        def dram(name, shape, dt=F32):
            return nc.dram_tensor(name, shape, dt).ap()
        d_parts = dram("d_parts", [3, 2, P, TOK], BF16)
        d_score = dram("d_score", [E0, TOK])
        d_keys = dram("d_keys", [2, E0 * REP, S], U16)
        d_sorted, d_ffn = dram("d_sorted", [TOK, D]), dram("d_ffn", [TOK, D])

        def carve(start, *shape):
            n = int(np.prod(shape))
            names = "abcd"[:len(shape)]
            dims = {c: k for c, k in zip(names, shape)}
            return arena[:, start:start + n].rearrange(f"p ({' '.join(names)}) -> p {' '.join(names)}", **dims)
        w1e, w2e = carve(0, 2, F0), carve(1024, 2, 4, D)
        zl, nT = carve(2048, 2, GT, D), carve(3072, 2, GN)
        hT, ho = carve(4096, 2, 4, GN), carve(8192, 2, GT, D)
        b1e, b2e = carve(9216, 2, 4), carve(9224, 2, D)
        xT_all, w1m, w2m = carve(0, NG, GN), carve(4096, E1, H1), carve(6144, E1, 2, D)
        hm, vsum = carve(8192, 2, 2, GN), carve(10240, B, D)
        routed = v_all
        wqkv8 = sb("wqkv8", [8, 4, D])
        bd_a, bd_v = sb("bd_a", [P, P]), sb("bd_v", [P, P])
        w_g, b1m, b2m = sb("w_g", [P, E1]), sb("b1m", [P, E1, 2]), sb("b2m", [E1, D])
        xsum = sb("xsum", [P, B])
        vrhs = sb("vrhs", [P, 2, D])
        late = o_b[:, :, :, :].rearrange("p a b n -> p (a b n)")
        ds = late[:, 0:NT * H].rearrange("p (t h) -> p t h", t=NT)
        gl = late[:, 512:512 + NT * E1].rearrange("p (t e) -> p t e", t=NT)
        scm = late[:, 768:768 + 2 * GT * E1].rearrange("p (a t e) -> p a t e", a=2, t=GT)
        scT = late[0:E1, 1024:1024 + 2 * GN].rearrange("p (a n) -> p a n", a=2)
        small = sb("small", [P, NT])
        hmax = sb("hmax", [P, 2 * H])
        pairs = pool_tile[:, 0:4, :].rearrange("p a n -> p (a n)").rearrange("p (t e f) -> p t e f", t=NT, e=E1)
        pairs2 = pool_tile[:, 4:8, :].rearrange("p a n -> p (a n)").rearrange("p (t e f) -> p t e f", t=NT, e=E1)
        x1T = pool_tile[:, 0:2, :]
        acc, gate = xst, zst
        outs = pool_tile[:, 4:8, :].rearrange("p a (t d) -> p a t d", t=GT)

        x_in = [sem(f"x_in{g}") for g in range(NG)]
        w_in, chain_s, pool_s = sem("w_in"), sem("dve_chain"), sem("pool_chain")
        idents, zeroed, var_ok, rstd_ok = sem("idents"), sem("zeroed"), sem("var_ok"), sem("rstd_ok")
        st_ready, xn_copied, tr_done, t_evac = sem("st_ready"), sem("xn_copied"), sem("tr_done"), sem("t_evac")
        proj_done, qk_evac, v_evac, sc_evac = sem("proj_done"), sem("qk_evac"), sem("v_evac"), sem("sc_evac")
        part1, rest1, part2, split_done = sem("part1"), sem("rest1"), sem("part2"), sem("split_done")
        parts_out, score_out, score_in = sem("parts_out"), sem("score_out"), sem("score_in")
        key_ready, key_out, keys_in = sem("key_ready"), sem("key_out"), sem("keys_in")
        stack_in, mx_ready, mx_free = sem("stack_in"), sem("mx_ready"), sem("mx_free")
        nm_ready, nm_tr, nm_evac, nm_in = sem("nm_ready"), sem("nm_tr"), sem("nm_evac"), sem("nm_in")
        v_ready, lt_ready, lt_free = sem("v_ready"), sem("lt_ready"), sem("lt_free")
        pv_done, pv_free = sem("pv_done"), sem("pv_free")
        cnt_ready, cnt_sum, fin_ready, fin_sum = sem("cnt_ready"), sem("cnt_sum"), sem("fin_ready"), sem("fin_sum")
        ot_done, vals_ready, vt_done, vt_evac = sem("ot_done"), sem("vals_ready"), sem("vt_done"), sem("vt_evac")
        s_done, s_evac = sem("s_done"), sem("s_evac")
        eid_ready, eid_tr, hot_ready, pos_mm = sem("eid_ready"), sem("eid_tr"), sem("hot_ready"), sem("pos_mm")
        z_ready, pos_ready, scattered, gathered = sem("z_ready"), sem("pos_ready"), sem("scattered"), sem("gathered")
        e_in = [sem("e_in0"), sem("e_in1")]
        zt_done, nt_ready, h_done, h_evac = sem("zt_done"), sem("nt_ready"), sem("h_done"), sem("h_evac")
        y_done, y_evac, ffn_out = sem("y_done"), sem("y_evac"), sem("ffn_out")
        gin_ready, silu_done = sem("gin_ready"), sem("silu_done")
        m_in, var1_ok, rstd1_ok, w8_done, w8_evac = (
            sem("m_in"), sem("var1_ok"), sem("rstd1_ok"), sem("w8_done"), sem("w8_evac"))
        st1_ready, tr1_done, x1_evac, x1_copied = sem("st1_ready"), sem("tr1_done"), sem("x1_evac"), sem("x1_copied")
        yg_done, yg_evac = sem("yg_done"), sem("yg_evac")
        lg_ready, exp_done, vrhs_ready, vs_mm, vs_evac = (
            sem("lg_ready"), sem("exp_done"), sem("vrhs_ready"), sem("vs_mm"), sem("vs_evac"))
        sct_in, sct_done, sct_evac, b2_done = sem("sct_in"), sem("sct_done"), sem("sct_evac"), sem("b2_done")
        hm_done, hm_evac, ym_done, ym_free = sem("hm_done"), sem("hm_evac"), sem("ym_done"), sem("ym_free")
        acc_ready, gate_done, out_ready, stored = sem("acc_ready"), sem("gate_done"), sem("out_ready"), sem("stored")

        x_t = a["x"].rearrange("(n p) d -> p n d", p=P)
        out_t = out.rearrange("(n p) d -> p n d", p=P)
        sorted_t = d_sorted.rearrange("(n p) d -> p n d", p=P)
        ffn_t = d_ffn.rearrange("(n p) d -> p n d", p=P)
        first_loads = [
            (ident[:, :], a["c_ident"]), (block_mask[:, :], a["c_block"]), (thr[:, :], a["c_thr"]),
            (pick[:, :], a["c_pick"]), (nge[:, :], a["c_nge"]), (neq[:, :], a["c_neq"]), (tri[:, :], a["c_tri"]),
            (low[:, :, :].rearrange("p a b -> p (a b)"), a["c_low"]),
            (w_q[:, :], a["w_q"]), (w_k[:, :], a["w_k"]), (w_v[:, :], a["w_v"]), (w_o[:, :], a["w_o"]),
            (cent[:, :], a["cent"]), (b_qk[:, 0:1], a["b_q"]), (b_qk[:, 1:2], a["b_k"]),
            (ln_gb[:, 0:1], a["ln_g"]), (ln_gb[:, 1:2], a["ln_b"]),
            (b_v[:, :], a["b_v"].broadcast_to([P, P])), (b_o[:, :], a["b_o"].broadcast_to([P, P])),
            (w_g[:, :], a["w_g"]), (b1m[:, :, :].rearrange("p e t -> p (e t)"), a["b1m"]), (b2m[:, :], a["b2m"]),
            (wqkv8[:, :, :].rearrange("p a n -> p (a n)"), a["w8"]),
        ]
        W_ALL = 16 * len(first_loads)
        HALF_LOAD = 16 * (len(SLOTS_Q) + len(SLOTS_K))
        ROUNDS_A = NG // 2
        PAIRS = (B - 2) // 2
        LT, MX, PV, CNT, TR = (2, 3), (0, 1), 4, 5, (6, 7)
        UNITS = [range(-(-h * 16 // 12), min(16, -(-(h + 1) * 16 // 12))) for h in range(H)]
        E_LOADS = 16 * 5
        SEARCH_LINKS = 35

        def hold(engine, semaphore, value):
            if not isinstance(value, int):
                value = engine.to_reg(value)
                engine.wait_ge(w_in, W_ALL)
            engine.wait_ge(semaphore, value)

        block = ctx.enter_context(nc.Block())

        @block.sync
        def _(sp):
            for g in range(NG):
                sp.dma_start(x_all[:, g * GT:(g + 1) * GT, :], x_t[:, g * GT:(g + 1) * GT, :]).then_inc(x_in[g], 16)
            sp.sem_inc(parts_out, 32)
            with sp.Fori(0, ROUNDS_A) as i:
                for par in range(2):
                    g = i * 2 + par
                    hold(sp, split_done, g + 3)
                    hold(sp, parts_out, (g + 2) * 16)
                    sp.dma_start(d_parts[:, :, :, bass.ds(g * GN, GN)].rearrange("i w p n -> p (i w) n"),
                                 parts[:, par].rearrange("p i w n -> p (i w) n")).then_inc(parts_out, 16)
            sp.wait_ge(parts_out, 16 * (NG + 2))

            def load_half(b, slot, half):
                hs = slice(half * H // 2, (half + 1) * H // 2)
                for w, slots in ((0, SLOTS_Q), (1, SLOTS_K)):
                    for s, part in enumerate(slots):
                        src = d_parts[part, w].rearrange("(h d) t -> d h t", d=HD)[:, hs, bass.ds(b * S, S)]
                        sp.dma_start(stacks[s * HD:(s + 1) * HD, slot, w, hs, :], src).then_inc(stack_in, 16)

            sp.wait_ge(zeroed, 1)
            load_half(0, 0, 0)
            sp.wait_ge(sc_evac, NG + 1)
            sp.dma_start(d_score, sT).then_inc(score_out, 16)
            sp.wait_ge(score_out, 16)
            sp.dma_start(key_f, d_score.rearrange("e (c f) -> (e c) f", f=S)).then_inc(score_in, 16)
            for n in range(1, 4):
                hold(sp, stack_in, HALF_LOAD * n)
                load_half(n // 2, n // 2, n % 2)
            sp.wait_ge(key_ready, 1)
            sp.dma_start(d_keys.rearrange("w r f -> r w f"), key_h).then_inc(key_out, 16)
            sp.wait_ge(key_out, 16)
            for g in range(NG):
                for w in range(2):
                    src = d_keys[w].rearrange("(e g c) f -> g e (c f)", e=E0, g=NG)[g:g + 1, 0:E0 - 1, :]
                    sp.dma_start(keys[g * REP:(g + 1) * REP, w, :, :],
                                 src.broadcast_to([REP, E0 - 1, GN])).then_inc(keys_in, 16)

            def put_max(b, slot):
                hold(sp, nm_evac, b + 1)
                for part in range(2):
                    sp.dma_start(stacks[MROW + part:MROW + part + 1, slot, 0, :, :].rearrange(
                        "p h (c q) -> p (h c) q", c=2), nmT[32 * part:32 * part + 32, :]).then_inc(nm_in, 16)

            put_max(0, 0)

            def refill(b, slot):
                for half in range(2):
                    hold(sp, lt_ready, H * b + (half + 1) * H // 2)
                    hold(sp, stack_in, HALF_LOAD * (2 * (b + 2) + half))
                    load_half(b + 2, slot, half)
                    if half == 0:
                        hold(sp, nm_in, 32 * (b + 1))
                        put_max(b + 1, 1 - slot)

            with sp.Fori(0, B // 2 - 1) as i:
                for slot in range(2):
                    refill(i * 2 + slot, slot)
            sp.wait_ge(nm_in, 32 * (B - 1))
            put_max(B - 1, (B - 1) % 2)

            def load_expert(e, par):
                sp.dma_start(w1e[:, par], flat(a["w1"][:, bass.ds(e, 1), :])).then_inc(e_in[par], 16)
                sp.dma_start(w2e[:, par].rearrange("p t n -> p (t n)"),
                             flat(a["w2"][:, bass.ds(e, 1), :])).then_inc(e_in[par], 16)
                sp.dma_start(b1e[:, par], flat(a["b1"][:, bass.ds(e, 1), :])).then_inc(e_in[par], 16)
                sp.dma_start(b2e[:, par], a["b2"][bass.ds(e, 1), :].broadcast_to([P, D])).then_inc(e_in[par], 16)
                sp.dma_start(zl[:, par], sorted_t[:, bass.ds(e * GT, GT), :]).then_inc(e_in[par], 16)

            sp.wait_ge(lt_ready, H * B)
            sp.wait_ge(scattered, 16 * NT)
            load_expert(0, 0)
            load_expert(1, 1)
            sp.sem_inc(ffn_out, 32)

            def next_expert(e, par, more):
                hold(sp, y_evac, e + 3)
                hold(sp, ffn_out, (e + 2) * 16)
                sp.dma_start(ffn_t[:, bass.ds(e * GT, GT), :], ho[:, par]).then_inc(ffn_out, 16)
                if more:
                    load_expert(e + 2, par)

            with sp.Fori(0, E0 // 2 - 1) as i:
                for par in range(2):
                    next_expert(i * 2 + par, par, True)
            for par in range(2):
                next_expert(E0 - 2 + par, par, False)

            sp.wait_ge(y_evac, E0 + 2)
            sp.wait_ge(ffn_out, 16 * (E0 + 2))
            sp.dma_start(w1m.rearrange("p e n -> p (e n)"), a["w1m"]).then_inc(m_in, 16)
            sp.dma_start(w2m.rearrange("p e t n -> p (e t n)"), a["w2m"]).then_inc(m_in, 16)
            sp.sem_inc(stored, 32)
            with sp.Fori(0, ROUNDS_A) as i:
                for par in range(2):
                    g = i * 2 + par
                    hold(sp, out_ready, g + 1)
                    hold(sp, stored, (g + 2) * 16)
                    sp.dma_start(out_t[:, bass.ds(g * GT, GT), :], outs[:, par]).then_inc(stored, 16)
            sp.wait_ge(stored, 16 * (NG + 2))

        @block.gpsimd
        def _(gp):
            pc = Chain(gp, pool_s)
            for dst, src in first_loads:
                gp.dma_start(dst, src).then_inc(w_in, 16)
            gp.sem_inc(xn_copied, 2)
            pc.link(gp.memset(half_neg[:, :], -0.5))
            pc.link(gp.memset(v_b[:, :, :, :, :], 0.0))
            pc.link(gp.memset(v_b[:, :, :, :, HD:HD + 1], 1.0))
            for n, to in ((1, rstd), (2, rstd2)):
                hold(gp, var_ok, n)
                gp.tensor_tensor(to[:, :], tmp_s[:, :], half_neg[:, :], ALU.pow).then_inc(rstd_ok, 1)
            with gp.Fori(0, ROUNDS_A) as i:
                for par in range(2):
                    g = i * 2 + par
                    hold(gp, st_ready, g + 1)
                    gp.tensor_copy(xn_all[:, bass.ds(g * GT, GT), :], xst[:, par]).then_inc(xn_copied, 1)
                    hold(gp, qk_evac, g + 1)
                    hold(gp, parts_out, (g + 1) * 16)
                    gp.tensor_copy(parts[:, par, 0], qkf[:, par]).then_inc(part1, 1)
                    hold(gp, rest1, g + 1)
                    gp.tensor_copy(parts[:, par, 1], qkf[:, par]).then_inc(part2, 1)
            pc.link(gp.memset(arena[:, 0:STACKS_END], 0.0))
            gp.memset(stacks[MROW:MROW + 2, :, 1, :, :], 1.0).then_inc(zeroed, 1)

            def copy_v(b, par):
                hold(gp, pv_done, b * 4 + 4)
                gp.tensor_copy(v_b[:, par, :, :, 0:HD], v_all[:, bass.ds(b * 2, 2), :].rearrange(
                    "p k (h d) -> p k h d", h=H)).then_inc(v_ready, 1)

            gp.wait_ge(zeroed, 1)
            gp.wait_ge(v_evac, NG + 1)
            with gp.Fori(0, B // 2) as i:
                for par in range(2):
                    copy_v(i * 2 + par, par)

            gp.wait_ge(z_ready, 1)
            gp.wait_ge(pos_ready, 1)
            for t in range(NT):
                gp.indirect_dma_start(d_sorted, bass.IndirectOffsetOnAxis(ap=pos[:, t:t + 1], axis=0),
                                      routed[:, t, :], None).then_inc(scattered, 16)
            gp.wait_ge(ffn_out, 16 * (E0 + 2))
            for t in range(NT):
                gp.indirect_dma_start(routed[:, t, :], None, d_ffn,
                                      bass.IndirectOffsetOnAxis(ap=pos[:, t:t + 1], axis=0)).then_inc(gathered, 16)
            gp.sem_inc(x1_copied, 2)
            gp.wait_ge(var1_ok, 1)
            gp.tensor_tensor(rstd[:, :], tmp_s[:, :], half_neg[:, :], ALU.pow).then_inc(rstd1_ok, 1)
            with gp.Fori(0, ROUNDS_A) as i:
                for par in range(2):
                    g = i * 2 + par
                    hold(gp, x1_evac, g + 1)
                    gp.tensor_copy(flat(xT_all[:, bass.ds(g, 1), :]), x1T[:, par]).then_inc(x1_copied, 1)

        @block.scalar
        def _(act):
            act.wait_ge(w_in, W_ALL)
            act.sem_inc(sc_evac, 1)
            with act.Fori(0, ROUNDS_A) as i:
                for par in range(2):
                    g = i * 2 + par
                    act.wait_ge(tr_done, g + 3)
                    nc.scalar.activation(xT[:, par], bank[0][:, :], ACT.Copy)
                    nc.scalar.activation(zT[:, par], bank[1][:, :], ACT.Identity, bias=ln_gb[:, 1:2],
                                         scale=ln_gb[:, 0:1]).then_inc(t_evac, 1)
                    act.wait_ge(proj_done, g + 1)
                    act.wait_ge(split_done, g + 1)
                    nc.scalar.activation(qkf[:, par, 0], bank[2][:, :], ACT.Identity, bias=b_qk[:, 0:1])
                    nc.scalar.activation(qkf[:, par, 1], bank[3][:, :], ACT.Identity,
                                         bias=b_qk[:, 1:2]).then_inc(qk_evac, 1)
                    nc.scalar.activation(sT[:, bass.ds(g * GN, GN)], bank[5][0:E0, :], ACT.Copy).then_inc(sc_evac, 1)

            act.sem_inc(lt_free, 2)
            act.sem_inc(pv_free, 1)

            def keep_o(m, par, quad):
                act.wait_ge(pv_done, m + 9)
                if quad == 0:
                    act.wait_ge(ot_done, m // 4 + 1)
                nc.scalar.activation(o_b[:, par, quad, :], bank[PV][:, 0:S], ACT.Copy).then_inc(pv_free, 1)

            def turn_vals(b):
                act.wait_ge(vt_done, b + 1)
                for qt in range(2):
                    ins = nc.scalar.activation(vT[:, qt, :], bank[TR[qt]][:, 0:P], ACT.Copy)
                ins.then_inc(vt_evac, 1)

            def batch(b, par, before):
                for quad in range(4):
                    act.wait_ge(pv_done, b * 4 + quad + 7)
                    for h in range(quad * 4, quad * 4 + 4):
                        act.wait_ge(lt_ready, b * H + h + 1)
                        nc.scalar.activation(probs[:, h % 8, :], bank[LT[h % 2]][:, :], ACT.Exp,
                                             scale=float(HD) ** -0.5).then_inc(lt_free, 1)
                    if quad:
                        keep_o(b * 4 + quad - 1, par, quad - 1)
                    elif before:
                        keep_o(b * 4 - 1, 1 - par, 3)
                    if quad == 2 and before:
                        turn_vals(b - 1)

            batch(0, 0, False)
            with act.Fori(0, PAIRS) as i:
                batch(i * 2 + 1, 1, True)
                batch(i * 2 + 2, 0, True)
            batch(B - 1, 1, True)
            keep_o(4 * B - 1, 1, 3)
            turn_vals(B - 1)

            act.sem_inc(h_evac, 2)

            def turn_z(e, par):
                act.wait_ge(zt_done, e + 1)
                nc.scalar.activation(nT[:, par], bank[0][:, :], ACT.Identity, bias=ln_gb[:, 1:2],
                                     scale=ln_gb[:, 0:1]).then_inc(nt_ready, 1)

            def expert(e, par, more):
                for ft in range(4):
                    act.wait_ge(h_done, e * 4 + ft + 1)
                    nc.scalar.activation(hT[:, par, ft, :], bank[1 + ft % 2][:, :], ACT.Gelu_apprx_tanh,
                                         bias=b1e[:, par, ft:ft + 1]).then_inc(h_evac, 1)
                if more:
                    turn_z(e + 1, 1 - par)

            turn_z(0, 0)
            with act.Fori(0, E0 // 2 - 1) as i:
                for par in range(2):
                    expert(i * 2 + par, par, True)
            expert(E0 - 2, 0, True)
            expert(E0 - 1, 1, False)

            with act.Fori(0, NG) as g:
                act.wait_ge(gin_ready, g + 1)
                v = routed[:, bass.ds(g * GT, GT), :]
                nc.scalar.activation(v, v, ACT.Silu).then_inc(silu_done, 1)

            with act.Fori(0, ROUNDS_A) as i:
                for par in range(2):
                    g = i * 2 + par
                    act.wait_ge(tr1_done, g + 3)
                    act.wait_ge(x1_copied, g + 1)
                    for c in range(2):
                        ins = nc.scalar.activation(x1T[:, par, c * S:(c + 1) * S], bank[0][:, c * S:(c + 1) * S],
                                                   ACT.Copy, accum_out=xsum[:, bass.ds(g * 2 + c, 1)])
                    ins.then_inc(x1_evac, 1)
            act.wait_ge(lg_ready, 1)
            nc.scalar.activation(gl, gl, ACT.Exp).then_inc(exp_done, 1)
            act.wait_ge(lg_ready, 2)
            nc.scalar.activation(ds, ds, ACT.Exp, scale=float(D) ** -0.5).then_inc(exp_done, 1)
            for r in range(B // 4):
                act.wait_ge(vs_mm, 4 * (r + 1))
                nc.scalar.activation(vsum[:, r * 4:(r + 1) * 4, :].rearrange("p c n -> p (c n)"),
                                     bank[3 + r % 2][:, :], ACT.Copy).then_inc(vs_evac, 1)
            act.sem_inc(hm_evac, 2)
            act.sem_inc(gate_done, 2)
            with act.Fori(0, ROUNDS_A) as i:
                for par in range(2):
                    g = i * 2 + par
                    act.wait_ge(sct_done, g + 1)
                    nc.scalar.activation(scT[:, par, :], bank[6][0:E1, :], ACT.Copy).then_inc(sct_evac, 1)
                    for e in range(E1):
                        act.wait_ge(hm_done, (g * E1 + e) + 1)
                        act.wait_ge(ym_done, (g * E1 + e) + 1)
                        for t in range(2):
                            ins = nc.scalar.activation(hm[:, e % 2, t, :], bank[2 * (e % 2) + t][:, :], ACT.Relu,
                                                       bias=b1m[:, e, t:t + 1])
                        ins.then_inc(hm_evac, 1)
                    act.wait_ge(acc_ready, g + 1)
                    nc.scalar.activation(gate[:, par], acc[:, par], ACT.Silu).then_inc(gate_done, 1)

        @block.tensor
        def _(pe):
            mm, turn = nc.tensor.matmul, nc.tensor.transpose
            pe.wait_ge(w_in, W_ALL)
            pe.wait_ge(idents, 1)
            pe.sem_inc(tr_done, 2)
            with pe.Fori(0, ROUNDS_A) as i:
                for par in range(2):
                    g = i * 2 + par
                    pe.wait_ge(st_ready, g + 1)
                    for n, src in ((0, xst), (1, zst)):
                        for t in range(GT):
                            ins = turn(bank[n][:, t * P:(t + 1) * P], src[:, par, t, :], ident[:, :])
                    ins.then_inc(tr_done, 1)
                    pe.wait_ge(t_evac, g + 1)
                    pe.wait_ge(sc_evac, g + 1)
                    mm(bank[2][:, :], w_q[:, :], xT[:, par], start=True, stop=True)
                    mm(bank[3][:, :], w_k[:, :], xT[:, par], start=True, stop=True)
                    pe.wait_ge(v_evac, g + 1)
                    for t in range(GT):
                        mm(bank[4][:, t * P:(t + 1) * P], xT[:, par, t * P:(t + 1) * P], w_v[:, :],
                           start=True, stop=True)
                    mm(bank[5][0:E0, :], cent[:, :], zT[:, par], start=True, stop=True).then_inc(proj_done, 1)

            pe.sem_inc(ot_done, 2)
            pe.sem_inc(pv_done, 8)
            pe.wait_ge(sc_evac, NG + 1)
            pe.wait_ge(v_evac, NG + 1)

            def max_unit(b, slot, u):
                if u % 8 == 0:
                    pe.wait_ge(stack_in, (2 * b + u // 8 + 1) * HALF_LOAD)
                pe.wait_ge(mx_free, b * 16 + u + 1)
                qt = u % 2
                for n in range(2):
                    h = u // 2 * 2 + n
                    ins = mm(bank[MX[u % 2]][:, n * S:(n + 1) * S], stacks[0:KROWS, slot, 0, h, qt * P:(qt + 1) * P],
                             stacks[0:KROWS, slot, 1, h, :], start=True, stop=True)
                ins.then_inc(mx_ready, 1)

            def logits(b, slot, h):
                pe.wait_ge(lt_free, b * H + h + 1)
                for kt in range(2):
                    ins = mm(bank[LT[h % 2]][:, kt * S:(kt + 1) * S], stacks[0:MROW + 2, slot, 1, h, kt * P:(kt + 1) * P],
                             stacks[0:MROW + 2, slot, 0, h, :], start=True, stop=True)
                ins.then_inc(lt_ready, 1)

            def weigh(m, quad, par):
                if quad == 0:
                    pe.wait_ge(v_ready, m // 4 + 1)
                pe.wait_ge(lt_free, m * 4 + 6)
                pe.wait_ge(pv_free, m + 1)
                for kt in range(2):
                    for n in range(4):
                        h = quad * 4 + n
                        ins = mm(bank[PV][32 * n:32 * n + 32, 0:S], v_b[:, par, kt, h, :],
                                 probs[:, h % 8, kt * S:(kt + 1) * S], start=kt == 0, stop=kt == 1,
                                 tile_position=(0, 32 * n))
                ins.then_inc(pv_done, 1)

            def turn_o(b, par):
                pe.wait_ge(pv_free, b * 4 + 5)
                pe.wait_ge(s_evac, b + 1)
                for qt in range(2):
                    for quad in range(4):
                        ins = turn(bank[TR[qt]][:, quad * P:(quad + 1) * P], o_b[:, par, quad, qt * P:(qt + 1) * P],
                                   ident[:, :])
                ins.then_inc(ot_done, 1)

            def turn_v(b):
                pe.wait_ge(vals_ready, b + 1)
                for qt in range(2):
                    ins = turn(bank[TR[qt]][:, 0:P], vals[:, qt, :], ident[:, :])
                ins.then_inc(vt_done, 1)

            def project(b):
                pe.wait_ge(vt_evac, b + 1)
                for qt in range(2):
                    ins = mm(bank[TR[qt]][:, P:2 * P], vT[:, qt, :], w_o[:, :], start=True, stop=True)
                ins.then_inc(s_done, 1)

            def count(k):
                pe.wait_ge(cnt_ready, k + 1)
                mm(bank[CNT][:, 0:REP], cnt[:, 0:1].broadcast_to([P, P]), pick[:, :],
                   start=True, stop=True).then_inc(cnt_sum, 1)

            def turn_max(b):
                pe.wait_ge(nm_ready, b + 1)
                turn(bank[CNT][:, :].bitcast(BF16)[:, P:2 * P], nm[:, :], ident_b[:, :]).then_inc(nm_tr, 1)

            def batch(b, par, before, ahead, half=None, e=None):
                pe.wait_ge(nm_in, (b + 1) * 32)
                for h in range(H):
                    logits(b, par, h)
                    if ahead:
                        for u in UNITS[h]:
                            max_unit(b + 1, 1 - par, u)
                    if h % 4 == 3:
                        if h > 3:
                            weigh(b * 4 + h // 4 - 1, h // 4 - 1, par)
                        elif before:
                            weigh(b * 4 - 1, 3, 1 - par)
                    if half is not None and h % 3 == 2 and h < 12:
                        count((b - 1) * ROUNDS + h // 3)
                    if before and h == 7:
                        turn_o(b - 1, 1 - par)
                    if before and h == 11:
                        turn_v(b - 1)
                    if ahead and h == 12:
                        turn_max(b + 1)
                    if before and h == 13:
                        project(b - 1)
                    if half == 1 and h == 14:
                        pe.wait_ge(fin_ready, e + 1)
                        mm(bank[CNT][:, 0:1], nge[:, :], cnt[:, 1:2], start=True, stop=False)
                        mm(bank[CNT][:, 0:1], neq[:, :], cnt[:, 2:3], start=False, stop=True).then_inc(fin_sum, 1)

            for u in range(16):
                max_unit(0, 0, u)
            turn_max(0)
            batch(0, 0, False, True)
            with pe.Fori(0, PAIRS) as i:
                batch(i * 2 + 1, 1, True, True, 0, i)
                batch(i * 2 + 2, 0, True, True, 1, i)
            batch(B - 1, 1, True, False)
            weigh(4 * B - 1, 3, 1)
            pe.wait_ge(eid_ready, 1)
            for c in range(GT):
                ins = turn(bank[CNT][:, :].bitcast(F16)[:, c * P:(c + 1) * P], eid[:, c * P:(c + 1) * P], ident_h[:, :])
            ins.then_inc(eid_tr, 1)
            pe.wait_ge(hot_ready, 1)
            hot_f = hot[:, :, :].rearrange("p e t -> p (e t)")
            mm(bank[0][:, 0:E0 * NT], tri[:, :], hot_f, start=True, stop=True)
            mm(bank[1][:, 0:E0 * NT], ones_h[:, 0:P], hot_f, start=True, stop=True).then_inc(pos_mm, 1)
            turn_o(B - 1, 1)
            turn_v(B - 1)
            project(B - 1)

            def turn_rows(e, par, round_):
                pe.wait_ge(e_in[par], (round_ + 1) * E_LOADS)
                for t in range(GT):
                    ins = turn(bank[0][:, t * P:(t + 1) * P], zl[:, par, t, :], ident[:, :])
                ins.then_inc(zt_done, 1)

            def expert(e, par, round_, more):
                pe.wait_ge(nt_ready, e + 1)
                for ft in range(4):
                    pe.wait_ge(h_evac, e * 4 + ft + 1)
                    mm(bank[1 + ft % 2][:, :], w1e[:, par, ft * P:(ft + 1) * P], nT[:, par],
                       start=True, stop=True).then_inc(h_done, 1)
                if more:
                    turn_rows(e + 1, 1 - par, round_ + par)
                pe.wait_ge(h_evac, e * 4 + 6)
                pe.wait_ge(y_evac, e + 1)
                for t in range(GT):
                    for ft in range(4):
                        ins = mm(bank[3 + par][:, t * P:(t + 1) * P], hT[:, par, ft, t * P:(t + 1) * P],
                                 w2e[:, par, ft, :], start=ft == 0, stop=ft == 3)
                ins.then_inc(y_done, 1)

            pe.wait_ge(pos_ready, 1)
            pe.wait_ge(pv_free, 4 * B + 1)
            turn_rows(0, 0, 0)
            with pe.Fori(0, E0 // 2 - 1) as i:
                for par in range(2):
                    expert(i * 2 + par, par, i, True)
            expert(E0 - 2, 0, E0 // 2 - 1, True)
            expert(E0 - 1, 1, E0 // 2 - 1, False)

            pe.wait_ge(s_evac, B + 1)
            mm(bank[6][:, 0:P], wqkv8[:, 0, :], wqkv8[:, 1, :], start=True, stop=True)
            mm(bank[6][:, P:2 * P], wqkv8[:, 2, :], wqkv8[:, 3, :], start=True, stop=True).then_inc(w8_done, 1)
            pe.sem_inc(tr1_done, 2)
            pe.wait_ge(w8_evac, 2)
            with pe.Fori(0, ROUNDS_A) as i:
                for par in range(2):
                    g = i * 2 + par
                    pe.wait_ge(st1_ready, g + 1)
                    for t in range(GT):
                        ins = turn(bank[0][:, t * P:(t + 1) * P], xst[:, par, t, :], ident[:, :])
                    ins.then_inc(tr1_done, 1)
                    pe.wait_ge(x1_evac, g + 1)
                    pe.wait_ge(yg_evac, g + 1)
                    for t in range(GT):
                        mm(bank[1][:, t * P:(t + 1) * P], x1T[:, par, t * P:(t + 1) * P], bd_a[:, :],
                           start=True, stop=True)
                    for t in range(GT):
                        ins = mm(bank[2][:, t * E1:(t + 1) * E1], x1T[:, par, t * P:(t + 1) * P], w_g[:, :],
                                 start=True, stop=True)
                    ins.then_inc(yg_done, 1)
            for r in range(B // 4):
                if r >= 2:
                    pe.wait_ge(vs_evac, r - 1)
                for n in range(4):
                    c = r * 4 + n
                    pe.wait_ge(vrhs_ready, c + 1)
                    ins = mm(bank[3 + r % 2][:, n * P:(n + 1) * P], ones_f[:, :], vrhs[:, c % 2, :],
                             start=True, stop=True)
                    ins.then_inc(vs_mm, 1)
            pe.wait_ge(vs_evac, B // 4)
            pe.wait_ge(m_in, 32)
            pe.sem_inc(ym_done, 2)
            with pe.Fori(0, ROUNDS_A) as i:
                for par in range(2):
                    g = i * 2 + par
                    pe.wait_ge(sct_in, g + 1)
                    for t in range(GT):
                        ins = turn(bank[6][0:E1, t * P:(t + 1) * P], scm[:, par, t, :], ident[:, :])
                    ins.then_inc(sct_done, 1)

                    def hidden(e):
                        pe.wait_ge(hm_evac, g * E1 + e + 1)
                        for t in range(2):
                            ins = mm(bank[2 * (e % 2) + t][:, :], w1m[:, e, t * P:(t + 1) * P],
                                     flat(xT_all[:, bass.ds(g, 1), :]), start=True, stop=True)
                        ins.then_inc(hm_done, 1)

                    hidden(0)
                    pe.wait_ge(sct_evac, g + 1)
                    for t in range(GT):
                        ins = mm(bank[7][:, t * P:(t + 1) * P], scT[:, par, t * P:(t + 1) * P], b2m[:, :],
                                 start=True, stop=True)
                    ins.then_inc(b2_done, 1)
                    for e in range(E1):
                        if e + 1 < E1:
                            hidden(e + 1)
                        pe.wait_ge(hm_evac, g * E1 + e + 3)
                        pe.wait_ge(ym_free, g * E1 + e + 1)
                        for t in range(GT):
                            for ft in range(2):
                                ins = mm(bank[4 + e % 2][:, t * P:(t + 1) * P], hm[:, e % 2, ft, t * P:(t + 1) * P],
                                         w2m[:, e, ft, :], start=ft == 0, stop=ft == 1)
                        ins.then_inc(ym_done, 1)

        @block.vector
        def _(dve):
            ch = Chain(dve, chain_s)
            v = nc.vector
            v.memset(ones_h[:, :], 1.0)
            v.memset(ones_f[:, :], 1.0)
            v.memset(eid[:, :], 0.0)
            v.memset(nm[:, :], 0.0)
            v.memset(avail[:, :], 1.0)
            dve.sem_inc(v_evac, 1)
            dve.sem_inc(split_done, 2)

            def statistics():
                s6 = [stat6[:, :, k] for k in range(6)]
                ch.link(v.tensor_tensor(mean[:, :], s6[1], s6[4], ALU.add))
                ch.link(v.tensor_scalar(mean[:, :], mean[:, :], 0.5, None, ALU.mult))
                ch.link(v.tensor_tensor(rstd2[:, :], s6[1], s6[4], ALU.subtract))
                ch.link(v.tensor_tensor(rstd2[:, :], rstd2[:, :], rstd2[:, :], ALU.mult))
                ch.link(v.tensor_tensor(var[:, :], s6[2], s6[5], ALU.add))
                ch.link(v.scalar_tensor_tensor(var[:, :], rstd2[:, :], D / 4.0, var[:, :], ALU.mult, ALU.add))
                ch.link(v.tensor_scalar(var[:, :], var[:, :], 1.0 / D, None, ALU.mult))

            for g in range(NG):
                dve.wait_ge(x_in[g], 16)
                for t in range(g * GT, (g + 1) * GT):
                    ins = v.bn_stats(stat6[:, t, :], x_all[:, t, :])
            ch.link(ins)
            statistics()
            v.tensor_scalar(tmp_s[:, :], var[:, :], EPS, None, ALU.add).then_inc(var_ok, 1)
            dve.wait_ge(rstd_ok, 1)
            ch.link(v.tensor_tensor(var[:, :], var[:, :], rstd[:, :], ALU.mult))
            ch.link(v.tensor_tensor(var[:, :], var[:, :], rstd[:, :], ALU.mult))
            v.tensor_scalar(tmp_s[:, :], var[:, :], EPS, None, ALU.add).then_inc(var_ok, 1)
            dve.wait_ge(rstd_ok, 2)
            ch.link(v.tensor_tensor(zscale[:, :], rstd2[:, :], rstd[:, :], ALU.mult))
            dve.wait_ge(w_in, W_ALL)
            v.tensor_copy(ident_b[:, :], ident[:, :])
            v.tensor_copy(ident_h[:, :], ident[:, :]).then_inc(idents, 1)

            with dve.Fori(0, ROUNDS_A) as i:
                for par in range(2):
                    g = i * 2 + par
                    dve.wait_ge(tr_done, g + 1)
                    dve.wait_ge(xn_copied, g + 1)
                    for dst, by in ((xst, rstd), (zst, zscale)):
                        for t in range(GT):
                            at = bass.ds(g * GT + t, 1)
                            ins = v.tensor_scalar(dst[:, par, t, :], flat(x_all[:, at, :]), mean[:, at], by[:, at],
                                                  ALU.subtract, ALU.mult)
                    ins.then_inc(st_ready, 1)
                    dve.wait_ge(proj_done, g + 1)
                    v.tensor_tensor(v_all[:, bass.ds(g * GT, GT), :],
                                    bank[4][:, :].rearrange("p (t n) -> p t n", t=GT),
                                    b_v[:, :].unsqueeze(1).broadcast_to([P, GT, P]), ALU.add).then_inc(v_evac, 1)
                    dve.wait_ge(part1, g + 1)
                    v.tensor_tensor(qkf[:, par], qkf[:, par], parts[:, par, 0], ALU.subtract).then_inc(rest1, 1)
                    dve.wait_ge(part2, g + 1)
                    v.tensor_tensor(parts[:, par, 2], qkf[:, par], parts[:, par, 1],
                                    ALU.subtract).then_inc(split_done, 1)

            dve.sem_inc(mx_free, 2)
            dve.sem_inc(s_evac, 1)

            def row_max(b, u):
                dve.wait_ge(mx_ready, b * 16 + u + 1)
                hp, qt = u // 2, u % 2
                return v.tensor_reduce(mx[:, 2 * hp:2 * hp + 2, qt],
                                       bank[MX[u % 2]][:, :].rearrange("p (h k) -> p h k", h=2),
                                       AX.X, ALU.max).then_inc(mx_free, 1)

            def split_max(b):
                dve.wait_ge(mx_free, b * 16 + 18)
                mx_f, hi, lo = mx[:, :, :].rearrange("p h c -> p (h c)"), nm[:, 0:2 * H], nm[:, 2 * H:4 * H]
                ch.link(v.tensor_scalar(hi, mx_f, -1.0, None, ALU.mult))
                v.scalar_tensor_tensor(lo, mx_f, -1.0, hi, ALU.mult,
                                       ALU.subtract).then_inc(nm_ready, 1)
                dve.wait_ge(nm_tr, b + 1)
                if not (isinstance(b, int) and b == 0):
                    dve.wait_ge(nm_in, b * 32)
                v.tensor_copy(nmT[:, :], bank[CNT][:, :].bitcast(BF16)[:, P:2 * P]).then_inc(nm_evac, 1)

            def values(b):
                dve.wait_ge(ot_done, b + 3)
                for qt in range(2):
                    o = bank[TR[qt]][:, :].rearrange("p (h n) -> p h n", n=32)
                    ins = v.reciprocal(rec[:, qt, :], o[:, :, HD])
                ch.link(ins)
                for qt in range(2):
                    o = bank[TR[qt]][:, :].rearrange("p (h n) -> p h n", n=32)
                    ins = v.tensor_tensor(vals[:, qt, :].rearrange("p (h n) -> p h n", n=HD), o[:, :, 0:HD],
                                          rec[:, qt, :].unsqueeze(2).broadcast_to([P, H, HD]), ALU.mult)
                ins.then_inc(vals_ready, 1)

            def keep_s(b):
                dve.wait_ge(s_done, b + 1)
                for qt in range(2):
                    ins = v.tensor_tensor(flat(s_all[:, bass.ds(b * 2 + qt, 1), :]), bank[TR[qt]][:, P:2 * P],
                                          b_o[:, :], ALU.add)
                ins.then_inc(s_evac, 1)

            def begin_high(e):
                v.tensor_copy(T, thr[:, 0:1])
                v.tensor_copy(BASE, thr[:, 1:2])
                v.memset(L, 0.0)
                ch.link(v.scalar_tensor_tensor(khi[:, :], flat(keys[:, 0, bass.ds(e, 1), :]), HALF, avail[:, :],
                                               ALU.mult, ALU.mult))

            def begin_low(e):
                v.tensor_copy(T, thr[:, ROUNDS:ROUNDS + 1])
                v.tensor_copy(BASE, thr[:, ROUNDS + 1:ROUNDS + 2])
                ch.link(v.tensor_scalar(QUOTA, L, -DONE[ROUNDS] * HALF, None, ALU.add))
                ch.link(v.scalar_tensor_tensor(key2[:, :], khi[:, :], QUOTA, flat(keys[:, 1, bass.ds(e, 1), :]),
                                               ALU.subtract, ALU.add))
                ch.link(v.memset(L, 0.0))

            def try_thresholds(half):
                src = (khi, key2)[half]
                v.tensor_scalar(junk[:, :], src[:, :], T, None, ALU.is_ge, ALU.add,
                                accum_out=cnt[:, 0:1]).then_inc(cnt_ready, 1)

            def next_digit(k, r, half):
                w = (HALF, 1.0)[half] * STEPS[r]
                dve.wait_ge(cnt_sum, k + 1)
                ch.link(v.tensor_scalar(junk16[:, :], bank[CNT][:, 0:REP], float(CAP), None, ALU.is_ge, ALU.add,
                                        accum_out=DIG))
                if r < ROUNDS - 1:
                    v.scalar_tensor_tensor(T, DIG, w, BASE, ALU.mult, ALU.add)
                ch.link(v.scalar_tensor_tensor(L, DIG, w, L, ALU.mult, ALU.add))
                if r < ROUNDS - 2:
                    col = half * ROUNDS + r + 2
                    ch.link(v.tensor_tensor(BASE, L, thr[:, col:col + 1], ALU.add))

            def choose(e):
                ch.link(v.tensor_scalar(T, L, -DONE[ROUNDS], None, ALU.add))
                v.tensor_scalar(ge[:, :], key2[:, :], T, None, ALU.is_ge, ALU.add, accum_out=cnt[:, 1:2])
                ins = v.tensor_scalar(eq[:, :], key2[:, :], T, None, ALU.is_equal, ALU.add, accum_out=cnt[:, 2:3])
                ins.then_inc(fin_ready, 1)
                dve.wait_ge(fin_ready, e + 1)
                ch.link(v.tensor_tensor_scan(pre[:, :], ones_h[:, :], eq[:, :], 0.0, ALU.mult, ALU.add))
                dve.wait_ge(fin_sum, e + 1)
                ch.link(v.tensor_scalar(QUOTA, bank[CNT][:, 0:1], float(CAP), None, ALU.add))
                ch.link(v.scalar_tensor_tensor(pre[:, :], pre[:, :], QUOTA, eq[:, :], ALU.is_gt, ALU.mult))
                ch.link(v.tensor_tensor(avail[:, :], avail[:, :], ge[:, :], ALU.subtract))
                ch.link(v.tensor_tensor(avail[:, :], avail[:, :], pre[:, :], ALU.add))
                ch.link(v.tensor_tensor(eid[:, :], eid[:, :], avail[:, :], ALU.add))

            def make_keys():
                dve.wait_ge(score_in, 16)
                bits = key_f[:, :].bitcast(I32)
                flip = key2[:, 0:S].bitcast(I32)
                ch.link(v.tensor_scalar(flip, bits, 31, -2147483648, ALU.arith_shift_right, ALU.bitwise_or))
                ch.link(v.tensor_tensor(flip, flip, bits, ALU.bitwise_xor))
                halves = key2[:, 0:S].bitcast(U16).rearrange("p (f w) -> p w f", w=2)
                v.tensor_copy(key_h[:, 1, :], halves[:, 0, :])
                v.tensor_copy(key_h[:, 0, :], halves[:, 1, :]).then_inc(key_ready, 1)

            def batch(b, before, ahead, half=None, e=None):
                for u in range(16):
                    if ahead:
                        row_max(b + 1, u)
                    if half is not None:
                        if u == 0:
                            (begin_high, begin_low)[half](e)
                        if u % 4 == 1:
                            try_thresholds(half)
                        if u % 4 == 3:
                            next_digit((b - 1) * ROUNDS + u // 4, u // 4, half)
                    if u == 11 and before:
                        values(b - 1)
                if ahead:
                    split_max(b + 1)
                if half == 1:
                    choose(e)
                if before:
                    keep_s(b - 1)

            for u in range(16):
                row_max(0, u)
            split_max(0)
            make_keys()
            batch(0, False, True)
            dve.wait_ge(keys_in, 16 * 2 * NG)
            with dve.Fori(0, PAIRS) as i:
                ch.loop(i, SEARCH_LINKS)
                batch(i * 2 + 1, True, True, 0, i)
                batch(i * 2 + 2, True, True, 1, i)
            ch.end(PAIRS)
            v.sem_inc(eid_ready, 1)
            batch(B - 1, True, False)
            dve.wait_ge(eid_tr, 1)
            ch.link(v.tensor_copy(eidT[:, :].rearrange("p (g c) -> p c g", c=GT),
                                  bank[CNT][:, :].bitcast(F16)[:, 0:GT * P].rearrange(
                                      "p (c g j) -> p c g j", c=GT, j=REP)[:, :, :, 0]))
            for e in range(E0):
                ins = v.tensor_scalar(hot[:, e, :], eidT[:, :], float(e), None, ALU.is_equal)
            ins.then_inc(hot_ready, 1)
            dve.wait_ge(v_ready, B)
            v.tensor_tensor(routed[:, :, :], xn_all[:, :, :], rstd2[:, :].unsqueeze(2).broadcast_to([P, NT, D]),
                            ALU.mult).then_inc(z_ready, 1)
            dve.wait_ge(pos_mm, 1)
            ch.link(v.tensor_copy(posa[:, :], bank[1][:, 0:E0 * NT]))
            ch.link(v.tensor_tensor_scan(tot[:, :], ones_h[:, 0:E0 * NT], posa[:, :], 0.0, ALU.mult, ALU.add))
            ch.link(v.tensor_tensor(posa[:, :], tot[:, :], posa[:, :], ALU.subtract))
            ch.link(v.tensor_tensor(posa[:, :], bank[0][:, 0:E0 * NT], posa[:, :], ALU.add))
            ch.link(v.tensor_tensor(posa[:, :], posa[:, :], hot[:, :, :].rearrange("p e t -> p (e t)"), ALU.mult))
            ch.link(v.tensor_reduce(pos_f[:, :], posa[:, :].rearrange("p (e t) -> p t e", e=E0), AX.X, ALU.add))
            v.tensor_copy(pos[:, :], pos_f[:, :]).then_inc(pos_ready, 1)
            values(B - 1)
            keep_s(B - 1)

            dve.sem_inc(y_evac, 2)

            def expert(e, par):
                dve.wait_ge(y_done, e + 1)
                dve.wait_ge(ffn_out, (e + 1) * 16)
                v.tensor_tensor(ho[:, par], bank[3 + par][:, :].rearrange("p (t n) -> p t n", t=GT),
                                b2e[:, par].unsqueeze(1).broadcast_to([P, GT, D]), ALU.add).then_inc(y_evac, 1)

            with dve.Fori(0, E0 // 2) as i:
                for par in range(2):
                    expert(i * 2 + par, par)

            dve.wait_ge(w8_done, 1)
            v.tensor_tensor(bd_a[:, :], bank[6][:, 0:P], block_mask[:, :], ALU.mult).then_inc(w8_evac, 1)
            v.tensor_tensor(bd_v[:, :], bank[6][:, P:2 * P], block_mask[:, :], ALU.mult).then_inc(w8_evac, 1)
            dve.wait_ge(gathered, 16 * NT)
            with dve.Fori(0, NG) as g:
                at = bass.ds(g * GT, GT)
                v.tensor_tensor(routed[:, at, :], routed[:, at, :], xn_all[:, at, :], ALU.add).then_inc(gin_ready, 1)
            with dve.Fori(0, NG) as g:
                at = bass.ds(g * GT, GT)
                ch.loop(g, 2)
                dve.wait_ge(silu_done, g + 1)
                ch.link(v.tensor_tensor(s_all[:, at, :], s_all[:, at, :], routed[:, at, :], ALU.mult))
                ch.link(v.tensor_tensor(x_all[:, at, :], x_all[:, at, :], s_all[:, at, :], ALU.add))
                for t in range(GT):
                    one = bass.ds(g * GT + t, 1)
                    ins = v.bn_stats(flat(stat6[:, one, :]), flat(x_all[:, one, :]))
            ch.end(NG)
            ch.link(v.memset(small[:, :], 0.0))
            statistics()
            v.tensor_scalar(tmp_s[:, :], var[:, :], EPS, None, ALU.add).then_inc(var1_ok, 1)
            dve.wait_ge(rstd1_ok, 1)

            dve.sem_inc(yg_evac, 1)
            with dve.Fori(0, ROUNDS_A) as i:
                ch.loop(i, 2)
                for par in range(2):
                    g = i * 2 + par
                    at = bass.ds(g * GT, GT)
                    dve.wait_ge(tr1_done, g + 1)
                    for t in range(GT):
                        one = bass.ds(g * GT + t, 1)
                        ins = v.tensor_scalar(xst[:, par, t, :], flat(x_all[:, one, :]), mean[:, one], rstd[:, one],
                                              ALU.subtract, ALU.mult)
                    ins.then_inc(st1_ready, 1)
                    dve.wait_ge(yg_done, g + 1)
                    ch.link(v.tensor_tensor(zst[:, par], bank[1][:, :].rearrange("p (t n) -> p t n", t=GT),
                                            xst[:, par], ALU.mult))
                    v.tensor_reduce(ds[:, at, :], zst[:, par].rearrange("p t (h n) -> p t h n", n=HD), AX.X, ALU.add)
                    v.tensor_copy(gl[:, at, :], bank[2][:, 0:GT * E1].rearrange(
                        "p (t e) -> p t e", t=GT)).then_inc(yg_evac, 1)
            ch.end(ROUNDS_A)
            ch.link(v.memset(small[:, :], 0.0))
            dve.wait_ge(x1_copied, NG + 2)

            mine = gl.unsqueeze(3).broadcast_to([P, NT, E1, E1])
            other = gl.unsqueeze(2).broadcast_to([P, NT, E1, E1])
            v.tensor_tensor(pairs, other, mine, ALU.is_gt)
            ch.link(v.tensor_tensor(pairs2, other, mine, ALU.is_equal))
            ch.link(v.tensor_tensor(pairs2, pairs2, low[:, :, :].unsqueeze(1).broadcast_to([P, NT, E1, E1]), ALU.mult))
            ch.link(v.tensor_tensor(pairs, pairs, pairs2, ALU.add))
            rank = key2[:, 0:NT * E1].rearrange("p (t e) -> p t e", t=NT)
            ch.link(v.tensor_reduce(rank, pairs, AX.X, ALU.add))
            ch.link(v.tensor_scalar(rank, rank, 2.0, None, ALU.is_lt))
            ch.link(v.tensor_reduce(small[:, :], gl, AX.X, ALU.max))
            v.tensor_tensor(gl, gl, small[:, :].unsqueeze(2).broadcast_to([P, NT, E1]),
                            ALU.subtract).then_inc(lg_ready, 1)
            by_batch = ds.rearrange("p (c f) h -> p f h c", f=2)
            hm2 = hmax[:, :].rearrange("p (f h) -> p f h", f=2)
            wide = hm2.unsqueeze(1).broadcast_to([P, B, 2, H])
            ds4 = ds.rearrange("p (c f) h -> p c f h", f=2)
            ch.link(v.tensor_reduce(hm2, by_batch, AX.X, ALU.max))
            v.tensor_tensor(ds4, ds4, wide, ALU.subtract).then_inc(lg_ready, 1)
            dve.wait_ge(exp_done, 1)
            ch.link(v.tensor_tensor(gl, gl, rank, ALU.mult))
            ch.link(v.tensor_reduce(small[:, :], gl, AX.X, ALU.add))
            ch.link(v.reciprocal(small[:, :], small[:, :]))
            ch.link(v.tensor_tensor(gl, gl, small[:, :].unsqueeze(2).broadcast_to([P, NT, E1]),
                                    ALU.mult))
            dve.wait_ge(exp_done, 2)
            ch.link(v.tensor_reduce(hm2, by_batch, AX.X, ALU.add))
            ch.link(v.reciprocal(hmax[:, :], hmax[:, :]))
            ch.link(v.tensor_tensor(ds4, ds4, wide, ALU.mult))
            for c in range(B):
                if c >= 2:
                    dve.wait_ge(vs_mm, c - 1)
                else:
                    dve.wait_ge(x1_evac, NG)
                v.tensor_scalar(vrhs[:, c % 2, :], bd_v[:, :], xsum[:, c:c + 1], None, ALU.mult).then_inc(vrhs_ready, 1)

            dve.sem_inc(ym_free, 2)
            with dve.Fori(0, ROUNDS_A) as i:
                ch.loop(i, 6)
                for par in range(2):
                    g = i * 2 + par
                    at = bass.ds(g * GT, GT)
                    v.tensor_copy(scm[:, par], gl[:, at, :]).then_inc(sct_in, 1)
                    dve.wait_ge(b2_done, g + 1)
                    dve.wait_ge(gate_done, g + 1)
                    ch.link(v.tensor_copy(acc[:, par].rearrange("p t n -> p (t n)"), bank[7][:, :]))
                    for e in range(E1):
                        dve.wait_ge(ym_done, g * E1 + e + 3)
                        for t in range(GT):
                            ins = v.scalar_tensor_tensor(acc[:, par, t, :], bank[4 + e % 2][:, t * P:(t + 1) * P],
                                                         scm[:, par, t, e:e + 1], acc[:, par, t, :], ALU.mult, ALU.add)
                        ins.then_inc(ym_free, 1)
                        dve.wait_ge(ym_free, g * E1 + e + 3)
                    v.sem_inc(acc_ready, 1)
                    dve.wait_ge(vs_evac, B // 4)
                    dve.wait_ge(stored, (g + 1) * 16)
                    for c in range(2):
                        pr = ds[:, bass.ds((g * 2 + c) * 2, 2), :].unsqueeze(3).broadcast_to([P, 2, H, HD])
                        vs = vsum[:, bass.ds(g * 2 + c, 1), :].broadcast_to([P, 2, D]).rearrange(
                            "p f (h n) -> p f h n", n=HD)
                        ins = v.tensor_tensor(outs[:, par, 2 * c:2 * c + 2, :].rearrange("p f (h n) -> p f h n", n=HD),
                                              pr, vs, ALU.mult)
                    ch.link(ins)
                    dve.wait_ge(gate_done, g + 3)
                    ch.link(v.tensor_tensor(outs[:, par], outs[:, par], gate[:, par], ALU.mult))
                    v.tensor_tensor(outs[:, par], outs[:, par], x_all[:, at, :], ALU.add).then_inc(out_ready, 1)
            ch.end(ROUNDS_A)


_INS = ["x", "w_q", "w_k", "w_v", "w_o", "b_q", "b_k", "b_v", "b_o", "cent", "ln_g", "ln_b", "w1", "b1", "w2", "b2",
        "w8", "w_g", "w1m", "b1m", "w2m", "b2m",
        "c_ident", "c_block", "c_thr", "c_pick", "c_nge", "c_neq", "c_tri", "c_low"]


def kernel(**inputs):
    import concourse.bacc as bacc
    from concourse.bass_utils import run_bass_kernel_spmd

    a = {k: np.asarray(t) for k, t in inputs.items()}
    w = a["L0_attn_w_qkv"].reshape(H, 3, HD, D)
    bias = a["L0_attn_b_qkv"].reshape(H, 3, HD)
    rep = lambda m: np.tile(m, (1, H))
    lay = {
        "x": a["L0_attn_x"].reshape(TOK, D),
        "w_q": w[:, 0].reshape(D, D).T, "w_k": w[:, 1].reshape(D, D).T, "w_v": w[:, 2].reshape(D, D).T,
        "w_o": a["L0_attn_w_o"].T,
        "b_q": bias[:, 0].reshape(D, 1), "b_k": bias[:, 1].reshape(D, 1), "b_v": bias[:, 2].reshape(1, D),
        "b_o": a["L0_attn_b_o"].reshape(1, D),
        "cent": a["L0_ffn_centroids"].T, "ln_g": a["L0_ffn_ln_g"].reshape(D, 1), "ln_b": a["L0_ffn_ln_b"].reshape(D, 1),
        "w1": a["L0_ffn_w1"].transpose(1, 0, 2),
        "b1": a["L0_ffn_b1"].reshape(E0, 4, P).transpose(2, 0, 1),
        "w2": a["L0_ffn_w2"].reshape(E0, 4, P, D).transpose(2, 0, 1, 3).reshape(P, E0, 4 * D),
        "b2": a["L0_ffn_b2"],
        "w8": np.concatenate([rep(a["L1_attn_Wq"]), rep(a["L1_attn_Wk"]), rep(a["L1_attn_Wv"]),
                              rep(np.eye(HD, dtype=np.float32))], 1),
        "w_g": a["L1_ffn_Wg"],
        "w1m": a["L1_ffn_W1"].transpose(1, 0, 2).reshape(D, E1 * H1),
        "b1m": a["L1_ffn_b1"].reshape(E1, 2, P).transpose(2, 0, 1).reshape(P, 2 * E1),
        "w2m": a["L1_ffn_W2"].reshape(E1, 2, P, D).transpose(2, 0, 1, 3).reshape(P, E1 * 2 * D),
        "b2m": a["L1_ffn_b2"],
        **host_constants(),
    }
    nc = bacc.Bacc("TRN2", target_bir_lowering=False, num_devices=1)
    arrays, aps = {}, {}
    for name in _INS:
        t = np.ascontiguousarray(lay[name])
        arrays[f"in_{name}"] = t
        aps[name] = nc.dram_tensor(f"in_{name}", t.shape, mybir.dt.from_np(t.dtype), kind="ExternalInput").ap()
    out = nc.dram_tensor("out_0", (TOK, D), F32, kind="ExternalOutput").ap()
    two_layers(nc, aps, out)
    got = run_bass_kernel_spmd(nc, [arrays], core_ids=[0])
    return got.results[0]["out_0"].reshape(B, S, D)
```

```python
from contextlib import ExitStack

import numpy as np

import concourse.bass as bass
from concourse import mybir

F32, BF16, F16 = mybir.dt.float32, mybir.dt.bfloat16, mybir.dt.float16
I32, U32, U16 = mybir.dt.int32, mybir.dt.uint32, mybir.dt.uint16
ALU, ACT, AX = mybir.AluOpType, mybir.ActivationFunctionType, mybir.AxisListType

P = 128
B, S, D = 16, 256, 128
H, HD = 16, 8
TOK = B * S
NT = TOK // P
GT = 4
GN = GT * P
NG = NT // GT
E0, F0 = 8, 512
CAP = TOK // E0
E1, H1 = 8, 256
EPS = 1e-5
REP = 16
ROUNDS = 4
HALF = 65536.0
STEPS = [float(REP ** (ROUNDS - 1 - r)) for r in range(ROUNDS)]
DONE = [sum(STEPS[:r]) for r in range(ROUNDS + 1)]
PIECES = (slice(0, 10), slice(10, H))
COUMINUS_TAT = ((3, 6, 9, 12), (1, 4, 7, 10))
SUM_AFTER = 2
RUNS = ((0, 3), (3, 2), (5, 1))
KROWS = 96
MROW = 96
PACK = {"c_ident": P, "c_sums": 4 * (HD + 1), "c_block": P, "c_iota": P, "c_token": NT, "c_thr": 2 * ROUNDS, "c_low": E1 * E1, "w_q": P, "w_k": P, "w_v": P, "w_o": P,
        "cent": E0, "b_qk": 2, "ln_gb": 2, "w_g": E1, "b1m": 2 * E1}
PACK_H = {"c_pick": REP, "c_nge": P, "c_neq": P, "c_tri": P}
STACK = 2


def host_constants():
    p = np.arange(P)
    j = (p % REP).astype(np.float64)
    cols = [(0.5 - j * STEPS[r] + DONE[r]) * unit for unit in (HALF, 1.0) for r in range(ROUNDS)]
    first = (p % REP == 0)[:, None]
    earlier = first & (p[:, None] // REP < p[None, :] // REP)
    sums = np.zeros((P, 4 * (HD + 1)))
    for n in range(4):
        sums[32 * n:32 * n + HD + 1, n * (HD + 1):(n + 1) * (HD + 1)] = np.eye(HD + 1)
    low = np.tril(np.ones((E1, E1)), -1)[None].repeat(P, 0)
    return {
        "c_ident": np.eye(P, dtype=np.float32),
        "c_iota": np.arange(P, dtype=np.float32)[None].repeat(P, 0),
        "c_token": (np.arange(NT)[None] * P + p[:, None]).astype(np.float32),
        "c_sums": sums.astype(np.float32),
        "c_block": (p[:, None] // HD == p[None, :] // HD).astype(np.float32),
        "c_thr": np.stack(cols, 1).astype(np.float32),
        "c_pick": (p[:, None] % REP == np.arange(REP)[None]).astype(np.float16),
        "c_nge": (-1.0 * first * np.ones((1, P))).astype(np.float16),
        "c_neq": (1.0 * first - 1.0 * earlier).astype(np.float16),
        "c_tri": (p[:, None] < p[None, :]).astype(np.float16),
        "c_low": low.reshape(P, E1 * E1).astype(np.float32),
    }


class Chain:

    def __init__(self, engine, sem):
        self.engine, self.sem, self.base, self.n = engine, sem, 0, 0

    def link(self, ins):
        ins.then_inc(self.sem, 1)
        self.n += 1
        self.engine.wait_ge(self.sem, self.base + self.n)

    def mark(self, ins):
        ins.then_inc(self.sem, 1)
        self.n += 1

    def need(self):
        self.engine.wait_ge(self.sem, self.base + self.n)

    def loop(self, i, per):
        self.start, self.per, self.base = self.n, per, i * per

    def end(self, rounds):
        assert self.n - self.start == self.per, f"{self.n - self.start} links in a round"
        self.base, self.n = 0, self.start + self.per * rounds


def flat(ap):
    return ap.rearrange("p a n -> p (a n)")


def two_layers(nc, a, out):
    with ExitStack() as ctx:
        def sb(name, shape, dt=F32):
            return ctx.enter_context(nc.sbuf_tensor(name, shape, dt))

        def sem(name):
            return ctx.enter_context(nc.semaphore(name))

        bank = [ctx.enter_context(nc.psum_tensor(f"bank{i}", [P, 512], F32)) for i in range(8)]

        pack, pack_h = sb("pack", [P, sum(PACK.values())]), sb("pack_h", [P, sum(PACK_H.values())], F16)

        def packed(tile, widths, name):
            start = sum(list(widths.values())[:list(widths).index(name)])
            return tile[:, start:start + widths[name]]
        ident, pick_sums, block_mask, iota, token, thr, low_f, w_q, w_k, w_v, w_o, cent, b_qk, ln_gb, w_g, b1m_f = (
            packed(pack, PACK, n) for n in PACK)
        pick, nge, neq, tri = (packed(pack_h, PACK_H, n) for n in PACK_H)
        low = low_f.rearrange("p (a b) -> p a b", a=E1)
        b1m = b1m_f.rearrange("p (e t) -> p e t", e=E1)
        ident_b, ident_h = sb("ident_b", [P, P], BF16), sb("ident_h", [P, P], F16)
        ones_h, ones_f = sb("ones_h", [P, GN], F16), sb("ones_f", [P, P])
        b_v, b_o = sb("b_v", [P, P]), sb("b_o", [P, P])
        x_all = sb("x_all", [P, NT, D])
        xn_all = sb("xn_all", [P, NT, D])
        s_all = sb("s_all", [P, NT, D])
        v_all = sb("v_all", [P, NT, D])
        arena = sb("arena", [P, 12288])
        STACKS_END = STACK * 2 * H * S // 2
        stacks = arena[:, 0:STACKS_END].bitcast(BF16).rearrange("p (s w h t) -> p s w h t", s=STACK, w=2, h=H)
        keys = sb("keys", [P, 2, E0 - 1, GN], U16)
        stat6, mean, var = sb("stat6", [P, NT, 6]), sb("mean", [P, NT]), sb("var", [P, NT])
        spare = sb("spare", [P, NT])
        squares, roots_all, scales = (sb(n, [P, 2 * NT]) for n in ("squares", "roots_all", "scales"))
        roots, rstd, zscale = roots_all[:, :], scales[:, 0:NT], scales[:, NT:2 * NT]
        xst, zst = sb("xst", [P, 2, GT, D]), sb("zst", [P, 2, GT, D])
        parts_sb = sb("parts_sb", [P, 2 * 3 * 2 * 512], BF16)
        pool_tile = sb("pool_tile", [P, 8, 512])
        xT, zT = pool_tile[:, 0:2, :], pool_tile[:, 2:4, :]
        qkf = pool_tile[:, 4:8, :].rearrange("p (a w) n -> p a w n", a=2)
        probs = pool_tile
        parts = parts_sb[:, :].rearrange("p (a i w n) -> p a i w n", a=2, i=3, w=2)
        sT = s_all[0:E0, :, :].rearrange("p t d -> p (t d)")
        v_b = sb("v_b", [P, 2, 2, H, 32])
        o_b = sb("o_b", [P, 2, 4, S])
        vals, vT = sb("vals", [P, 2, P]), sb("vT", [P, 2, P])
        rec = sb("rec", [P, 2, H])
        mx = sb("mx", [P, H, 2])
        nm = sb("nm", [P, P], BF16)
        nmT = sb("nmT", [P, P], BF16)
        khi, key2 = sb("khi", [P, GN]), sb("key2", [P, GN])
        junk, ge, eq, pre = (sb(n, [P, GN], F16) for n in ("junk", "ge", "eq", "pre"))
        avail, eid = sb("avail", [P, GN], F16), sb("eid", [P, GN], F16)
        cnt = sb("cnt", [P, 3], F16)
        junk16 = sb("junk16", [P, REP])
        st = sb("st", [P, 6])
        T, L, BASE, DIG, QUOTA, MINUS_T = (st[:, i:i + 1] for i in range(6))
        eidT = sb("eidT", [P, NT])
        hot = sb("hot", [P, E0, NT], F16)
        key_f, key_h = khi[:, 0:S], khi[:, S:2 * S].bitcast(U16).rearrange("p (w f) -> p w f", w=2)
        tot, posa = khi[:, 0:E0 * NT], khi[:, E0 * NT:2 * E0 * NT]
        pos_f, pos = sb("pos_f", [P, NT]), sb("pos", [P, NT], I32)
        idx = sb("idx", [P, NT], I32)
        lo_i, hi_i = sb("lo_i", [P, NT], I32), sb("hi_i", [P, NT], I32)
        lo_f, hi_f = sb("lo_f", [P, NT]), sb("hi_f", [P, NT])
        at_low = arena[:, STACKS_END:STACKS_END + NT * P].rearrange("p (t q) -> p t q", t=NT)
        at_high = keys[:, :, :, :].rearrange("p w e n -> p (w e n)").bitcast(F32)[:, 0:NT * NT].rearrange(
            "p (t c) -> p t c", t=NT)

        def dram(name, shape, dt=F32):
            return nc.dram_tensor(name, shape, dt).ap()
        d_parts = dram("d_parts", [2, 3 * HD, H, TOK], BF16)
        d_score = dram("d_score", [E0, TOK])
        d_keys = dram("d_keys", [NG, 2, E0, GN], U16)
        d_z, d_ffn = dram("d_z", [TOK, D]), dram("d_ffn", [TOK, D])

        def carve(start, *shape):
            n = int(np.prod(shape))
            names = "abcd"[:len(shape)]
            dims = {c: k for c, k in zip(names, shape)}
            return arena[:, start:start + n].rearrange(f"p ({' '.join(names)}) -> p {' '.join(names)}", **dims)
        w1e, w2e = carve(0, 2, F0), carve(1024, 2, 4, D)
        zl, nT = carve(2048, 2, GT, D), carve(3072, 2, GN)
        hT, ho = carve(4096, 2, 4, GN), carve(8192, 2, GT, D)
        b1e, b2e = carve(9216, 2, 4), carve(9224, 2, D)
        xT_all, w1m, w2m = carve(0, NG, GN), carve(4096, E1, H1), carve(6144, E1, 2, D)
        hm, vsum = carve(8192, 2, 2, GN), carve(10240, B, D)
        routed = v_all
        wqkv8 = sb("wqkv8", [8, 4, D])
        bd_a, bd_v = sb("bd_a", [P, P]), sb("bd_v", [P, P])
        b2m = sb("b2m", [E1, D])
        xsum = sb("xsum", [P, B])
        vrhs = carve(8192, B, D)
        late = o_b[:, :, :, :].rearrange("p a b n -> p (a b n)")
        ds = late[:, 0:NT * H].rearrange("p (t h) -> p t h", t=NT)
        gl = late[:, 512:512 + NT * E1].rearrange("p (t e) -> p t e", t=NT)
        scm = late[:, 768:768 + 2 * GT * E1].rearrange("p (a t e) -> p a t e", a=2, t=GT)
        scT = late[0:E1, 1024:1024 + 2 * GN].rearrange("p (a n) -> p a n", a=2)
        small = sb("small", [P, NT])
        hmax = sb("hmax", [P, 2 * H])
        pairs = pool_tile[:, 0:4, :].rearrange("p a n -> p (a n)").rearrange("p (t e f) -> p t e f", t=NT, e=E1)
        pairs2 = pool_tile[:, 4:8, :].rearrange("p a n -> p (a n)").rearrange("p (t e f) -> p t e f", t=NT, e=E1)
        x1T = pool_tile[:, 0:2, :]
        acc, gate = xst, zst
        outs = pool_tile[:, 4:8, :].rearrange("p a (t d) -> p a t d", t=GT)

        x_in = [sem(f"x_in{g}") for g in range(NG)]
        w_in, chain_s, pool_s = sem("w_in"), sem("dve_chain"), sem("pool_chain")
        idents, zeroed, var_ok, root_ok = sem("idents"), sem("zeroed"), sem("var_ok"), sem("root_ok")
        st_ready, xn_copied, tr_done, t_evac = sem("st_ready"), sem("xn_copied"), sem("tr_done"), sem("t_evac")
        proj_done, qk_evac, v_evac, sc_evac = sem("proj_done"), sem("qk_evac"), sem("v_evac"), sem("sc_evac")
        rest1, part2, split_done = sem("rest1"), sem("part2"), sem("split_done")
        parts_out = [sem("parts_out0"), sem("parts_out1")]
        score_out, score_in = sem("score_out"), sem("score_in")
        key_ready, key_out, keys_in = sem("key_ready"), sem("key_out"), sem("keys_in")
        stack_in, mx_ready, mx_free = sem("stack_in"), sem("mx_ready"), sem("mx_free")
        nm_ready, nm_tr, nm_evac, nm_in = sem("nm_ready"), sem("nm_tr"), sem("nm_evac"), sem("nm_in")
        v_ready, lt_ready, lt_free = sem("v_ready"), sem("lt_ready"), sem("lt_free")
        pv_done, pv_free = sem("pv_done"), sem("pv_free")
        cnt_ready, cnt_sum, fin_ready, fin_sum = sem("cnt_ready"), sem("cnt_sum"), sem("fin_ready"), sem("fin_sum")
        ot_done, vals_ready, vt_done, vt_evac = sem("ot_done"), sem("vals_ready"), sem("vt_done"), sem("vt_evac")
        s_done, s_evac = sem("s_done"), sem("s_evac")
        thr_ready = sem("thr_ready")
        eid_ready, eid_tr, hot_ready, pos_mm = sem("eid_ready"), sem("eid_tr"), sem("hot_ready"), sem("pos_mm")
        z_out, zl_in, spread = ([sem(f"{n}{par}") for par in range(2)] for n in ("z_out", "zl_in", "spread"))
        low_ready, idx_mm, idx_ready = sem("low_ready"), sem("idx_mm"), sem("idx_ready")
        back_in = [sem(f"back_in{g}") for g in range(NG)]
        e_in = [sem("e_in0"), sem("e_in1")]
        zt_done, nt_ready, h_done, h_evac = sem("zt_done"), sem("nt_ready"), sem("h_done"), sem("h_evac")
        y_done, y_evac = sem("y_done"), sem("y_evac")
        gin_ready, silu_done, sg_ready = sem("gin_ready"), sem("silu_done"), sem("sg_ready")
        m_in, var1_ok, root1_ok, w8_done, w8_evac = (
            sem("m_in"), sem("var1_ok"), sem("root1_ok"), sem("w8_done"), sem("w8_evac"))
        st1_ready, tr1_done, x1_evac, x1_copied = sem("st1_ready"), sem("tr1_done"), sem("x1_evac"), sem("x1_copied")
        yg_done, yg_evac = sem("yg_done"), sem("yg_evac")
        lg_ready, exp_done, vrhs_ready, vs_mm, vs_evac = (
            sem("lg_ready"), sem("exp_done"), sem("vrhs_ready"), sem("vs_mm"), sem("vs_evac"))
        sct_in, sct_done, sct_evac, b2_done = sem("sct_in"), sem("sct_done"), sem("sct_evac"), sem("b2_done")
        hm_done, hm_evac, ym_done, ym_free = sem("hm_done"), sem("hm_evac"), sem("ym_done"), sem("ym_free")
        acc_ready, gate_done, out_ready, stored = sem("acc_ready"), sem("gate_done"), sem("out_ready"), sem("stored")

        x_t = a["x"].rearrange("(n p) d -> p n d", p=P)
        out_t = out.rearrange("(n p) d -> p n d", p=P)
        z_t = d_z.rearrange("(n p) d -> p n d", p=P)
        ffn_t = d_ffn.rearrange("(n p) d -> p n d", p=P)
        first_loads = [
            (pack[:, :], a["pack"]), (b_v[:, :], a["b_v"].broadcast_to([P, P])), (pack_h[:, :], a["pack_h"]),
            (b_o[:, :], a["b_o"].broadcast_to([P, P])), (b2m[:, :], a["b2m"]),
            (wqkv8[:, :, :].rearrange("p a n -> p (a n)"), a["w8"]),
        ]
        W_ALL = 16 * len(first_loads)
        PIECE_LOAD = 16 * 2 * len(RUNS)
        LOW_TILES = 8
        PARTS_STORE = 16 * 3 * 2
        QW = 4 * (HD + 1)
        ROUNDS_A = NG // 2
        PAIRS = (B - 2) // 2
        T1, Y1, G1 = (0, 5), (1, 3), (2, 4)
        TX, TZ = (0, 6), (1, 7)
        LT, MX, PV, CNT, TR = (2, 3), (0, 1, 7), 4, 5, 6
        MX_OF = [MX[u % 3] for u in range(15)] + [MX[1]]
        MX_LAG = [min(k for k in range(1, 17) if MX_OF[u - k] == MX_OF[u]) for u in range(16)]
        UNITS = [range(2 + -(-h * 14 // 11), min(16, 2 + -(-(h + 1) * 14 // 11))) if h < 11 else () for h in range(H)]
        E_LOADS = 16 * 4
        ROWS = 16 * GT
        EARLY = UNITS[0].stop
        SEARCH_LINKS = 30
        KEY_STORES = 2 * 2
        ENOUGH = float(2 * CAP - TOK)

        def hold(engine, semaphore, value):
            if not isinstance(value, int):
                value = engine.to_reg(value)
                engine.wait_ge(w_in, W_ALL)
            engine.wait_ge(semaphore, value)

        block = ctx.enter_context(nc.Block())

        @block.sync
        def _(sp):
            for g in range(NG):
                sp.dma_start(x_all[:, g * GT:(g + 1) * GT, :], x_t[:, g * GT:(g + 1) * GT, :]).then_inc(x_in[g], 16)
            def store_parts(g, par):
                hold(sp, split_done, g + 3)
                for part in range(3):
                    for w in range(2):
                        first = (part, 2 - part)[w] * HD
                        sp.dma_start(d_parts[w, first:first + HD, :, bass.ds(g * GN, GN)].rearrange("d h t -> h d t"),
                                     parts[:, par, part, w, :]).then_inc(parts_out[par], 16)

            def load_piece(b, slot, piece):
                hs = PIECES[piece]
                for w in range(2):
                    for start, n in RUNS:
                        first = (0, 3 - n)[w] * HD
                        sp.dma_start(stacks[start * HD:(start + n) * HD, slot, w, hs, :],
                                     d_parts[w, first:first + n * HD, hs, bass.ds(b * S, S)]).then_inc(stack_in, 16)

            def put_max(b, slot):
                hold(sp, nm_evac, b + 1)
                for part in range(2):
                    sp.dma_start(stacks[MROW + part:MROW + part + 1, slot, 0, :, :].rearrange(
                        "p h (c q) -> p (h c) q", c=2), nmT[32 * part:32 * part + 32, :]).then_inc(nm_in, 16)

            for g in range(2):
                store_parts(g, g)
            sp.wait_ge(zeroed, 1)
            sp.wait_ge(parts_out[0], PARTS_STORE)
            for n in range(4):
                store_parts(2 + n, n % 2)
                if n:
                    sp.wait_ge(stack_in, PIECE_LOAD * n)
                load_piece(n // 2, n // 2, n % 2)
            for g in range(6, NG):
                store_parts(g, g % 2)
            for par in range(2):
                sp.wait_ge(parts_out[par], PARTS_STORE * ROUNDS_A)
            put_max(0, 0)

            def refill(b, slot):
                for piece in range(2):
                    hold(sp, lt_ready, H * b + PIECES[piece].stop)
                    hold(sp, stack_in, PIECE_LOAD * (2 * (b + 2) + piece))
                    load_piece(b + 2, slot, piece)
                    if piece == 0:
                        hold(sp, nm_in, 32 * (b + 1))
                        put_max(b + 1, 1 - slot)

            with sp.Fori(0, B // 2 - 1) as i:
                for slot in range(2):
                    refill(i * 2 + slot, slot)
            sp.wait_ge(nm_in, 32 * (B - 1))
            put_max(B - 1, (B - 1) % 2)

            def load_expert(e, par):
                sp.dma_start(w1e[:, par], flat(a["w1"][:, bass.ds(e, 1), :])).then_inc(e_in[par], 16)
                sp.dma_start(w2e[:, par].rearrange("p t n -> p (t n)"),
                             flat(a["w2"][:, bass.ds(e, 1), :])).then_inc(e_in[par], 16)
                sp.dma_start(b1e[:, par], flat(a["b1"][:, bass.ds(e, 1), :])).then_inc(e_in[par], 16)
                sp.dma_start(b2e[:, par], a["b2"][bass.ds(e, 1), :].broadcast_to([P, D])).then_inc(e_in[par], 16)

            sp.wait_ge(lt_ready, H * B)
            sp.wait_ge(idx_mm, 1)
            load_expert(0, 0)
            load_expert(1, 1)
            with sp.Fori(0, E0 // 2 - 1) as i:
                for par in range(2):
                    hold(sp, y_evac, i * 2 + par + 3)
                    load_expert(i * 2 + par + 2, par)
            for par in range(2):
                sp.wait_ge(spread[par], ROWS * E0 // 2)
            for g in range(NG):
                at = slice(g * GT, (g + 1) * GT)
                sp.dma_start(routed[:, at, :], ffn_t[:, at, :]).then_inc(back_in[g], 16)

            sp.wait_ge(y_evac, E0 + 2)
            sp.dma_start(w1m.rearrange("p e n -> p (e n)"), a["w1m"]).then_inc(m_in, 16)
            sp.dma_start(w2m.rearrange("p e t n -> p (e t n)"), a["w2m"]).then_inc(m_in, 16)
            sp.sem_inc(stored, 32)
            with sp.Fori(0, ROUNDS_A) as i:
                for par in range(2):
                    g = i * 2 + par
                    hold(sp, out_ready, g + 1)
                    hold(sp, stored, (g + 2) * 16)
                    sp.dma_start(out_t[:, bass.ds(g * GT, GT), :], outs[:, par]).then_inc(stored, 16)
            sp.wait_ge(stored, 16 * (NG + 2))

        @block.gpsimd
        def _(gp):
            pc = Chain(gp, pool_s)
            gp.sem_inc(xn_copied, 2)
            pc.link(gp.memset(arena[:, 0:STACKS_END], 0.0))
            gp.memset(stacks[MROW:MROW + 2, :, 1, :, :], 1.0).then_inc(zeroed, 1)
            gp.wait_ge(zeroed, 1)
            pc.link(gp.memset(v_b[:, :, :, :, :], 0.0))
            pc.link(gp.memset(v_b[:, :, :, :, HD:HD + 1], 1.0))
            with gp.Fori(0, ROUNDS_A) as i:
                for par in range(2):
                    g = i * 2 + par
                    hold(gp, st_ready, g + 1)
                    gp.dma_start(z_t[:, bass.ds(g * GT, GT), :], zst[:, par]).then_inc(z_out[par], 16)
                    gp.tensor_copy(xn_all[:, bass.ds(g * GT, GT), :], xst[:, par]).then_inc(xn_copied, 1)

            def copy_v(b, par):
                hold(gp, pv_done, b * 4 + 4)
                gp.tensor_copy(v_b[:, par, :, :, 0:HD], v_all[:, bass.ds(b * 2, 2), :].rearrange(
                    "p k (h d) -> p k h d", h=H)).then_inc(v_ready, 1)

            gp.wait_ge(v_evac, NG + 1)
            for par in range(2):
                copy_v(par, par)
            gp.wait_ge(sc_evac, NG + 1)
            gp.dma_start(d_score, sT).then_inc(score_out, 16)
            gp.wait_ge(score_out, 16)
            for c in range(2):
                gp.dma_start(key_f[c * P // 2:(c + 1) * P // 2, :], d_score.rearrange(
                    "e (g c f) -> c g e f", c=2, f=S)[c]).then_inc(score_in, 16)
            gp.wait_ge(key_ready, 1)
            for w in range(2):
                for c in range(2):
                    gp.dma_start(d_keys[:, w, :, c * S:(c + 1) * S],
                                 key_h[c * P // 2:(c + 1) * P // 2, w, :]).then_inc(key_out, 16)
            gp.wait_ge(key_out, 16 * KEY_STORES)
            for g in range(NG):
                gp.dma_start(keys[g * REP:(g + 1) * REP, :, :, :], d_keys[g:g + 1, :, 0:E0 - 1, :].rearrange(
                    "a w e n -> a w (e n)").broadcast_to([REP, 2, (E0 - 1) * GN])).then_inc(keys_in, 16)
            with gp.Fori(1, B // 2) as i:
                for par in range(2):
                    copy_v(i * 2 + par, par)

            def gather(e):
                if e >= 2:
                    gp.wait_ge(zt_done, e - 1)
                for t in range(GT):
                    gp.indirect_dma_start(zl[:, e % 2, t, :], None, d_z, bass.IndirectOffsetOnAxis(
                        ap=idx[:, e * GT + t:e * GT + t + 1], axis=0)).then_inc(zl_in[e % 2], 16)

            for par in range(2):
                gp.wait_ge(z_out[par], 16 * ROUNDS_A)
            gp.wait_ge(idx_ready, 1)
            gp.wait_ge(lt_ready, H * B)
            gather(0)
            gather(1)
            for e in range(E0):
                if e + 2 < E0:
                    gather(e + 2)
                gp.wait_ge(y_evac, e + 3)
                for t in range(GT):
                    gp.indirect_dma_start(d_ffn, bass.IndirectOffsetOnAxis(
                        ap=idx[:, e * GT + t:e * GT + t + 1], axis=0), ho[:, e % 2, t, :], None).then_inc(
                            spread[e % 2], 16)
            for g in range(NG + 1):
                if g < NG:
                    at = slice(g * GT, (g + 1) * GT)
                    gp.wait_ge(back_in[g], 16)
                    gp.tensor_tensor(routed[:, at, :], routed[:, at, :], xn_all[:, at, :],
                                     ALU.add).then_inc(gin_ready, 1)
                if g > 0:
                    at = slice((g - 1) * GT, g * GT)
                    gp.wait_ge(silu_done, g)
                    gp.tensor_tensor(s_all[:, at, :], s_all[:, at, :], routed[:, at, :], ALU.mult).then_inc(sg_ready, 1)
            gp.sem_inc(x1_copied, 2)
            with gp.Fori(0, ROUNDS_A) as i:
                for par in range(2):
                    g = i * 2 + par
                    hold(gp, x1_evac, g + 1)
                    gp.tensor_copy(flat(xT_all[:, bass.ds(g, 1), :]), x1T[:, par]).then_inc(x1_copied, 1)

        @block.scalar
        def _(act):
            for dst, src in first_loads:
                nc.scalar.dma_start(dst, src).then_inc(w_in, 16)
            act.wait_ge(var_ok, 1)
            nc.scalar.activation(roots, roots, ACT.Sqrt).then_inc(root_ok, 1)
            act.wait_ge(w_in, W_ALL)
            act.sem_inc(sc_evac, 1)

            def turned(g, par):
                act.wait_ge(tr_done, g + 1)
                nc.scalar.activation(xT[:, par], bank[TX[par]][:, :], ACT.Copy)
                nc.scalar.activation(zT[:, par], bank[TZ[par]][:, :], ACT.Identity, bias=ln_gb[:, 1:2],
                                     scale=ln_gb[:, 0:1]).then_inc(t_evac, 1)

            def projected(g, par, more, stored_before):
                act.wait_ge(proj_done, g + 1)
                act.wait_ge(split_done, g + 1)
                if stored_before is not None:
                    act.wait_ge(parts_out[par], stored_before)
                for w in range(2):
                    nc.scalar.activation(qkf[:, par, w], bank[2 + w][:, :], ACT.Identity, bias=b_qk[:, w:w + 1])
                for w in range(2):
                    ins = nc.scalar.activation(parts[:, par, 0, w], bank[2 + w][:, :], ACT.Identity,
                                               bias=b_qk[:, w:w + 1])
                ins.then_inc(qk_evac, 1)
                nc.scalar.activation(sT[:, bass.ds(g * GN, GN)], bank[5][0:E0, :], ACT.Copy).then_inc(sc_evac, 1)
                if more:
                    turned(g + 2, par)
                act.wait_ge(rest1, g + 1)
                nc.scalar.activation(parts[:, par, 1], qkf[:, par], ACT.Copy).then_inc(part2, 1)

            for par in range(2):
                turned(par, par)
            for par in range(2):
                projected(par, par, True, None)
            with act.Fori(1, ROUNDS_A - 1) as i:
                for par in range(2):
                    projected(i * 2 + par, par, True, i * PARTS_STORE)
            for par in range(2):
                projected(NG - 2 + par, par, False, (ROUNDS_A - 1) * PARTS_STORE)

            act.sem_inc(lt_free, 2)
            act.sem_inc(pv_free, 1)

            def keep_o(m, par, quad):
                act.wait_ge(pv_done, m + 9)
                if quad == 0:
                    act.wait_ge(ot_done, m // 4 + 1)
                nc.scalar.activation(o_b[:, par, quad, :], bank[PV][:, 0:S], ACT.Copy).then_inc(pv_free, 1)

            def turn_vals(b):
                act.wait_ge(vt_done, b + 1)
                nc.scalar.activation(vT[:, :, :].rearrange("p a n -> p (a n)"), bank[TR][:, 0:2 * P],
                                     ACT.Copy).then_inc(vt_evac, 1)

            def count(k, half):
                act.wait_ge(thr_ready, k + 1)
                with nc.allow_low_precision(reason="whole numbers up to 512 are exact"):
                    nc.scalar.activation(junk[:, :], (khi, key2)[half][:, :], ACT.Sign, bias=MINUS_T,
                                         accum_out=cnt[:, 0:1]).then_inc(cnt_ready, 1)

            def batch(b, par, before, half=None):
                for h in range(H):
                    if h % 4 == 0:
                        act.wait_ge(pv_done, b * 4 + h // 4 + 7)
                    act.wait_ge(lt_ready, b * H + h + 1)
                    nc.scalar.activation(probs[:, h % 8, :], bank[LT[h % 2]][:, :], ACT.Exp,
                                         scale=float(HD) ** -0.5).then_inc(lt_free, 1)
                    if h % 4 == 0 and h >= 8:
                        keep_o(b * 4 + h // 4 - 2, par, h // 4 - 2)
                    elif h % 4 == 0 and before:
                        keep_o(b * 4 + h // 4 - 2, 1 - par, h // 4 + 2)
                    if half is not None and h in COUMINUS_TAT[half]:
                        count((b - 1) * ROUNDS + COUMINUS_TAT[half].index(h), half)
                    if before and h == 9:
                        turn_vals(b - 1)

            batch(0, 0, False)
            with act.Fori(0, PAIRS) as i:
                batch(i * 2 + 1, 1, True, 0)
                batch(i * 2 + 2, 0, True, 1)
            batch(B - 1, 1, True)
            keep_o(4 * B - 2, 1, 2)
            keep_o(4 * B - 1, 1, 3)
            turn_vals(B - 1)

            act.sem_inc(h_evac, 2)

            def turn_z(e, par):
                act.wait_ge(zt_done, e + 1)
                nc.scalar.activation(nT[:, par], bank[0][:, :], ACT.Identity, bias=ln_gb[:, 1:2],
                                     scale=ln_gb[:, 0:1]).then_inc(nt_ready, 1)

            def expert(e, par, more):
                for ft in range(4):
                    act.wait_ge(h_done, e * 4 + ft + 1)
                    nc.scalar.activation(hT[:, par, ft, :], bank[1 + ft % 2][:, :], ACT.Gelu_apprx_tanh,
                                         bias=b1e[:, par, ft:ft + 1]).then_inc(h_evac, 1)
                if more:
                    turn_z(e + 1, 1 - par)

            turn_z(0, 0)
            with act.Fori(0, E0 // 2 - 1) as i:
                for par in range(2):
                    expert(i * 2 + par, par, True)
            expert(E0 - 2, 0, True)
            expert(E0 - 1, 1, False)

            for g in range(NG):
                act.wait_ge(gin_ready, g + 1)
                v = routed[:, g * GT:(g + 1) * GT, :]
                nc.scalar.activation(v, v, ACT.Silu).then_inc(silu_done, 1)

            act.wait_ge(var1_ok, 1)
            nc.scalar.activation(roots[:, 0:NT], roots[:, 0:NT], ACT.Sqrt).then_inc(root1_ok, 1)
            with act.Fori(0, ROUNDS_A) as i:
                for par in range(2):
                    g = i * 2 + par
                    act.wait_ge(tr1_done, g + 3)
                    act.wait_ge(x1_copied, g + 1)
                    for c in range(2):
                        ins = nc.scalar.activation(x1T[:, par, c * S:(c + 1) * S], bank[T1[par]][:, c * S:(c + 1) * S],
                                                   ACT.Copy, accum_out=xsum[:, bass.ds(g * 2 + c, 1)])
                    ins.then_inc(x1_evac, 1)
            for r in range(B // 4):
                act.wait_ge(vs_mm, r + 1)
                nc.scalar.activation(vsum[:, r * 4:(r + 1) * 4, :].rearrange("p c n -> p (c n)"),
                                     bank[3 + r % 2][:, :], ACT.Copy).then_inc(vs_evac, 1)
            act.wait_ge(lg_ready, 1)
            nc.scalar.activation(gl, gl, ACT.Exp).then_inc(exp_done, 1)
            act.wait_ge(lg_ready, 2)
            nc.scalar.activation(ds, ds, ACT.Exp, scale=float(D) ** -0.5).then_inc(exp_done, 1)
            act.sem_inc(hm_evac, 2)

            def keep_scores(g, par):
                act.wait_ge(sct_done, g + 1)
                nc.scalar.activation(scT[:, par, :], bank[6][0:E1, :], ACT.Copy).then_inc(sct_evac, 1)

            def hidden_relu(g, e):
                act.wait_ge(hm_done, (g * E1 + e) + 1)
                act.wait_ge(ym_done, (g * E1 + e) + 1)
                for t in range(2):
                    ins = nc.scalar.activation(hm[:, e % 2, t, :], bank[2 * (e % 2) + t][:, :], ACT.Relu,
                                               bias=b1m[:, e, t:t + 1])
                ins.then_inc(hm_evac, 1)

            def silu(g, par):
                act.wait_ge(acc_ready, g + 1)
                nc.scalar.activation(gate[:, par], acc[:, par], ACT.Silu).then_inc(gate_done, 1)

            def group(g, par, before, more):
                for e in range(1, E1):
                    hidden_relu(g, e)
                    if e == 1 and before:
                        silu(g - 1, 1 - par)
                if more:
                    keep_scores(g + 1, 1 - par)
                    hidden_relu(g + 1, 0)

            keep_scores(0, 0)
            hidden_relu(0, 0)
            group(0, 0, False, True)
            with act.Fori(0, ROUNDS_A - 1) as i:
                for n in range(2):
                    group(i * 2 + n + 1, 1 - n, True, True)
            group(NG - 1, 1, True, False)
            silu(NG - 1, 1)

        @block.tensor
        def _(pe):
            mm, turn = nc.tensor.matmul, nc.tensor.transpose
            pe.wait_ge(w_in, W_ALL)
            pe.wait_ge(idents, 1)

            def turn_rows_a(g, par):
                pe.wait_ge(st_ready, g + 1)
                for n, src in ((TX[par], xst), (TZ[par], zst)):
                    for t in range(GT):
                        ins = turn(bank[n][:, t * P:(t + 1) * P], src[:, par, t, :], ident[:, :])
                ins.then_inc(tr_done, 1)

            def projections(g, par):
                pe.wait_ge(t_evac, g + 1)
                pe.wait_ge(sc_evac, g + 1)
                mm(bank[2][:, :], w_q[:, :], xT[:, par], start=True, stop=True)
                mm(bank[3][:, :], w_k[:, :], xT[:, par], start=True, stop=True)
                pe.wait_ge(v_evac, g + 1)
                for t in range(GT):
                    mm(bank[4][:, t * P:(t + 1) * P], xT[:, par, t * P:(t + 1) * P], w_v[:, :],
                       start=True, stop=True)
                mm(bank[5][0:E0, :], cent[:, :], zT[:, par], start=True, stop=True).then_inc(proj_done, 1)

            turn_rows_a(0, 0)
            turn_rows_a(1, 1)
            projections(0, 0)
            with pe.Fori(0, ROUNDS_A - 1) as i:
                for par in range(2):
                    g = i * 2 + par + 1
                    pe.wait_ge(t_evac, g)
                    turn_rows_a(g + 1, par)
                    projections(g, 1 - par)
            projections(NG - 1, 1)

            pe.sem_inc(ot_done, 2)
            pe.sem_inc(pv_done, 8)
            pe.wait_ge(sc_evac, NG + 1)
            pe.wait_ge(v_evac, NG + 1)

            def max_unit(b, slot, u):
                for piece in range(2):
                    if 2 * (u // 2) == PIECES[piece].start and u % 2 == 0:
                        pe.wait_ge(stack_in, (2 * b + piece + 1) * PIECE_LOAD)
                if not (isinstance(b, int) and b == 0 and u < MX_LAG[u]):
                    pe.wait_ge(mx_free, b * 16 + u - MX_LAG[u] + 3)
                qt = u % 2
                for n in range(2):
                    h = u // 2 * 2 + n
                    ins = mm(bank[MX_OF[u]][:, n * S:(n + 1) * S], stacks[0:KROWS, slot, 0, h, qt * P:(qt + 1) * P],
                             stacks[0:KROWS, slot, 1, h, :], start=True, stop=True)
                ins.then_inc(mx_ready, 1)

            def logits(b, slot, h):
                pe.wait_ge(lt_free, b * H + h + 1)
                for kt in range(2):
                    ins = mm(bank[LT[h % 2]][:, kt * S:(kt + 1) * S], stacks[0:MROW + 2, slot, 1, h, kt * P:(kt + 1) * P],
                             stacks[0:MROW + 2, slot, 0, h, :], start=True, stop=True)
                ins.then_inc(lt_ready, 1)

            def weigh(m, quad, par, kt):
                if kt == 0:
                    if quad == 0:
                        pe.wait_ge(v_ready, m // 4 + 1)
                    pe.wait_ge(lt_free, m * 4 + 6)
                    pe.wait_ge(pv_free, m + 1)
                for n in range(4):
                    h = quad * 4 + n
                    ins = mm(bank[PV][32 * n:32 * n + 32, 0:S], v_b[:, par, kt, h, :],
                             probs[:, h % 8, kt * S:(kt + 1) * S], start=kt == 0, stop=kt == 1,
                             tile_position=(0, 32 * n))
                if kt == 1:
                    ins.then_inc(pv_done, 1)

            def turn_o(b, par):
                pe.wait_ge(pv_free, b * 4 + 5)
                pe.wait_ge(s_evac, b + 1)
                for qt in range(2):
                    for quad in range(4):
                        ins = mm(bank[TR][:, (qt * 4 + quad) * QW:(qt * 4 + quad + 1) * QW],
                                 o_b[:, par, quad, qt * P:(qt + 1) * P], pick_sums, start=True, stop=True)
                ins.then_inc(ot_done, 1)

            def turn_v(b):
                pe.wait_ge(vals_ready, b + 1)
                for qt in range(2):
                    ins = turn(bank[TR][:, qt * P:(qt + 1) * P], vals[:, qt, :], ident[:, :])
                ins.then_inc(vt_done, 1)

            def project(b):
                pe.wait_ge(vt_evac, b + 1)
                for qt in range(2):
                    ins = mm(bank[TR][:, qt * P:(qt + 1) * P], vT[:, qt, :], w_o[:, :], start=True, stop=True)
                ins.then_inc(s_done, 1)

            def count(k):
                pe.wait_ge(cnt_ready, k + 1)
                mm(bank[CNT][:, 0:REP], cnt[:, 0:1].broadcast_to([P, P]), pick[:, :],
                   start=True, stop=True).then_inc(cnt_sum, 1)

            def turn_max(b):
                pe.wait_ge(nm_ready, b + 1)
                turn(bank[TR][:, :].bitcast(BF16)[:, 6 * P:7 * P], nm[:, :], ident_b[:, :]).then_inc(nm_tr, 1)

            def batch(b, par, before, ahead, ahead2, half=None, e=None, beside=None):
                pe.wait_ge(nm_in, (b + 1) * 32)
                for h in range(H):
                    logits(b, par, h)
                    if ahead:
                        for u in UNITS[h]:
                            max_unit(b + 1, 1 - par, u)
                    if h % 4 >= 2:
                        if h > 3:
                            weigh(b * 4 + h // 4 - 1, h // 4 - 1, par, h % 4 - 2)
                        elif before:
                            weigh(b * 4 - 1, 3, 1 - par, h % 4 - 2)
                    if half is not None and h - SUM_AFTER in COUMINUS_TAT[half]:
                        count((b - 1) * ROUNDS + COUMINUS_TAT[half].index(h - SUM_AFTER))
                    if before and h == 6:
                        turn_o(b - 1, 1 - par)
                    if before and h == 9:
                        turn_v(b - 1)
                    if before and h == 11:
                        project(b - 1)
                    if ahead and h == 11:
                        turn_max(b + 1)
                    if beside and h in beside:
                        beside[h]()
                if ahead2:
                    for u in range(2):
                        max_unit(b + 2, par, u)
                if half == 1:
                    pe.wait_ge(fin_ready, e + 1)
                    mm(bank[CNT][:, 0:1], nge[:, :], cnt[:, 1:2], start=True, stop=False)
                    mm(bank[CNT][:, 0:1], neq[:, :], cnt[:, 2:3], start=False, stop=True).then_inc(fin_sum, 1)

            for u in range(16):
                max_unit(0, 0, u)
            turn_max(0)
            for u in range(2):
                max_unit(1, 1, u)
            batch(0, 0, False, True, True)
            with pe.Fori(0, PAIRS - 1) as i:
                batch(i * 2 + 1, 1, True, True, True, 0, i)
                batch(i * 2 + 2, 0, True, True, True, 1, i)
            batch(B - 3, 1, True, True, True, 0, PAIRS - 1)
            batch(B - 2, 0, True, True, False, 1, PAIRS - 1)

            def turn_experts():
                pe.wait_ge(eid_ready, PAIRS)
                for c in range(GT):
                    ins = turn(bank[CNT][:, :].bitcast(F16)[:, c * P:(c + 1) * P], eid[:, c * P:(c + 1) * P],
                               ident_h[:, :])
                ins.then_inc(eid_tr, 1)

            def add_places():
                pe.wait_ge(hot_ready, 1)
                hot_f = hot[:, :, :].rearrange("p e t -> p (e t)")
                mm(bank[0][:, 0:E0 * NT], tri[:, :], hot_f, start=True, stop=True)
                mm(bank[1][:, 0:E0 * NT], ones_h[:, 0:P], hot_f, start=True, stop=True).then_inc(pos_mm, 1)

            batch(B - 1, 1, True, False, False, beside={3: turn_experts, 6: add_places})
            for kt in range(2):
                weigh(4 * B - 1, 3, 1, kt)
            for t in range(NT):
                if t % LOW_TILES == 0:
                    pe.wait_ge(low_ready, t // LOW_TILES + 1)
                ins = mm(bank[7][:, 0:NT], at_low[:, t, :], at_high[:, t, :], start=t == 0, stop=t == NT - 1)
            ins.then_inc(idx_mm, 1)
            turn_o(B - 1, 1)
            turn_v(B - 1)
            project(B - 1)

            def turn_rows(e, par, round_):
                pe.wait_ge(zl_in[par], (round_ + 1) * ROWS)
                for t in range(GT):
                    ins = turn(bank[0][:, t * P:(t + 1) * P], zl[:, par, t, :], ident[:, :])
                ins.then_inc(zt_done, 1)

            def expert(e, par, round_, more):
                pe.wait_ge(nt_ready, e + 1)
                pe.wait_ge(e_in[par], (round_ + 1) * E_LOADS)
                for ft in range(4):
                    pe.wait_ge(h_evac, e * 4 + ft + 1)
                    mm(bank[1 + ft % 2][:, :], w1e[:, par, ft * P:(ft + 1) * P], nT[:, par],
                       start=True, stop=True).then_inc(h_done, 1)
                if more:
                    turn_rows(e + 1, 1 - par, round_ + par)
                pe.wait_ge(h_evac, e * 4 + 6)
                pe.wait_ge(y_evac, e + 1)
                for t in range(GT):
                    for ft in range(4):
                        ins = mm(bank[3 + par][:, t * P:(t + 1) * P], hT[:, par, ft, t * P:(t + 1) * P],
                                 w2e[:, par, ft, :], start=ft == 0, stop=ft == 3)
                ins.then_inc(y_done, 1)

            pe.wait_ge(pv_free, 4 * B + 1)
            turn_rows(0, 0, 0)
            with pe.Fori(0, E0 // 2 - 1) as i:
                for par in range(2):
                    expert(i * 2 + par, par, i, True)
            expert(E0 - 2, 0, E0 // 2 - 1, True)
            expert(E0 - 1, 1, E0 // 2 - 1, False)

            pe.wait_ge(s_evac, B + 1)
            mm(bank[6][:, 0:P], wqkv8[:, 0, :], wqkv8[:, 1, :], start=True, stop=True)
            mm(bank[6][:, P:2 * P], wqkv8[:, 2, :], wqkv8[:, 3, :], start=True, stop=True).then_inc(w8_done, 1)
            pe.sem_inc(tr1_done, 2)
            pe.wait_ge(w8_evac, 2)

            def turn_x1(g, par):
                pe.wait_ge(st1_ready, g + 1)
                for t in range(GT):
                    ins = turn(bank[T1[par]][:, t * P:(t + 1) * P], xst[:, par, t, :], ident[:, :])
                ins.then_inc(tr1_done, 1)

            def products_x1(g, par):
                pe.wait_ge(x1_evac, g + 1)
                pe.wait_ge(yg_evac, g + 1)
                for t in range(GT):
                    mm(bank[Y1[par]][:, t * P:(t + 1) * P], x1T[:, par, t * P:(t + 1) * P], bd_a[:, :],
                       start=True, stop=True)
                for t in range(GT):
                    ins = mm(bank[G1[par]][:, t * E1:(t + 1) * E1], x1T[:, par, t * P:(t + 1) * P], w_g[:, :],
                             start=True, stop=True)
                ins.then_inc(yg_done, 1)

            turn_x1(0, 0)
            turn_x1(1, 1)
            products_x1(0, 0)
            with pe.Fori(0, ROUNDS_A - 1) as i:
                for par in range(2):
                    g = i * 2 + par + 1
                    products_x1(g, 1 - par)
                    turn_x1(g + 1, par)
            products_x1(NG - 1, 1)
            for r in range(B // 4):
                if r == 0:
                    pe.wait_ge(vrhs_ready, 1)
                    pe.wait_ge(yg_evac, NG + 2)
                if r >= 2:
                    pe.wait_ge(vs_evac, r - 1)
                mm(bank[3 + r % 2][:, :], ones_f[:, :], vrhs[:, 4 * r:4 * r + 4, :].rearrange("p c n -> p (c n)"),
                   start=True, stop=True).then_inc(vs_mm, 1)
            pe.wait_ge(vs_evac, B // 4)
            pe.wait_ge(m_in, 32)
            pe.sem_inc(ym_done, 2)

            def turn_scores(g, par):
                pe.wait_ge(sct_in, g + 1)
                for t in range(GT):
                    ins = turn(bank[6][0:E1, t * P:(t + 1) * P], scm[:, par, t, :], ident[:, :])
                ins.then_inc(sct_done, 1)

            def hidden(g, e):
                pe.wait_ge(hm_evac, g * E1 + e + 1)
                for t in range(2):
                    ins = mm(bank[2 * (e % 2) + t][:, :], w1m[:, e, t * P:(t + 1) * P],
                             flat(xT_all[:, bass.ds(g, 1), :]), start=True, stop=True)
                ins.then_inc(hm_done, 1)

            def group(g, par, more):
                pe.wait_ge(sct_evac, g + 1)
                for t in range(GT):
                    ins = mm(bank[7][:, t * P:(t + 1) * P], scT[:, par, t * P:(t + 1) * P], b2m[:, :],
                             start=True, stop=True)
                ins.then_inc(b2_done, 1)
                for e in range(E1):
                    if e + 1 < E1:
                        hidden(g, e + 1)
                    elif more:
                        turn_scores(g + 1, 1 - par)
                        hidden(g + 1, 0)
                    pe.wait_ge(hm_evac, g * E1 + e + 3)
                    pe.wait_ge(ym_free, g * E1 + e + 1)
                    for t in range(GT):
                        for ft in range(2):
                            ins = mm(bank[4 + e % 2][:, t * P:(t + 1) * P], hm[:, e % 2, ft, t * P:(t + 1) * P],
                                     w2m[:, e, ft, :], start=ft == 0, stop=ft == 1)
                    ins.then_inc(ym_done, 1)

            turn_scores(0, 0)
            hidden(0, 0)
            group(0, 0, True)
            with pe.Fori(0, ROUNDS_A - 1) as i:
                for n in range(2):
                    group(i * 2 + n + 1, 1 - n, True)
            group(NG - 1, 1, False)

        @block.vector
        def _(dve):
            ch = Chain(dve, chain_s)
            v = nc.vector
            v.memset(ones_h[:, :], 1.0)
            v.memset(ones_f[:, :], 1.0)
            v.memset(eid[:, :], 0.0)
            v.memset(nm[:, :], 0.0)
            v.memset(avail[:, :], 1.0)
            dve.sem_inc(v_evac, 1)
            dve.sem_inc(split_done, 2)

            def statistics():
                s6 = [stat6[:, :, k] for k in range(6)]
                ch.link(v.tensor_tensor(mean[:, :], s6[1], s6[4], ALU.add))
                ch.link(v.tensor_scalar(mean[:, :], mean[:, :], 0.5, None, ALU.mult))
                ch.link(v.tensor_tensor(spare[:, :], s6[1], s6[4], ALU.subtract))
                ch.link(v.tensor_tensor(spare[:, :], spare[:, :], spare[:, :], ALU.mult))
                ch.link(v.tensor_tensor(var[:, :], s6[2], s6[5], ALU.add))
                ch.link(v.scalar_tensor_tensor(var[:, :], spare[:, :], D / 4.0, var[:, :], ALU.mult, ALU.add))
                ch.link(v.tensor_scalar(var[:, :], var[:, :], 1.0 / D, None, ALU.mult))

            def both_scales(ready, rooted, n=2):
                sq, rt, sc = squares[:, 0:n * NT], roots_all[:, 0:n * NT], scales[:, 0:n * NT]
                ch.link(v.tensor_scalar(sq[:, 0:NT], var[:, :], EPS, None, ALU.add))
                if n == 2:
                    ch.link(v.tensor_scalar(sq[:, NT:], var[:, :], 1 + EPS, EPS * EPS, ALU.mult, ALU.add))
                v.tensor_copy(rt, sq).then_inc(ready, 1)
                dve.wait_ge(rooted, 1)
                ch.link(v.reciprocal(sc, rt))
                ch.link(v.tensor_tensor(rt, sc, sc, ALU.mult))
                ch.link(v.tensor_tensor(rt, rt, sq, ALU.mult))
                ch.link(v.tensor_scalar(rt, rt, -0.5, 1.5, ALU.mult, ALU.add))
                ch.link(v.tensor_tensor(sc, sc, rt, ALU.mult))

            for g in range(NG):
                dve.wait_ge(x_in[g], 16)
                for t in range(g * GT, (g + 1) * GT):
                    ins = v.bn_stats(stat6[:, t, :], x_all[:, t, :])
            ch.link(ins)
            statistics()
            both_scales(var_ok, root_ok)
            dve.wait_ge(w_in, W_ALL)
            v.tensor_copy(ident_b[:, :], ident[:, :])
            v.tensor_copy(ident_h[:, :], ident[:, :]).then_inc(idents, 1)

            def normalise(g, par):
                for dst, by in ((xst, rstd), (zst, zscale)):
                    for t in range(GT):
                        at = bass.ds(g * GT + t, 1)
                        ins = v.tensor_scalar(dst[:, par, t, :], flat(x_all[:, at, :]), mean[:, at], by[:, at],
                                              ALU.subtract, ALU.mult)
                ins.then_inc(st_ready, 1)

            def keep_v_and_split(g, par, round_, more):
                dve.wait_ge(proj_done, g + 1)
                v.tensor_tensor(v_all[:, bass.ds(g * GT, GT), :],
                                bank[4][:, :].rearrange("p (t n) -> p t n", t=GT),
                                b_v[:, :].unsqueeze(1).broadcast_to([P, GT, P]), ALU.add).then_inc(v_evac, 1)
                if more:
                    dve.wait_ge(xn_copied, g + 3)
                    dve.wait_ge(z_out[par], (round_ + 1) * 16)
                    normalise(g + 2, par)
                dve.wait_ge(qk_evac, g + 1)
                v.tensor_tensor(qkf[:, par], qkf[:, par], parts[:, par, 0], ALU.subtract).then_inc(rest1, 1)
                dve.wait_ge(part2, g + 1)
                v.tensor_tensor(parts[:, par, 2], qkf[:, par], parts[:, par, 1],
                                ALU.subtract).then_inc(split_done, 1)

            for par in range(2):
                normalise(par, par)
            with dve.Fori(0, ROUNDS_A - 1) as i:
                for par in range(2):
                    keep_v_and_split(i * 2 + par, par, i, True)
            for par in range(2):
                keep_v_and_split(NG - 2 + par, par, None, False)

            dve.sem_inc(mx_free, 2)
            dve.sem_inc(s_evac, 1)

            def row_max(b, u):
                dve.wait_ge(mx_ready, b * 16 + u + 1)
                hp, qt = u // 2, u % 2
                return v.tensor_reduce(mx[:, 2 * hp:2 * hp + 2, qt],
                                       bank[MX_OF[u]][:, :].rearrange("p (h k) -> p h k", h=2),
                                       AX.X, ALU.max).then_inc(mx_free, 1)

            def split_max(b):
                dve.wait_ge(mx_free, b * 16 + 18)
                mx_f, hi, lo = mx[:, :, :].rearrange("p h c -> p (h c)"), nm[:, 0:2 * H], nm[:, 2 * H:4 * H]
                ch.link(v.tensor_scalar(hi, mx_f, -1.0, None, ALU.mult))
                v.scalar_tensor_tensor(lo, mx_f, -1.0, hi, ALU.mult,
                                       ALU.subtract).then_inc(nm_ready, 1)

            def keep_max(b):
                dve.wait_ge(nm_tr, b + 1)
                if not (isinstance(b, int) and b == 0):
                    dve.wait_ge(nm_in, b * 32)
                v.tensor_copy(nmT[:, :], bank[TR][:, :].bitcast(BF16)[:, 6 * P:7 * P]).then_inc(nm_evac, 1)

            def values(b):
                dve.wait_ge(ot_done, b + 3)
                for qt in range(2):
                    o = bank[TR][:, qt * 4 * QW:(qt + 1) * 4 * QW].rearrange("p (h n) -> p h n", n=HD + 1)
                    ins = v.reciprocal(rec[:, qt, :], o[:, :, HD])
                ch.link(ins)
                for qt in range(2):
                    o = bank[TR][:, qt * 4 * QW:(qt + 1) * 4 * QW].rearrange("p (h n) -> p h n", n=HD + 1)
                    ins = v.tensor_tensor(vals[:, qt, :].rearrange("p (h n) -> p h n", n=HD), o[:, :, 0:HD],
                                          rec[:, qt, :].unsqueeze(2).broadcast_to([P, H, HD]), ALU.mult)
                ins.then_inc(vals_ready, 1)

            def keep_s(b):
                dve.wait_ge(s_done, b + 1)
                for qt in range(2):
                    ins = v.tensor_tensor(flat(s_all[:, bass.ds(b * 2 + qt, 1), :]), bank[TR][:, qt * P:(qt + 1) * P],
                                          b_o[:, :], ALU.add)
                ins.then_inc(s_evac, 1)

            def begin_high(e):
                v.tensor_copy(MINUS_T, thr[:, 0:1])
                v.tensor_copy(BASE, thr[:, 1:2])
                v.memset(L, 0.0)
                v.scalar_tensor_tensor(khi[:, :], flat(keys[:, 0, bass.ds(e, 1), :]), HALF, avail[:, :],
                                       ALU.mult, ALU.mult).then_inc(thr_ready, 1)

            def begin_low(e, k):
                v.tensor_copy(MINUS_T, thr[:, ROUNDS:ROUNDS + 1])
                v.tensor_copy(BASE, thr[:, ROUNDS + 1:ROUNDS + 2])
                ch.link(v.tensor_scalar(QUOTA, L, -1.0, -DONE[ROUNDS] * HALF, ALU.mult, ALU.add))
                v.memset(L, 0.0)
                v.scalar_tensor_tensor(key2[:, :], khi[:, :], QUOTA, flat(keys[:, 1, bass.ds(e, 1), :]),
                                       ALU.subtract, ALU.add).then_inc(thr_ready, 1)
                dve.wait_ge(thr_ready, k + 1)

            def next_digit(k, r, half):
                w = (HALF, 1.0)[half] * STEPS[r]
                dve.wait_ge(cnt_sum, k + 1)
                ch.link(v.tensor_scalar(junk16[:, :], bank[CNT][:, 0:REP], ENOUGH, None, ALU.is_ge, ALU.add,
                                        accum_out=DIG))
                if r < ROUNDS - 1:
                    v.scalar_tensor_tensor(MINUS_T, DIG, -w, BASE, ALU.mult, ALU.add).then_inc(thr_ready, 1)
                ch.link(v.scalar_tensor_tensor(L, DIG, -w, L, ALU.mult, ALU.add))
                if r < ROUNDS - 2:
                    col = half * ROUNDS + r + 2
                    ch.link(v.tensor_tensor(BASE, L, thr[:, col:col + 1], ALU.add))

            def choose(e, beside=()):
                units = iter(beside)

                def unit():
                    for b, u in [next(units, (None, None))]:
                        if u is not None:
                            row_max(b, u)
                ch.link(v.tensor_scalar(T, L, -1.0, -DONE[ROUNDS], ALU.mult, ALU.add))
                v.tensor_scalar(ge[:, :], key2[:, :], T, None, ALU.is_ge, ALU.add, accum_out=cnt[:, 1:2])
                v.tensor_scalar(eq[:, :], key2[:, :], T, None, ALU.is_equal, ALU.add,
                                accum_out=cnt[:, 2:3]).then_inc(fin_ready, 1)
                unit()
                dve.wait_ge(fin_ready, e + 1)
                ch.mark(v.tensor_tensor_scan(pre[:, :], ones_h[:, :], eq[:, :], 0.0, ALU.mult, ALU.add))
                unit()
                dve.wait_ge(fin_sum, e + 1)
                ch.link(v.tensor_scalar(QUOTA, bank[CNT][:, 0:1], float(CAP), None, ALU.add))
                v.scalar_tensor_tensor(pre[:, :], pre[:, :], QUOTA, eq[:, :], ALU.is_gt, ALU.mult)
                ch.mark(v.tensor_tensor(avail[:, :], avail[:, :], ge[:, :], ALU.subtract))
                unit()
                ch.need()
                ch.mark(v.tensor_tensor(avail[:, :], avail[:, :], pre[:, :], ALU.add))
                unit()
                ch.need()
                v.tensor_tensor(eid[:, :], eid[:, :], avail[:, :], ALU.add).then_inc(eid_ready, 1)

            def make_keys():
                dve.wait_ge(score_in, 16 * 2)
                bits = key_f[:, :].bitcast(I32)
                flip = key2[:, 0:S].bitcast(I32)
                ch.link(v.tensor_scalar(flip, bits, 31, -2147483648, ALU.arith_shift_right, ALU.bitwise_or))
                ch.link(v.tensor_tensor(flip, flip, bits, ALU.bitwise_xor))
                halves = key2[:, 0:S].bitcast(U16).rearrange("p (f w) -> p w f", w=2)
                v.tensor_copy(key_h[:, 1, :], halves[:, 0, :])
                v.tensor_copy(key_h[:, 0, :], halves[:, 1, :]).then_inc(key_ready, 1)

            def batch(b, before, ahead, ahead2, half=None, e=None, beside=None):
                for h in range(H):
                    if ahead and h:
                        for u in UNITS[h]:
                            row_max(b + 1, u)
                    if half == 0 and h == 0:
                        begin_high(e)
                    if half is not None and h - SUM_AFTER in COUMINUS_TAT[half]:
                        r = COUMINUS_TAT[half].index(h - SUM_AFTER)
                        next_digit((b - 1) * ROUNDS + r, r, half)
                    if beside and h in beside:
                        beside[h]()
                    if before and h == 7:
                        values(b - 1)
                    if ahead and h == 10:
                        split_max(b + 1)
                    if ahead and h == 11:
                        keep_max(b + 1)
                    if before and h == 11:
                        keep_s(b - 1)
                if half == 0:
                    begin_low(e, b * ROUNDS)
                units = [(b + 2, u) for u in range(EARLY)] if ahead2 else []
                if half == 1:
                    choose(e, units)
                else:
                    for unit in units:
                        row_max(*unit)

            for u in range(16):
                row_max(0, u)
            split_max(0)
            keep_max(0)
            for u in range(EARLY):
                row_max(1, u)
            make_keys()
            batch(0, False, True, True)
            dve.wait_ge(keys_in, 16 * NG)
            with dve.Fori(0, PAIRS - 1) as i:
                ch.loop(i, SEARCH_LINKS)
                batch(i * 2 + 1, True, True, True, 0, i)
                batch(i * 2 + 2, True, True, True, 1, i)
            ch.end(PAIRS - 1)
            batch(B - 3, True, True, True, 0, PAIRS - 1)
            batch(B - 2, True, True, False, 1, PAIRS - 1)

            def experts_hot():
                dve.wait_ge(eid_tr, 1)
                ch.link(v.tensor_copy(eidT[:, :].rearrange("p (g c) -> p c g", c=GT),
                                      bank[CNT][:, :].bitcast(F16)[:, 0:GT * P].rearrange(
                                          "p (c g j) -> p c g j", c=GT, j=REP)[:, :, :, 0]))
                for e in range(E0):
                    ins = v.tensor_scalar(hot[:, e, :], eidT[:, :], float(e), None, ALU.is_equal)
                ins.then_inc(hot_ready, 1)

            def places():
                dve.wait_ge(pos_mm, 1)
                ch.link(v.tensor_copy(posa[:, :], bank[1][:, 0:E0 * NT]))
                ch.link(v.tensor_tensor_scan(tot[:, :], ones_h[:, 0:E0 * NT], posa[:, :], 0.0, ALU.mult, ALU.add))
                ch.link(v.tensor_tensor(posa[:, :], tot[:, :], posa[:, :], ALU.subtract))
                ch.link(v.tensor_tensor(posa[:, :], bank[0][:, 0:E0 * NT], posa[:, :], ALU.add))
                ch.link(v.tensor_tensor(posa[:, :], posa[:, :], hot[:, :, :].rearrange("p e t -> p (e t)"), ALU.mult))
                ch.link(v.tensor_reduce(pos_f[:, :], posa[:, :].rearrange("p (e t) -> p t e", e=E0), AX.X, ALU.add))
                ch.link(v.tensor_copy(pos[:, :], pos_f[:, :]))
                v.tensor_scalar(lo_i[:, :], pos[:, :], P - 1, None, ALU.bitwise_and)
                ch.link(v.tensor_scalar(hi_i[:, :], pos[:, :], int(np.log2(P)), None, ALU.arith_shift_right))
                v.tensor_copy(lo_f[:, :], lo_i[:, :])
                ch.link(v.tensor_copy(hi_f[:, :], hi_i[:, :]))
                ch.link(v.tensor_tensor(at_high, iota[:, 0:NT].unsqueeze(1).broadcast_to([P, NT, NT]),
                                        hi_f[:, :].unsqueeze(2).broadcast_to([P, NT, NT]), ALU.is_equal))
                v.tensor_tensor(at_high, at_high, token.unsqueeze(2).broadcast_to([P, NT, NT]), ALU.mult)
                for n in range(NT // LOW_TILES):
                    at = slice(n * LOW_TILES, (n + 1) * LOW_TILES)
                    v.tensor_tensor(at_low[:, at, :], iota.unsqueeze(1).broadcast_to([P, LOW_TILES, P]),
                                    lo_f[:, at].unsqueeze(2).broadcast_to([P, LOW_TILES, P]),
                                    ALU.is_equal).then_inc(low_ready, 1)

            batch(B - 1, True, False, False, beside={6: experts_hot, 8: places})
            dve.wait_ge(idx_mm, 1)
            v.tensor_copy(idx[:, :], bank[7][:, 0:NT]).then_inc(idx_ready, 1)
            values(B - 1)
            keep_s(B - 1)

            dve.sem_inc(y_evac, 2)

            def expert(e, par, round_):
                dve.wait_ge(y_done, e + 1)
                if round_ is not None:
                    dve.wait_ge(spread[par], round_ * ROWS)
                v.tensor_tensor(ho[:, par], bank[3 + par][:, :].rearrange("p (t n) -> p t n", t=GT),
                                b2e[:, par].unsqueeze(1).broadcast_to([P, GT, D]), ALU.add).then_inc(y_evac, 1)

            for par in range(2):
                expert(par, par, None)
            with dve.Fori(1, E0 // 2) as i:
                for par in range(2):
                    expert(i * 2 + par, par, i)

            dve.wait_ge(w8_done, 1)
            v.tensor_tensor(bd_a[:, :], bank[6][:, 0:P], block_mask[:, :], ALU.mult).then_inc(w8_evac, 1)
            v.tensor_tensor(bd_v[:, :], bank[6][:, P:2 * P], block_mask[:, :], ALU.mult).then_inc(w8_evac, 1)
            with dve.Fori(0, NG) as g:
                at = bass.ds(g * GT, GT)
                ch.loop(g, 1)
                dve.wait_ge(sg_ready, g + 1)
                ch.link(v.tensor_tensor(x_all[:, at, :], x_all[:, at, :], s_all[:, at, :], ALU.add))
                for t in range(GT):
                    one = bass.ds(g * GT + t, 1)
                    ins = v.bn_stats(flat(stat6[:, one, :]), flat(x_all[:, one, :]))
            ch.end(NG)
            ch.link(v.memset(small[:, :], 0.0))
            statistics()
            both_scales(var1_ok, root1_ok, 1)

            dve.sem_inc(yg_evac, 2)

            def normalise_x1(g, par):
                dve.wait_ge(tr1_done, g + 1)
                for t in range(GT):
                    one = bass.ds(g * GT + t, 1)
                    ins = v.tensor_scalar(xst[:, par, t, :], flat(x_all[:, one, :]), mean[:, one], rstd[:, one],
                                          ALU.subtract, ALU.mult)
                ins.then_inc(st1_ready, 1)

            def diagonal(g, par, more):
                at = bass.ds(g * GT, GT)
                dve.wait_ge(yg_done, g + 1)
                ch.link(v.tensor_tensor(zst[:, par], bank[Y1[par]][:, :].rearrange("p (t n) -> p t n", t=GT),
                                        xst[:, par], ALU.mult))
                if more:
                    normalise_x1(g + 2, par)
                v.tensor_reduce(ds[:, at, :], zst[:, par].rearrange("p t (h n) -> p t h n", n=HD), AX.X, ALU.add)
                v.tensor_copy(gl[:, at, :], bank[G1[par]][:, 0:GT * E1].rearrange(
                    "p (t e) -> p t e", t=GT)).then_inc(yg_evac, 1)

            for par in range(2):
                normalise_x1(par, par)
            with dve.Fori(0, ROUNDS_A - 1) as i:
                ch.loop(i, 2)
                for par in range(2):
                    diagonal(i * 2 + par, par, True)
            ch.end(ROUNDS_A - 1)
            for par in range(2):
                diagonal(NG - 2 + par, par, False)
            ch.link(v.memset(small[:, :], 0.0))
            dve.wait_ge(x1_evac, NG)
            v.tensor_tensor(vrhs, bd_v[:, :].unsqueeze(1).broadcast_to([P, B, P]),
                            xsum[:, :].unsqueeze(2).broadcast_to([P, B, P]), ALU.mult).then_inc(vrhs_ready, 1)
            dve.wait_ge(x1_copied, NG + 2)

            mine = gl.unsqueeze(3).broadcast_to([P, NT, E1, E1])
            other = gl.unsqueeze(2).broadcast_to([P, NT, E1, E1])
            v.tensor_tensor(pairs, other, mine, ALU.is_gt)
            ch.link(v.tensor_tensor(pairs2, other, mine, ALU.is_equal))
            ch.link(v.tensor_tensor(pairs2, pairs2, low[:, :, :].unsqueeze(1).broadcast_to([P, NT, E1, E1]), ALU.mult))
            ch.link(v.tensor_tensor(pairs, pairs, pairs2, ALU.add))
            rank = key2[:, 0:NT * E1].rearrange("p (t e) -> p t e", t=NT)
            ch.link(v.tensor_reduce(rank, pairs, AX.X, ALU.add))
            ch.link(v.tensor_scalar(rank, rank, 2.0, None, ALU.is_lt))
            ch.link(v.tensor_reduce(small[:, :], gl, AX.X, ALU.max))
            v.tensor_tensor(gl, gl, small[:, :].unsqueeze(2).broadcast_to([P, NT, E1]),
                            ALU.subtract).then_inc(lg_ready, 1)
            by_batch = ds.rearrange("p (c f) h -> p f h c", f=2)
            hm2 = hmax[:, :].rearrange("p (f h) -> p f h", f=2)
            wide = hm2.unsqueeze(1).broadcast_to([P, B, 2, H])
            ds4 = ds.rearrange("p (c f) h -> p c f h", f=2)
            ch.link(v.tensor_reduce(hm2, by_batch, AX.X, ALU.max))
            v.tensor_tensor(ds4, ds4, wide, ALU.subtract).then_inc(lg_ready, 1)
            dve.wait_ge(exp_done, 1)
            ch.link(v.tensor_tensor(gl, gl, rank, ALU.mult))
            ch.link(v.tensor_reduce(small[:, :], gl, AX.X, ALU.add))
            ch.link(v.reciprocal(small[:, :], small[:, :]))
            ch.link(v.tensor_tensor(gl, gl, small[:, :].unsqueeze(2).broadcast_to([P, NT, E1]),
                                    ALU.mult))
            dve.wait_ge(exp_done, 2)
            ch.link(v.tensor_reduce(hm2, by_batch, AX.X, ALU.add))
            ch.link(v.reciprocal(hmax[:, :], hmax[:, :]))
            ch.link(v.tensor_tensor(ds4, ds4, wide, ALU.mult))
            dve.sem_inc(ym_free, 2)

            def give_scores(g, par):
                v.tensor_copy(scm[:, par], gl[:, bass.ds(g * GT, GT), :]).then_inc(sct_in, 1)

            def finish(g, par):
                dve.wait_ge(stored, (g + 1) * 16)
                for c in range(2):
                    pr = ds[:, bass.ds((g * 2 + c) * 2, 2), :].unsqueeze(3).broadcast_to([P, 2, H, HD])
                    vs = vsum[:, bass.ds(g * 2 + c, 1), :].broadcast_to([P, 2, D]).rearrange(
                        "p f (h n) -> p f h n", n=HD)
                    ins = v.tensor_tensor(outs[:, par, 2 * c:2 * c + 2, :].rearrange("p f (h n) -> p f h n", n=HD),
                                          pr, vs, ALU.mult)
                ch.link(ins)
                dve.wait_ge(gate_done, g + 1)
                ch.link(v.tensor_tensor(outs[:, par], outs[:, par], gate[:, par], ALU.mult))
                v.tensor_tensor(outs[:, par], outs[:, par], x_all[:, bass.ds(g * GT, GT), :],
                                ALU.add).then_inc(out_ready, 1)

            def group(g, par, before, more):
                dve.wait_ge(b2_done, g + 1)
                ch.link(v.tensor_copy(acc[:, par].rearrange("p t n -> p (t n)"), bank[7][:, :]))
                if more:
                    give_scores(g + 1, 1 - par)
                for e in range(E1):
                    dve.wait_ge(ym_done, g * E1 + e + 3)
                    for t in range(GT):
                        ins = v.scalar_tensor_tensor(acc[:, par, t, :], bank[4 + e % 2][:, t * P:(t + 1) * P],
                                                     scm[:, par, t, e:e + 1], acc[:, par, t, :], ALU.mult, ALU.add)
                    ins.then_inc(ym_free, 1)
                    dve.wait_ge(ym_free, g * E1 + e + 3)
                    if e == 3 and before:
                        finish(g - 1, 1 - par)
                v.sem_inc(acc_ready, 1)

            give_scores(0, 0)
            dve.wait_ge(vs_evac, B // 4)
            group(0, 0, False, True)
            with dve.Fori(0, ROUNDS_A - 1) as i:
                ch.loop(i, 6)
                for n in range(2):
                    group(i * 2 + n + 1, 1 - n, True, True)
            ch.end(ROUNDS_A - 1)
            group(NG - 1, 1, True, False)
            finish(NG - 1, 1)


_INS = ["x", "pack", "pack_h", "b_v", "b_o", "w1", "b1", "w2", "b2", "w8", "w1m", "w2m", "b2m"]


def kernel(**inputs):
    import concourse.bacc as bacc
    from concourse.bass_utils import run_bass_kernel_spmd

    a = {k: np.asarray(t) for k, t in inputs.items()}
    w = a["L0_attn_w_qkv"].reshape(H, 3, HD, D)
    bias = a["L0_attn_b_qkv"].reshape(H, 3, HD)
    rep = lambda m: np.tile(m, (1, H))
    lay = {
        "x": a["L0_attn_x"].reshape(TOK, D),
        "w_q": w[:, 0].reshape(D, D).T, "w_k": w[:, 1].reshape(D, D).T, "w_v": w[:, 2].reshape(D, D).T,
        "w_o": a["L0_attn_w_o"].T,
        "b_qk": bias[:, 0:2].transpose(0, 2, 1).reshape(D, 2), "b_v": bias[:, 2].reshape(1, D),
        "b_o": a["L0_attn_b_o"].reshape(1, D),
        "cent": a["L0_ffn_centroids"].T, "ln_gb": np.stack([a["L0_ffn_ln_g"], a["L0_ffn_ln_b"]], 1),
        "w1": a["L0_ffn_w1"].transpose(1, 0, 2),
        "b1": a["L0_ffn_b1"].reshape(E0, 4, P).transpose(2, 0, 1),
        "w2": a["L0_ffn_w2"].reshape(E0, 4, P, D).transpose(2, 0, 1, 3).reshape(P, E0, 4 * D),
        "b2": a["L0_ffn_b2"],
        "w8": np.concatenate([rep(a["L1_attn_Wq"]), rep(a["L1_attn_Wk"]), rep(a["L1_attn_Wv"]),
                              rep(np.eye(HD, dtype=np.float32))], 1),
        "w_g": a["L1_ffn_Wg"],
        "w1m": a["L1_ffn_W1"].transpose(1, 0, 2).reshape(D, E1 * H1),
        "b1m": a["L1_ffn_b1"].reshape(E1, 2, P).transpose(2, 0, 1).reshape(P, 2 * E1),
        "w2m": a["L1_ffn_W2"].reshape(E1, 2, P, D).transpose(2, 0, 1, 3).reshape(P, E1 * 2 * D),
        "b2m": a["L1_ffn_b2"],
        **host_constants(),
    }
    lay["pack"] = np.concatenate([lay[n] for n in PACK], 1)
    lay["pack_h"] = np.concatenate([lay[n] for n in PACK_H], 1)
    nc = bacc.Bacc("TRN2", target_bir_lowering=False, num_devices=1)
    arrays, aps = {}, {}
    for name in _INS:
        t = np.ascontiguousarray(lay[name])
        arrays[f"in_{name}"] = t
        aps[name] = nc.dram_tensor(f"in_{name}", t.shape, mybir.dt.from_np(t.dtype), kind="ExternalInput").ap()
    out = nc.dram_tensor("out_0", (TOK, D), F32, kind="ExternalOutput").ap()
    two_layers(nc, aps, out)
    got = run_bass_kernel_spmd(nc, [arrays], core_ids=[0])
    return got.results[0]["out_0"].reshape(B, S, D)
```

```python
from contextlib import ExitStack

import numpy as np

import concourse.bass as bass
from concourse import mybir

F32, BF16, F16 = mybir.dt.float32, mybir.dt.bfloat16, mybir.dt.float16
I32, U16 = mybir.dt.int32, mybir.dt.uint16
ALU, ACT, AX = mybir.AluOpType, mybir.ActivationFunctionType, mybir.AxisListType

P = 128
B, S, D = 16, 256, 128
H, HD = 16, 8
TOK = B * S
NT = TOK // P
GT = 4
GN = GT * P
NG = NT // GT
E0, F0 = 8, 512
CAP = TOK // E0
E1, H1 = 8, 256
EPS = 1e-5
REP = 16
ROUNDS = 4
HALF = 65536.0
STEPS = [float(REP ** (ROUNDS - 1 - r)) for r in range(ROUNDS)]
DONE = [sum(STEPS[:r]) for r in range(ROUNDS + 1)]
PIECES = (slice(0, 10), slice(10, H))
COUNT_AT = ((2, 5, 8, 11), (1, 4, 7, 10))
SUM_AFTER = 2
RUNS = ((0, 3), (3, 2), (5, 1))
KROWS = 96
MROW = 96
PACK = {"c_ident": P, "c_sums": 4 * (HD + 1), "c_block": P, "c_iota": P, "c_token": 1,
        "c_thr": 2 * ROUNDS, "c_first": E1, "w_q": P, "w_k": P, "w_v": P, "w_o": P,
        "cent": E0, "b_qk": 2, "ln_gb": 2, "w_g": E1, "b1m": 2 * E1}
PACK_H = {"c_pick": REP, "c_nge": P, "c_neq": P, "c_tri": P}
STACK = 2


def host_constants():
    p = np.arange(P)
    j = (p % REP).astype(np.float64)
    cols = [(0.5 - j * STEPS[r] + DONE[r]) * unit for unit in (HALF, 1.0) for r in range(ROUNDS)]
    first = (p % REP == 0)[:, None]
    earlier = first & (p[:, None] // REP < p[None, :] // REP)
    sums = np.zeros((P, 4 * (HD + 1)))
    for n in range(4):
        sums[32 * n:32 * n + HD + 1, n * (HD + 1):(n + 1) * (HD + 1)] = np.eye(HD + 1)
    return {
        "c_ident": np.eye(P, dtype=np.float32),
        "c_iota": np.arange(P, dtype=np.float32)[None].repeat(P, 0),
        "c_token": p[:, None].astype(np.float32),
        "c_sums": sums.astype(np.float32),
        "c_block": (p[:, None] // HD == p[None, :] // HD).astype(np.float32),
        "c_thr": np.stack(cols, 1).astype(np.float32),
        "c_pick": (p[:, None] % REP == np.arange(REP)[None]).astype(np.float16),
        "c_nge": (-1.0 * first * np.ones((1, P))).astype(np.float16),
        "c_neq": (1.0 * first - 1.0 * earlier).astype(np.float16),
        "c_tri": (p[:, None] < p[None, :]).astype(np.float16),
        "c_first": (E1 - np.arange(E1, dtype=np.float32))[None].repeat(P, 0),
    }


class Chain:

    def __init__(self, engine, sem):
        self.engine, self.sem, self.base, self.n = engine, sem, 0, 0

    def link(self, ins):
        ins.then_inc(self.sem, 1)
        self.n += 1
        self.engine.wait_ge(self.sem, self.base + self.n)

    def mark(self, ins):
        ins.then_inc(self.sem, 1)
        self.n += 1

    def need(self):
        self.engine.wait_ge(self.sem, self.base + self.n)

    def loop(self, i, per):
        self.start, self.per, self.base = self.n, per, i * per

    def end(self, rounds):
        assert self.n - self.start == self.per, f"{self.n - self.start} links in a round"
        self.base, self.n = 0, self.start + self.per * rounds


def flat(ap):
    return ap.rearrange("p a n -> p (a n)")


def two_layers(nc, a, out):
    with ExitStack() as ctx:
        def sb(name, shape, dt=F32):
            return ctx.enter_context(nc.sbuf_tensor(name, shape, dt))

        def sem(name):
            return ctx.enter_context(nc.semaphore(name))

        bank = [ctx.enter_context(nc.psum_tensor(f"bank{i}", [P, 512], F32)) for i in range(8)]

        pack, pack_h = sb("pack", [P, sum(PACK.values())]), sb("pack_h", [P, sum(PACK_H.values())], F16)

        def packed(tile, widths, name):
            start = sum(list(widths.values())[:list(widths).index(name)])
            return tile[:, start:start + widths[name]]
        ident, pick_sums, block_mask, iota, token, thr, first_f, w_q, w_k, w_v, w_o, cent, b_qk, ln_gb, w_g, b1m_f = (
            packed(pack, PACK, n) for n in PACK)
        pick, nge, neq, tri = (packed(pack_h, PACK_H, n) for n in PACK_H)
        b1m = b1m_f.rearrange("p (e t) -> p e t", e=E1)
        ident_b, ident_h = sb("ident_b", [P, P], BF16), sb("ident_h", [P, P], F16)
        ones_h, ones_f = sb("ones_h", [P, GN], F16), sb("ones_f", [P, P])
        b_v, b_o = sb("b_v", [P, P]), sb("b_o", [P, P])
        x_all = sb("x_all", [P, NT, D])
        xn_all = sb("xn_all", [P, NT, D])
        s_all = sb("s_all", [P, NT, D])
        v_all = sb("v_all", [P, NT, D])
        arena = sb("arena", [P, 12288])
        STACKS_END = STACK * 2 * H * S // 2
        stacks = arena[:, 0:STACKS_END].bitcast(BF16).rearrange("p (s w h t) -> p s w h t", s=STACK, w=2, h=H)
        keys = sb("keys", [P, 2, E0 - 1, GN], U16)
        stat6, mean, var = sb("stat6", [P, NT, 6]), sb("mean", [P, NT]), sb("var", [P, NT])
        spare = sb("spare", [P, NT])
        squares, roots_all, scales = (sb(n, [P, 2 * NT]) for n in ("squares", "roots_all", "scales"))
        roots, rstd, zscale = roots_all[:, :], scales[:, 0:NT], scales[:, NT:2 * NT]
        xst, zst = sb("xst", [P, 2, GT, D]), sb("zst", [P, 2, GT, D])
        parts_sb = sb("parts_sb", [P, 2 * 3 * 2 * 512], BF16)
        pool_tile = sb("pool_tile", [P, 8, 512])
        xT, zT = pool_tile[:, 0:2, :], pool_tile[:, 2:4, :]
        qkf = pool_tile[:, 4:8, :].rearrange("p (a w) n -> p a w n", a=2)
        probs = pool_tile
        parts = parts_sb[:, :].rearrange("p (a i w n) -> p a i w n", a=2, i=3, w=2)
        sT = s_all[0:E0, :, :].rearrange("p t d -> p (t d)")
        v_b = sb("v_b", [P, 2, 2, H, 32])
        o_b = sb("o_b", [P, 2, 4, S])
        vals, vT = sb("vals", [P, 2, P]), sb("vT", [P, 2, P])
        rec = sb("rec", [P, 2, H])
        mx = sb("mx", [P, H, 2])
        nm = sb("nm", [P, P], BF16)
        nmT = sb("nmT", [P, P], BF16)
        khi, key2 = sb("khi", [P, GN]), sb("key2", [P, GN])
        junk, ge, eq, pre = (sb(n, [P, GN], F16) for n in ("junk", "ge", "eq", "pre"))
        avail, eid = sb("avail", [P, GN], F16), sb("eid", [P, GN], F16)
        cnt = sb("cnt", [P, 3], F16)
        junk16 = sb("junk16", [P, REP])
        st = sb("st", [P, 6])
        T, L, BASE, DIG, QUOTA, MINUS_T = (st[:, i:i + 1] for i in range(6))
        eidT = sb("eidT", [P, NT])
        hot = sb("hot", [P, E0, NT], F16)
        key_f, key_h = khi[:, 0:S], khi[:, S:2 * S].bitcast(U16).rearrange("p (w f) -> p w f", w=2)
        tot, posa = khi[:, 0:E0 * NT], khi[:, E0 * NT:2 * E0 * NT]
        pos_f, pos = sb("pos_f", [P, NT]), sb("pos", [P, NT], I32)
        idx = sb("idx", [P, NT], I32)
        lo_i, hi_i = sb("lo_i", [P, NT], I32), sb("hi_i", [P, NT], I32)
        lo_f, hi_f = sb("lo_f", [P, NT]), sb("hi_f", [P, NT])
        at_low = arena[:, STACKS_END:STACKS_END + NT * P // 2].bitcast(F16).rearrange("p (t q) -> p t q", t=NT)
        at_high = keys[:, :, :, :].rearrange("p w e n -> p (w e n)").bitcast(F16)[:, 0:3 * NT * NT].rearrange(
            "p (k t c) -> p t k c", t=NT, k=3)

        def dram(name, shape, dt=F32):
            return nc.dram_tensor(name, shape, dt).ap()
        d_parts = dram("d_parts", [2, 3 * HD, H, TOK], BF16)
        d_score = dram("d_score", [E0, TOK])
        d_keys = dram("d_keys", [NG, 2, E0, GN], U16)
        d_z, d_ffn = dram("d_z", [TOK, D]), dram("d_ffn", [TOK, D])

        def carve(start, *shape):
            n = int(np.prod(shape))
            names = "abcd"[:len(shape)]
            dims = {c: k for c, k in zip(names, shape)}
            return arena[:, start:start + n].rearrange(f"p ({' '.join(names)}) -> p {' '.join(names)}", **dims)
        w1e, w2e = carve(0, 2, F0), carve(1024, 2, 4, D)
        zl, nT = carve(2048, 2, GT, D), carve(3072, 2, GN)
        hT, ho = carve(4096, 2, 4, GN), carve(8192, 2, GT, D)
        b1e, b2e = carve(9216, 2, 4), carve(9224, 2, D)
        xT_all, w1m, w2m = carve(0, NG, GN), carve(4096, E1, H1), carve(6144, E1, 2, D)
        hm, vsum = carve(8192, 2, 2, GN), carve(10240, B, D)
        routed = v_all
        wqkv8 = sb("wqkv8", [8, 4, D])
        bd_ag, bd_v = sb("bd_ag", [P, P + E1]), sb("bd_v", [P, P])
        b2m = sb("b2m", [E1, D])
        xsum = sb("xsum", [P, B])
        vrhs = carve(8192, B, D)
        late = o_b[:, :, :, :].rearrange("p a b n -> p (a b n)")
        ds = late[:, 0:NT * H].rearrange("p (t h) -> p t h", t=NT)
        gl = late[:, 512:512 + NT * E1].rearrange("p (t e) -> p t e", t=NT)
        scm = late[:, 768:768 + 2 * GT * E1].rearrange("p (a t e) -> p a t e", a=2, t=GT)
        scT = late[0:E1, 1024:1024 + 2 * GN].rearrange("p (a n) -> p a n", a=2)
        small, small2, small3 = (sb(n, [P, NT]) for n in ("small", "small2", "small3"))
        hmax = sb("hmax", [P, 2 * H])
        x1T = pool_tile[:, 0:2, :]
        acc, gate = xst, zst
        outs = pool_tile[:, 4:8, :].rearrange("p a (t d) -> p a t d", t=GT)

        x_in = [sem(f"x_in{g}") for g in range(NG)]
        w_in, chain_s, pool_s = sem("w_in"), sem("dve_chain"), sem("pool_chain")
        idents, zeroed, var_ok, root_ok = sem("idents"), sem("zeroed"), sem("var_ok"), sem("root_ok")
        st_ready, xn_copied, tr_done, t_evac = sem("st_ready"), sem("xn_copied"), sem("tr_done"), sem("t_evac")
        v_done, q_done, k_done, q_evac = sem("v_done"), sem("q_done"), sem("k_done"), sem("q_evac")
        sc_done, qk_evac, v_evac, sc_evac = sem("sc_done"), sem("qk_evac"), sem("v_evac"), sem("sc_evac")
        rest1, part2, split_done = sem("rest1"), sem("part2"), sem("split_done")
        parts_out = [sem("parts_out0"), sem("parts_out1")]
        score_out, score_in = sem("score_out"), sem("score_in")
        key_ready, key_out, keys_in = sem("key_ready"), sem("key_out"), sem("keys_in")
        stack_in, mx_ready, mx_free = sem("stack_in"), sem("mx_ready"), sem("mx_free")
        nm_ready, nm_tr, nm_evac, nm_in = sem("nm_ready"), sem("nm_tr"), sem("nm_evac"), sem("nm_in")
        v_ready, lt_ready, lt_free = sem("v_ready"), sem("lt_ready"), sem("lt_free")
        pv_done, pv_free = sem("pv_done"), sem("pv_free")
        cnt_ready, cnt_sum, fin_ready, fin_sum = sem("cnt_ready"), sem("cnt_sum"), sem("fin_ready"), sem("fin_sum")
        ot_done, vals_ready, vt_done, vt_evac = sem("ot_done"), sem("vals_ready"), sem("vt_done"), sem("vt_evac")
        s_done, s_evac = sem("s_done"), sem("s_evac")
        thr_ready, bias_done = sem("thr_ready"), sem("bias_done")
        eid_ready, eid_tr, hot_ready, pos_mm = sem("eid_ready"), sem("eid_tr"), sem("hot_ready"), sem("pos_mm")
        z_out, zl_in, spread = ([sem(f"{n}{par}") for par in range(2)] for n in ("z_out", "zl_in", "spread"))
        low_ready, idx_mm, idx_ready = sem("low_ready"), sem("idx_mm"), sem("idx_ready")
        back_in = [sem(f"back_in{g}") for g in range(NG)]
        e_in = [sem("e_in0"), sem("e_in1")]
        zt_done, nt_ready, h_done, h_evac = sem("zt_done"), sem("nt_ready"), sem("h_done"), sem("h_evac")
        y_done, y_evac = sem("y_done"), sem("y_evac")
        gin_ready, silu_done, sg_ready = sem("gin_ready"), sem("silu_done"), sem("sg_ready")
        m_in, var1_ok, root1_ok, w8_done, w8_evac = (
            sem("m_in"), sem("var1_ok"), sem("root1_ok"), sem("w8_done"), sem("w8_evac"))
        st1_ready, tr1_done, x1_evac, x1_copied = sem("st1_ready"), sem("tr1_done"), sem("x1_evac"), sem("x1_copied")
        yg_done, yg_evac = sem("yg_done"), sem("yg_evac")
        lg_ready, exp_done, vrhs_ready, vs_mm, vs_evac = (
            sem("lg_ready"), sem("exp_done"), sem("vrhs_ready"), sem("vs_mm"), sem("vs_evac"))
        sct_in, sct_done, sct_evac, b2_done = sem("sct_in"), sem("sct_done"), sem("sct_evac"), sem("b2_done")
        hm_done, hm_evac, ym_done, ym_free = sem("hm_done"), sem("hm_evac"), sem("ym_done"), sem("ym_free")
        acc_ready, gate_done, out_ready, stored = sem("acc_ready"), sem("gate_done"), sem("out_ready"), sem("stored")

        x_t = a["x"].rearrange("(n p) d -> p n d", p=P)
        out_t = out.rearrange("(n p) d -> p n d", p=P)
        z_t = d_z.rearrange("(n p) d -> p n d", p=P)
        ffn_t = d_ffn.rearrange("(n p) d -> p n d", p=P)
        first_loads = [
            (pack[:, :], a["pack"]), (b_v[:, :], a["b_v"].broadcast_to([P, P])), (pack_h[:, :], a["pack_h"]),
            (b_o[:, :], a["b_o"].broadcast_to([P, P])), (b2m[:, :], a["b2m"]),
            (wqkv8[:, :, :].rearrange("p a n -> p (a n)"), a["w8"]),
        ]
        W_ALL = 16 * len(first_loads)
        PIECE_LOAD = 16 * 2 * len(RUNS)
        LOW_TILES = 8
        PARTS_STORE = 16 * 3 * 2
        QW = 4 * (HD + 1)
        ROUNDS_A = NG // 2
        PAIRS = (B - 2) // 2
        T1, Y1, G1 = (0, 5), (1, 3), (2, 4)
        TX, TZ = 0, 1
        LT, MX, PV, CNT, TR = (2, 3), (0, 1, 7), 4, 5, 6
        MX_OF = [MX[u % 3] for u in range(15)] + [MX[1]]
        MX_FIRST = (7, 6)
        WITH_A = 2
        MX_LAG = [min(k for k in range(1, 17) if MX_OF[u - k] == MX_OF[u]) for u in range(16)]
        UNITS = [range(2 + -(-h * 14 // 12), min(16, 2 + -(-(h + 1) * 14 // 12))) if h < 12 else () for h in range(H)]
        E_LOADS = 16 * 4
        ROWS = 16 * GT
        EARLY = UNITS[0].stop
        SEARCH_LINKS = 30
        KEY_STORES = 2 * 2
        TURN_AT = {1: (0, 1), 5: (2,), 6: (3,)}
        KEEP_AT = 12
        ENOUGH = float(2 * CAP - TOK)

        def hold(engine, semaphore, value):
            if not isinstance(value, int):
                value = engine.to_reg(value)
                engine.wait_ge(w_in, W_ALL)
            engine.wait_ge(semaphore, value)

        block = ctx.enter_context(nc.Block())

        @block.sync
        def _(sp):
            for g in range(NG):
                sp.dma_start(x_all[:, g * GT:(g + 1) * GT, :], x_t[:, g * GT:(g + 1) * GT, :]).then_inc(x_in[g], 16)
            def store_parts(g, par):
                hold(sp, split_done, g + 3)
                for part in range(3):
                    for w in range(2):
                        first = (part, 2 - part)[w] * HD
                        sp.dma_start(d_parts[w, first:first + HD, :, bass.ds(g * GN, GN)].rearrange("d h t -> h d t"),
                                     parts[:, par, part, w, :]).then_inc(parts_out[par], 16)

            def load_piece(b, slot, piece):
                hs = PIECES[piece]
                for w in range(2):
                    for start, n in RUNS:
                        first = (0, 3 - n)[w] * HD
                        sp.dma_start(stacks[start * HD:(start + n) * HD, slot, w, hs, :],
                                     d_parts[w, first:first + n * HD, hs, bass.ds(b * S, S)]).then_inc(stack_in, 16)

            def put_max(b, slot):
                hold(sp, nm_evac, b + 1)
                for part in range(2):
                    sp.dma_start(stacks[MROW + part:MROW + part + 1, slot, 0, :, :].rearrange(
                        "p h (c q) -> p (h c) q", c=2), nmT[32 * part:32 * part + 32, :]).then_inc(nm_in, 16)

            for g in range(2):
                store_parts(g, g)
            sp.wait_ge(zeroed, 1)
            sp.wait_ge(parts_out[0], PARTS_STORE)
            for n in range(4):
                store_parts(2 + n, n % 2)
                if n:
                    sp.wait_ge(stack_in, PIECE_LOAD * n)
                load_piece(n // 2, n // 2, n % 2)
            for g in range(6, NG):
                store_parts(g, g % 2)
            put_max(0, 0)
            for par in range(2):
                sp.wait_ge(parts_out[par], PARTS_STORE * ROUNDS_A)

            def refill(b, slot):
                for piece in range(2):
                    hold(sp, lt_ready, H * b + PIECES[piece].stop)
                    hold(sp, stack_in, PIECE_LOAD * (2 * (b + 2) + piece))
                    load_piece(b + 2, slot, piece)
                    if piece == 0:
                        hold(sp, nm_in, 32 * (b + 1))
                        put_max(b + 1, 1 - slot)

            with sp.Fori(0, B // 2 - 1) as i:
                for slot in range(2):
                    refill(i * 2 + slot, slot)
            sp.wait_ge(nm_in, 32 * (B - 1))
            put_max(B - 1, (B - 1) % 2)

            def load_expert(e, par):
                sp.dma_start(w1e[:, par], flat(a["w1"][:, bass.ds(e, 1), :])).then_inc(e_in[par], 16)
                sp.dma_start(w2e[:, par].rearrange("p t n -> p (t n)"),
                             flat(a["w2"][:, bass.ds(e, 1), :])).then_inc(e_in[par], 16)
                sp.dma_start(b1e[:, par], flat(a["b1"][:, bass.ds(e, 1), :])).then_inc(e_in[par], 16)
                sp.dma_start(b2e[:, par], a["b2"][bass.ds(e, 1), :].broadcast_to([P, D])).then_inc(e_in[par], 16)

            sp.wait_ge(lt_ready, H * B)
            sp.wait_ge(idx_mm, 1)
            load_expert(0, 0)
            load_expert(1, 1)
            with sp.Fori(0, E0 // 2 - 1) as i:
                for par in range(2):
                    hold(sp, y_evac, i * 2 + par + 3)
                    load_expert(i * 2 + par + 2, par)
            for par in range(2):
                sp.wait_ge(spread[par], ROWS * E0 // 2)
            for g in range(NG):
                at = slice(g * GT, (g + 1) * GT)
                sp.dma_start(routed[:, at, :], ffn_t[:, at, :]).then_inc(back_in[g], 16)

            sp.wait_ge(y_evac, E0 + 2)
            sp.dma_start(w1m.rearrange("p e n -> p (e n)"), a["w1m"]).then_inc(m_in, 16)
            sp.dma_start(w2m.rearrange("p e t n -> p (e t n)"), a["w2m"]).then_inc(m_in, 16)
            sp.sem_inc(stored, 32)
            with sp.Fori(0, ROUNDS_A) as i:
                for par in range(2):
                    g = i * 2 + par
                    hold(sp, out_ready, g + 1)
                    hold(sp, stored, (g + 2) * 16)
                    sp.dma_start(out_t[:, bass.ds(g * GT, GT), :], outs[:, par]).then_inc(stored, 16)
            sp.wait_ge(stored, 16 * (NG + 2))

        @block.gpsimd
        def _(gp):
            pc = Chain(gp, pool_s)
            gp.sem_inc(xn_copied, 2)
            pc.link(gp.memset(arena[:, 0:STACKS_END], 0.0))
            gp.memset(stacks[MROW:MROW + 2, :, 1, :, :], 1.0).then_inc(zeroed, 1)
            gp.wait_ge(zeroed, 1)
            pc.link(gp.memset(v_b[:, :, :, :, :], 0.0))
            pc.link(gp.memset(v_b[:, :, :, :, HD:HD + 1], 1.0))
            with gp.Fori(0, ROUNDS_A) as i:
                for par in range(2):
                    g = i * 2 + par
                    hold(gp, st_ready, g + 1)
                    gp.dma_start(z_t[:, bass.ds(g * GT, GT), :], zst[:, par]).then_inc(z_out[par], 16)
                    gp.tensor_copy(xn_all[:, bass.ds(g * GT, GT), :], xst[:, par]).then_inc(xn_copied, 1)

            def copy_v(b, par):
                hold(gp, pv_done, b * 4 + 4)
                gp.tensor_copy(v_b[:, par, :, :, 0:HD], v_all[:, bass.ds(b * 2, 2), :].rearrange(
                    "p k (h d) -> p k h d", h=H)).then_inc(v_ready, 1)

            def add_bias(b):
                hold(gp, s_evac, b + 2)
                two = s_all[:, bass.ds(b * 2, 2), :]
                gp.tensor_tensor(two, two, b_o[:, :].unsqueeze(1).broadcast_to([P, 2, P]),
                                 ALU.add).then_inc(bias_done, 1)

            gp.wait_ge(v_evac, NG + 1)
            for par in range(2):
                copy_v(par, par)
            gp.wait_ge(sc_evac, NG + 1)
            gp.dma_start(d_score, sT).then_inc(score_out, 16)
            gp.wait_ge(score_out, 16)
            for c in range(2):
                gp.dma_start(key_f[c * P // 2:(c + 1) * P // 2, :], d_score.rearrange(
                    "e (g c f) -> c g e f", c=2, f=S)[c]).then_inc(score_in, 16)
            gp.wait_ge(key_ready, 1)
            for w in range(2):
                for c in range(2):
                    gp.dma_start(d_keys[:, w, :, c * S:(c + 1) * S],
                                 key_h[c * P // 2:(c + 1) * P // 2, w, :]).then_inc(key_out, 16)
            gp.wait_ge(key_out, 16 * KEY_STORES)
            for g in range(NG):
                gp.dma_start(keys[g * REP:(g + 1) * REP, :, :, :], d_keys[g:g + 1, :, 0:E0 - 1, :].rearrange(
                    "a w e n -> a w (e n)").broadcast_to([REP, 2, (E0 - 1) * GN])).then_inc(keys_in, 16)
            with gp.Fori(1, B // 2) as i:
                for par in range(2):
                    copy_v(i * 2 + par, par)
                    add_bias(i * 2 + par - 2)
            add_bias(B - 2)

            def gather(e):
                if e >= 2:
                    gp.wait_ge(zt_done, e - 1)
                for t in range(GT):
                    gp.indirect_dma_start(zl[:, e % 2, t, :], None, d_z, bass.IndirectOffsetOnAxis(
                        ap=idx[:, e * GT + t:e * GT + t + 1], axis=0)).then_inc(zl_in[e % 2], 16)

            for par in range(2):
                gp.wait_ge(z_out[par], 16 * ROUNDS_A)
            gp.wait_ge(idx_ready, 1)
            gp.wait_ge(lt_ready, H * B)
            gather(0)
            gather(1)
            add_bias(B - 1)
            for e in range(E0):
                if e + 2 < E0:
                    gather(e + 2)
                gp.wait_ge(y_evac, e + 3)
                for t in range(GT):
                    gp.indirect_dma_start(d_ffn, bass.IndirectOffsetOnAxis(
                        ap=idx[:, e * GT + t:e * GT + t + 1], axis=0), ho[:, e % 2, t, :], None).then_inc(
                            spread[e % 2], 16)
            for g in range(NG):
                at = slice(g * GT, (g + 1) * GT)
                gp.wait_ge(back_in[g], 16)
                gp.tensor_tensor(routed[:, at, :], routed[:, at, :], xn_all[:, at, :], ALU.add).then_inc(gin_ready, 1)
                if g % 2 == 1:
                    at = slice((g - 1) * GT, g * GT)
                    gp.wait_ge(silu_done, g)
                    gp.tensor_tensor(s_all[:, at, :], s_all[:, at, :], routed[:, at, :], ALU.mult).then_inc(sg_ready, 1)
            gp.sem_inc(x1_copied, 2)
            with gp.Fori(0, ROUNDS_A) as i:
                for par in range(2):
                    g = i * 2 + par
                    hold(gp, x1_evac, g + 1)
                    gp.tensor_copy(flat(xT_all[:, bass.ds(g, 1), :]), x1T[:, par]).then_inc(x1_copied, 1)
            gp.wait_ge(w8_evac, 2)
            gp.wait_ge(x1_evac, NG)
            gp.tensor_tensor(vrhs, bd_v[:, :].unsqueeze(1).broadcast_to([P, B, P]),
                             xsum[:, :].unsqueeze(2).broadcast_to([P, B, P]), ALU.mult).then_inc(vrhs_ready, 1)

        @block.scalar
        def _(act):
            for dst, src in first_loads:
                nc.scalar.dma_start(dst, src).then_inc(w_in, 16)
            act.wait_ge(var_ok, 1)
            nc.scalar.activation(roots, roots, ACT.Sqrt).then_inc(root_ok, 1)
            act.wait_ge(w_in, W_ALL)
            for evac in (q_evac, qk_evac, sc_evac):
                act.sem_inc(evac, 1)

            def turned(g, par):
                act.wait_ge(tr_done, g + 1)
                nc.scalar.activation(xT[:, par], bank[TX][:, :], ACT.Copy)
                nc.scalar.activation(zT[:, par], bank[TZ][:, :], ACT.Identity, bias=ln_gb[:, 1:2],
                                     scale=ln_gb[:, 0:1]).then_inc(t_evac, 1)

            def projected(g, par, more, stored_before):
                act.wait_ge(split_done, g + 1)
                if stored_before is not None:
                    act.wait_ge(parts_out[par], stored_before)
                for w, done, evac in ((0, q_done, q_evac), (1, k_done, qk_evac)):
                    act.wait_ge(done, g + 1)
                    nc.scalar.activation(qkf[:, par, w], bank[2 + w][:, :], ACT.Identity, bias=b_qk[:, w:w + 1])
                    nc.scalar.activation(parts[:, par, 0, w], bank[2 + w][:, :], ACT.Identity,
                                         bias=b_qk[:, w:w + 1]).then_inc(evac, 1)
                act.wait_ge(sc_done, g + 1)
                nc.scalar.activation(sT[:, bass.ds(g * GN, GN)], bank[5][0:E0, :], ACT.Copy).then_inc(sc_evac, 1)
                if more:
                    turned(g + 2, par)
                act.wait_ge(rest1, g + 1)
                nc.scalar.activation(parts[:, par, 1], qkf[:, par], ACT.Copy).then_inc(part2, 1)

            for par in range(2):
                turned(par, par)
            for par in range(2):
                projected(par, par, True, None)
            with act.Fori(1, ROUNDS_A - 1) as i:
                for par in range(2):
                    projected(i * 2 + par, par, True, i * PARTS_STORE)
            for par in range(2):
                projected(NG - 2 + par, par, False, (ROUNDS_A - 1) * PARTS_STORE)

            act.sem_inc(lt_free, 2)
            act.sem_inc(pv_free, 1)
            act.sem_inc(s_evac, 1)

            def keep_o(m, par, quad):
                act.wait_ge(pv_done, m + 9)
                if quad == 0:
                    act.wait_ge(ot_done, m // 4 + 1)
                nc.scalar.activation(o_b[:, par, quad, :], bank[PV][:, 0:S], ACT.Copy).then_inc(pv_free, 1)

            def turn_vals(b):
                act.wait_ge(vt_done, b + 1)
                nc.scalar.activation(vT[:, :, :].rearrange("p a n -> p (a n)"), bank[TR][:, 0:2 * P],
                                     ACT.Copy).then_inc(vt_evac, 1)

            def count(k, half):
                act.wait_ge(thr_ready, k + 1)
                with nc.allow_low_precision(reason="whole numbers up to 512 are exact"):
                    nc.scalar.activation(junk[:, :], (khi, key2)[half][:, :], ACT.Sign, bias=MINUS_T,
                                         accum_out=cnt[:, 0:1]).then_inc(cnt_ready, 1)

            def keep_max(b):
                act.wait_ge(nm_tr, b + 1)
                if not (isinstance(b, int) and b == 0):
                    act.wait_ge(nm_in, b * 32)
                nc.scalar.activation(nmT[:, :], bank[TR][:, :].bitcast(BF16)[:, 6 * P:7 * P],
                                     ACT.Copy).then_inc(nm_evac, 1)

            def keep_s(b):
                act.wait_ge(s_done, b + 1)
                nc.scalar.activation(s_all[:, bass.ds(b * 2, 2), :], bank[TR][:, 0:2 * P].rearrange(
                    "p (q n) -> p q n", q=2), ACT.Copy).then_inc(s_evac, 1)

            def batch(b, par, before, ahead, half=None):
                for h in range(H):
                    if h % 4 == 0:
                        act.wait_ge(pv_done, b * 4 + h // 4 + 7)
                    act.wait_ge(lt_ready, b * H + h + 1)
                    nc.scalar.activation(probs[:, h % 8, :], bank[LT[h % 2]][:, :], ACT.Exp,
                                         scale=float(HD) ** -0.5).then_inc(lt_free, 1)
                    if h % 4 == 0 and h >= 8:
                        keep_o(b * 4 + h // 4 - 2, par, h // 4 - 2)
                    elif h % 4 == 0 and before:
                        keep_o(b * 4 + h // 4 - 2, 1 - par, h // 4 + 2)
                    if half is not None and h in COUNT_AT[half]:
                        count((b - 1) * ROUNDS + COUNT_AT[half].index(h), half)
                    if before and h == 10:
                        turn_vals(b - 1)
                    if ahead and h == KEEP_AT:
                        keep_max(b + 1)
                    if before and h == KEEP_AT:
                        keep_s(b - 1)

            keep_max(0)
            batch(0, 0, False, True)
            with act.Fori(0, PAIRS) as i:
                batch(i * 2 + 1, 1, True, True, 0)
                batch(i * 2 + 2, 0, True, True, 1)
            batch(B - 1, 1, True, False)
            keep_o(4 * B - 2, 1, 2)
            keep_o(4 * B - 1, 1, 3)
            turn_vals(B - 1)
            keep_s(B - 1)

            act.sem_inc(h_evac, 2)

            def turn_z(e, par):
                act.wait_ge(zt_done, e + 1)
                nc.scalar.activation(nT[:, par], bank[0][:, :], ACT.Identity, bias=ln_gb[:, 1:2],
                                     scale=ln_gb[:, 0:1]).then_inc(nt_ready, 1)

            def expert(e, par, more):
                for ft in range(4):
                    act.wait_ge(h_done, e * 4 + ft + 1)
                    nc.scalar.activation(hT[:, par, ft, :], bank[1 + ft % 2][:, :], ACT.Gelu_apprx_tanh,
                                         bias=b1e[:, par, ft:ft + 1]).then_inc(h_evac, 1)
                if more:
                    turn_z(e + 1, 1 - par)

            turn_z(0, 0)
            with act.Fori(0, E0 // 2 - 1) as i:
                for par in range(2):
                    expert(i * 2 + par, par, True)
            expert(E0 - 2, 0, True)
            expert(E0 - 1, 1, False)

            for g in range(NG):
                act.wait_ge(gin_ready, g + 1)
                v = routed[:, g * GT:(g + 1) * GT, :]
                nc.scalar.activation(v, v, ACT.Silu).then_inc(silu_done, 1)

            act.wait_ge(var1_ok, 1)
            nc.scalar.activation(roots[:, 0:NT], roots[:, 0:NT], ACT.Sqrt).then_inc(root1_ok, 1)
            with act.Fori(0, ROUNDS_A) as i:
                for par in range(2):
                    g = i * 2 + par
                    act.wait_ge(tr1_done, g + 3)
                    act.wait_ge(x1_copied, g + 1)
                    for c in range(2):
                        ins = nc.scalar.activation(x1T[:, par, c * S:(c + 1) * S], bank[T1[par]][:, c * S:(c + 1) * S],
                                                   ACT.Copy, accum_out=xsum[:, bass.ds(g * 2 + c, 1)])
                    ins.then_inc(x1_evac, 1)
            act.wait_ge(lg_ready, 1)
            nc.scalar.activation(gl, gl, ACT.Exp).then_inc(exp_done, 1)
            for r in range(B // 4):
                act.wait_ge(vs_mm, r + 1)
                nc.scalar.activation(vsum[:, r * 4:(r + 1) * 4, :].rearrange("p c n -> p (c n)"),
                                     bank[1 + r][:, :], ACT.Copy).then_inc(vs_evac, 1)
            act.wait_ge(lg_ready, 2)
            nc.scalar.activation(ds, ds, ACT.Exp, scale=float(D) ** -0.5).then_inc(exp_done, 1)
            act.sem_inc(hm_evac, 2)

            def keep_scores(g, par):
                act.wait_ge(sct_done, g + 1)
                nc.scalar.activation(scT[:, par, :], bank[6][0:E1, :], ACT.Copy).then_inc(sct_evac, 1)

            def hidden_relu(g, e):
                act.wait_ge(hm_done, (g * E1 + e) + 1)
                act.wait_ge(ym_done, (g * E1 + e) + 1)
                for t in range(2):
                    ins = nc.scalar.activation(hm[:, e % 2, t, :], bank[2 * (e % 2) + t][:, :], ACT.Relu,
                                               bias=b1m[:, e, t:t + 1])
                ins.then_inc(hm_evac, 1)

            def silu(g, par):
                act.wait_ge(acc_ready, g + 1)
                nc.scalar.activation(gate[:, par], acc[:, par], ACT.Silu).then_inc(gate_done, 1)

            def group(g, par, before, more):
                for e in range(1, E1):
                    hidden_relu(g, e)
                    if e == 1 and before:
                        silu(g - 1, 1 - par)
                if more:
                    keep_scores(g + 1, 1 - par)
                    hidden_relu(g + 1, 0)

            keep_scores(0, 0)
            hidden_relu(0, 0)
            group(0, 0, False, True)
            with act.Fori(0, ROUNDS_A - 1) as i:
                for n in range(2):
                    group(i * 2 + n + 1, 1 - n, True, True)
            group(NG - 1, 1, True, False)
            silu(NG - 1, 1)

        @block.tensor
        def _(pe):
            mm, turn = nc.tensor.matmul, nc.tensor.transpose
            pe.wait_ge(w_in, W_ALL)
            pe.wait_ge(idents, 1)

            def turn_rows_a(g, par):
                pe.wait_ge(st_ready, g + 1)
                for n, src in ((TX, xst), (TZ, zst)):
                    for t in range(GT):
                        ins = turn(bank[n][:, t * P:(t + 1) * P], src[:, par, t, :], ident[:, :])
                ins.then_inc(tr_done, 1)

            def projections(g, par):
                pe.wait_ge(t_evac, g + 1)
                pe.wait_ge(v_evac, g + 1)
                for t in range(GT):
                    ins = mm(bank[4][:, t * P:(t + 1) * P], xT[:, par, t * P:(t + 1) * P], w_v[:, :],
                             start=True, stop=True)
                ins.then_inc(v_done, 1)
                pe.wait_ge(q_evac, g + 1)
                mm(bank[2][:, :], w_q[:, :], xT[:, par], start=True, stop=True).then_inc(q_done, 1)
                pe.wait_ge(qk_evac, g + 1)
                mm(bank[3][:, :], w_k[:, :], xT[:, par], start=True, stop=True).then_inc(k_done, 1)
                pe.wait_ge(sc_evac, g + 1)
                mm(bank[5][0:E0, :], cent[:, :], zT[:, par], start=True, stop=True).then_inc(sc_done, 1)

            turn_rows_a(0, 0)
            pe.wait_ge(t_evac, 1)
            turn_rows_a(1, 1)
            projections(0, 0)
            with pe.Fori(0, ROUNDS_A - 1) as i:
                for par in range(2):
                    g = i * 2 + par + 1
                    pe.wait_ge(t_evac, g + 1)
                    turn_rows_a(g + 1, par)
                    projections(g, 1 - par)
            def max_unit(b, slot, u):
                for piece in range(2):
                    if 2 * (u // 2) == PIECES[piece].start and u % 2 == 0:
                        pe.wait_ge(stack_in, (2 * b + piece + 1) * PIECE_LOAD)
                first = isinstance(b, int) and b == 0
                to = MX_FIRST[u % 2] if first else MX_OF[u]
                pe.wait_ge(mx_free, b * 16 + u - (2 if first else MX_LAG[u]) + 3)
                qt = u % 2
                for n in range(2):
                    h = u // 2 * 2 + n
                    ins = mm(bank[to][:, n * S:(n + 1) * S], stacks[0:KROWS, slot, 0, h, qt * P:(qt + 1) * P],
                             stacks[0:KROWS, slot, 1, h, :], start=True, stop=True)
                ins.then_inc(mx_ready, 1)

            for u in range(WITH_A):
                max_unit(0, 0, u)
            projections(NG - 1, 1)
            for u in range(WITH_A, 16):
                max_unit(0, 0, u)

            pe.sem_inc(ot_done, 2)
            pe.sem_inc(pv_done, 8)
            pe.wait_ge(sc_evac, NG + 1)
            pe.wait_ge(v_evac, NG + 1)

            def logits(b, slot, h):
                pe.wait_ge(lt_free, b * H + h + 1)
                for kt in range(2):
                    ins = mm(bank[LT[h % 2]][:, kt * S:(kt + 1) * S],
                             stacks[0:MROW + 2, slot, 1, h, kt * P:(kt + 1) * P],
                             stacks[0:MROW + 2, slot, 0, h, :], start=True, stop=True)
                ins.then_inc(lt_ready, 1)

            def weigh(m, quad, par, kt):
                if kt == 0:
                    if quad == 0:
                        pe.wait_ge(v_ready, m // 4 + 1)
                    pe.wait_ge(lt_free, m * 4 + 6)
                    pe.wait_ge(pv_free, m + 1)
                for n in range(4):
                    h = quad * 4 + n
                    ins = mm(bank[PV][32 * n:32 * n + 32, 0:S], v_b[:, par, kt, h, :],
                             probs[:, h % 8, kt * S:(kt + 1) * S], start=kt == 0, stop=kt == 1,
                             tile_position=(0, 32 * n))
                if kt == 1:
                    ins.then_inc(pv_done, 1)

            def turn_o(b, par, quads):
                pe.wait_ge(pv_free, b * 4 + quads[-1] + 2)
                if quads[0] == 0:
                    pe.wait_ge(s_evac, b + 1)
                for quad in quads:
                    for qt in range(2):
                        ins = mm(bank[TR][:, (qt * 4 + quad) * QW:(qt * 4 + quad + 1) * QW],
                                 o_b[:, par, quad, qt * P:(qt + 1) * P], pick_sums, start=True, stop=True)
                if quads[-1] == 3:
                    ins.then_inc(ot_done, 1)

            def turn_v(b):
                pe.wait_ge(vals_ready, b + 1)
                for qt in range(2):
                    ins = turn(bank[TR][:, qt * P:(qt + 1) * P], vals[:, qt, :], ident[:, :])
                ins.then_inc(vt_done, 1)

            def project(b):
                pe.wait_ge(vt_evac, b + 1)
                for qt in range(2):
                    ins = mm(bank[TR][:, qt * P:(qt + 1) * P], vT[:, qt, :], w_o[:, :], start=True, stop=True)
                ins.then_inc(s_done, 1)

            def count(k):
                pe.wait_ge(cnt_ready, k + 1)
                mm(bank[CNT][:, 0:REP], cnt[:, 0:1].broadcast_to([P, P]), pick[:, :],
                   start=True, stop=True).then_inc(cnt_sum, 1)

            def turn_max(b):
                pe.wait_ge(nm_ready, b + 1)
                turn(bank[TR][:, :].bitcast(BF16)[:, 6 * P:7 * P], nm[:, :], ident_b[:, :]).then_inc(nm_tr, 1)

            def batch(b, par, before, ahead, ahead2, half=None, e=None, beside=None):
                pe.wait_ge(nm_in, (b + 1) * 32)
                for h in range(H):
                    logits(b, par, h)
                    if ahead:
                        for u in UNITS[h]:
                            max_unit(b + 1, 1 - par, u)
                    if h % 4 >= 2:
                        if h > 3:
                            weigh(b * 4 + h // 4 - 1, h // 4 - 1, par, h % 4 - 2)
                        elif before:
                            weigh(b * 4 - 1, 3, 1 - par, h % 4 - 2)
                    if half is not None and h - SUM_AFTER in COUNT_AT[half]:
                        count((b - 1) * ROUNDS + COUNT_AT[half].index(h - SUM_AFTER))
                    if before and h in TURN_AT:
                        turn_o(b - 1, 1 - par, TURN_AT[h])
                    if before and h == 10:
                        turn_v(b - 1)
                    if before and h == 12:
                        project(b - 1)
                    if ahead and h == 12:
                        turn_max(b + 1)
                    if beside and h in beside:
                        beside[h]()
                if ahead2:
                    for u in range(2):
                        max_unit(b + 2, par, u)
                if half == 1:
                    pe.wait_ge(fin_ready, e + 1)
                    mm(bank[CNT][:, 0:1], nge[:, :], cnt[:, 1:2], start=True, stop=False)
                    mm(bank[CNT][:, 0:1], neq[:, :], cnt[:, 2:3], start=False, stop=True).then_inc(fin_sum, 1)

            turn_max(0)
            for u in range(2):
                max_unit(1, 1, u)
            batch(0, 0, False, True, True)
            with pe.Fori(0, PAIRS - 1) as i:
                batch(i * 2 + 1, 1, True, True, True, 0, i)
                batch(i * 2 + 2, 0, True, True, True, 1, i)
            batch(B - 3, 1, True, True, True, 0, PAIRS - 1)
            batch(B - 2, 0, True, True, False, 1, PAIRS - 1)

            def turn_experts():
                pe.wait_ge(eid_ready, PAIRS)
                for c in range(GT):
                    ins = turn(bank[CNT][:, :].bitcast(F16)[:, c * P:(c + 1) * P], eid[:, c * P:(c + 1) * P],
                               ident_h[:, :])
                ins.then_inc(eid_tr, 1)

            def add_places():
                pe.wait_ge(hot_ready, 1)
                hot_f = hot[:, :, :].rearrange("p e t -> p (e t)")
                mm(bank[0][:, 0:E0 * NT], tri[:, :], hot_f, start=True, stop=True)
                mm(bank[1][:, 0:E0 * NT], ones_h[:, 0:P], hot_f, start=True, stop=True).then_inc(pos_mm, 1)

            batch(B - 1, 1, True, False, False, beside={2: turn_experts, 4: add_places})
            for kt in range(2):
                weigh(4 * B - 1, 3, 1, kt)
            for t in range(NT):
                if t % LOW_TILES == 0:
                    pe.wait_ge(low_ready, t // LOW_TILES + 1)
                ins = mm(bank[7][:, 0:2 * NT], at_low[:, t, :], at_high[:, t, 1:3, :], start=t == 0, stop=t == NT - 1)
            ins.then_inc(idx_mm, 1)
            turn_o(B - 1, 1, (0, 1, 2, 3))
            turn_v(B - 1)
            project(B - 1)

            def turn_rows(e, par, round_):
                pe.wait_ge(zl_in[par], (round_ + 1) * ROWS)
                for t in range(GT):
                    ins = turn(bank[0][:, t * P:(t + 1) * P], zl[:, par, t, :], ident[:, :])
                ins.then_inc(zt_done, 1)

            def expert(e, par, round_, more):
                pe.wait_ge(nt_ready, e + 1)
                pe.wait_ge(e_in[par], (round_ + 1) * E_LOADS)
                for ft in range(4):
                    pe.wait_ge(h_evac, e * 4 + ft + 1)
                    mm(bank[1 + ft % 2][:, :], w1e[:, par, ft * P:(ft + 1) * P], nT[:, par],
                       start=True, stop=True).then_inc(h_done, 1)
                if more:
                    turn_rows(e + 1, 1 - par, round_ + par)
                pe.wait_ge(h_evac, e * 4 + 6)
                pe.wait_ge(y_evac, e + 1)
                for t in range(GT):
                    for ft in range(4):
                        ins = mm(bank[3 + par][:, t * P:(t + 1) * P], hT[:, par, ft, t * P:(t + 1) * P],
                                 w2e[:, par, ft, :], start=ft == 0, stop=ft == 3)
                ins.then_inc(y_done, 1)

            pe.wait_ge(pv_free, 4 * B + 1)
            turn_rows(0, 0, 0)
            with pe.Fori(0, E0 // 2 - 1) as i:
                for par in range(2):
                    expert(i * 2 + par, par, i, True)
            expert(E0 - 2, 0, E0 // 2 - 1, True)
            expert(E0 - 1, 1, E0 // 2 - 1, False)

            pe.wait_ge(s_evac, B + 1)
            mm(bank[6][:, 0:P], wqkv8[:, 0, :], wqkv8[:, 1, :], start=True, stop=True)
            mm(bank[6][:, P:2 * P], wqkv8[:, 2, :], wqkv8[:, 3, :], start=True, stop=True).then_inc(w8_done, 1)
            pe.sem_inc(tr1_done, 2)
            pe.wait_ge(w8_evac, 2)

            def turn_x1(g, par):
                pe.wait_ge(st1_ready, g + 1)
                for t in range(GT):
                    ins = turn(bank[T1[par]][:, t * P:(t + 1) * P], xst[:, par, t, :], ident[:, :])
                ins.then_inc(tr1_done, 1)

            def products_x1(g, par):
                pe.wait_ge(x1_evac, g + 1)
                pe.wait_ge(yg_evac, g + 1)
                for t in range(GT):
                    ins = mm(bank[(Y1, G1)[t // 2][par]][:, t % 2 * (P + E1):(t % 2 + 1) * (P + E1)],
                             x1T[:, par, t * P:(t + 1) * P], bd_ag[:, :], start=True, stop=True)
                ins.then_inc(yg_done, 1)

            turn_x1(0, 0)
            turn_x1(1, 1)
            products_x1(0, 0)
            with pe.Fori(0, ROUNDS_A - 1) as i:
                for par in range(2):
                    g = i * 2 + par + 1
                    products_x1(g, 1 - par)
                    turn_x1(g + 1, par)
            products_x1(NG - 1, 1)
            for r in range(B // 4):
                if r == 0:
                    pe.wait_ge(vrhs_ready, 1)
                    pe.wait_ge(yg_evac, NG + 2)
                mm(bank[1 + r][:, :], ones_f[:, :], vrhs[:, 4 * r:4 * r + 4, :].rearrange("p c n -> p (c n)"),
                   start=True, stop=True).then_inc(vs_mm, 1)
            pe.wait_ge(vs_evac, B // 4)
            pe.wait_ge(m_in, 32)
            pe.sem_inc(ym_done, 2)

            def turn_scores(g, par):
                pe.wait_ge(sct_in, g + 1)
                for t in range(GT):
                    ins = turn(bank[6][0:E1, t * P:(t + 1) * P], scm[:, par, t, :], ident[:, :])
                ins.then_inc(sct_done, 1)

            def hidden(g, e):
                pe.wait_ge(hm_evac, g * E1 + e + 1)
                for t in range(2):
                    ins = mm(bank[2 * (e % 2) + t][:, :], w1m[:, e, t * P:(t + 1) * P],
                             flat(xT_all[:, bass.ds(g, 1), :]), start=True, stop=True)
                ins.then_inc(hm_done, 1)

            def group(g, par, more):
                pe.wait_ge(sct_evac, g + 1)
                for t in range(GT):
                    ins = mm(bank[7][:, t * P:(t + 1) * P], scT[:, par, t * P:(t + 1) * P], b2m[:, :],
                             start=True, stop=True)
                ins.then_inc(b2_done, 1)
                for e in range(E1):
                    if e + 1 < E1:
                        hidden(g, e + 1)
                    elif more:
                        turn_scores(g + 1, 1 - par)
                        hidden(g + 1, 0)
                    pe.wait_ge(hm_evac, g * E1 + e + 3)
                    pe.wait_ge(ym_free, g * E1 + e + 1)
                    for t in range(GT):
                        for ft in range(2):
                            ins = mm(bank[4 + e % 2][:, t * P:(t + 1) * P], hm[:, e % 2, ft, t * P:(t + 1) * P],
                                     w2m[:, e, ft, :], start=ft == 0, stop=ft == 1)
                    ins.then_inc(ym_done, 1)

            turn_scores(0, 0)
            hidden(0, 0)
            group(0, 0, True)
            with pe.Fori(0, ROUNDS_A - 1) as i:
                for n in range(2):
                    group(i * 2 + n + 1, 1 - n, True)
            group(NG - 1, 1, False)

        @block.vector
        def _(dve):
            ch = Chain(dve, chain_s)
            v = nc.vector
            v.memset(ones_h[:, :], 1.0)
            v.memset(ones_f[:, :], 1.0)
            v.memset(eid[:, :], 0.0)
            v.memset(nm[:, :], 0.0)
            v.memset(avail[:, :], 1.0)
            dve.sem_inc(v_evac, 1)
            dve.sem_inc(split_done, 2)

            def statistics():
                s6 = [stat6[:, :, k] for k in range(6)]
                ch.link(v.tensor_tensor(mean[:, :], s6[1], s6[4], ALU.add))
                ch.link(v.tensor_scalar(mean[:, :], mean[:, :], 0.5, None, ALU.mult))
                ch.link(v.tensor_tensor(spare[:, :], s6[1], s6[4], ALU.subtract))
                ch.link(v.tensor_tensor(spare[:, :], spare[:, :], spare[:, :], ALU.mult))
                ch.link(v.tensor_tensor(var[:, :], s6[2], s6[5], ALU.add))
                ch.link(v.scalar_tensor_tensor(var[:, :], spare[:, :], D / 4.0, var[:, :], ALU.mult, ALU.add))
                ch.link(v.tensor_scalar(var[:, :], var[:, :], 1.0 / D, None, ALU.mult))

            def both_scales(ready, rooted, n=2):
                sq, rt, sc = squares[:, 0:n * NT], roots_all[:, 0:n * NT], scales[:, 0:n * NT]
                ch.link(v.tensor_scalar(sq[:, 0:NT], var[:, :], EPS, None, ALU.add))
                if n == 2:
                    ch.link(v.tensor_scalar(sq[:, NT:], var[:, :], 1 + EPS, EPS * EPS, ALU.mult, ALU.add))
                v.tensor_copy(rt, sq).then_inc(ready, 1)
                dve.wait_ge(rooted, 1)
                ch.link(v.reciprocal(sc, rt))
                ch.link(v.tensor_tensor(rt, sc, sc, ALU.mult))
                ch.link(v.tensor_tensor(rt, rt, sq, ALU.mult))
                ch.link(v.tensor_scalar(rt, rt, -0.5, 1.5, ALU.mult, ALU.add))
                ch.link(v.tensor_tensor(sc, sc, rt, ALU.mult))

            for g in range(NG):
                dve.wait_ge(x_in[g], 16)
                for t in range(g * GT, (g + 1) * GT):
                    ins = v.bn_stats(stat6[:, t, :], x_all[:, t, :])
            ch.link(ins)
            statistics()
            both_scales(var_ok, root_ok)
            dve.wait_ge(w_in, W_ALL)
            v.tensor_copy(ident_b[:, :], ident[:, :])
            v.tensor_copy(ident_h[:, :], ident[:, :]).then_inc(idents, 1)

            dve.sem_inc(mx_free, 2)

            def row_max(b, u):
                dve.wait_ge(mx_ready, b * 16 + u + 1)
                hp, qt = u // 2, u % 2
                of = MX_FIRST[u % 2] if isinstance(b, int) and b == 0 else MX_OF[u]
                return v.tensor_reduce(mx[:, 2 * hp:2 * hp + 2, qt],
                                       bank[of][:, :].rearrange("p (h k) -> p h k", h=2),
                                       AX.X, ALU.max).then_inc(mx_free, 1)

            def normalise(g, par):
                for dst, by in ((xst, rstd), (zst, zscale)):
                    for t in range(GT):
                        at = bass.ds(g * GT + t, 1)
                        ins = v.tensor_scalar(dst[:, par, t, :], flat(x_all[:, at, :]), mean[:, at], by[:, at],
                                              ALU.subtract, ALU.mult)
                ins.then_inc(st_ready, 1)

            def keep_v_and_split(g, par, round_, more, beside=((), (), ())):
                if more:
                    dve.wait_ge(tr_done, g + 1)
                    dve.wait_ge(xn_copied, g + 3)
                    dve.wait_ge(z_out[par], (round_ + 1) * 16)
                    normalise(g + 2, par)
                dve.wait_ge(v_done, g + 1)
                v.tensor_tensor(v_all[:, bass.ds(g * GT, GT), :],
                                bank[4][:, :].rearrange("p (t n) -> p t n", t=GT),
                                b_v[:, :].unsqueeze(1).broadcast_to([P, GT, P]), ALU.add).then_inc(v_evac, 1)
                for u in beside[0]:
                    row_max(0, u)
                dve.wait_ge(qk_evac, g + 2)
                v.tensor_tensor(qkf[:, par], qkf[:, par], parts[:, par, 0], ALU.subtract).then_inc(rest1, 1)
                for u in beside[1]:
                    row_max(0, u)
                dve.wait_ge(part2, g + 1)
                v.tensor_tensor(parts[:, par, 2], qkf[:, par], parts[:, par, 1],
                                ALU.subtract).then_inc(split_done, 1)
                for u in beside[2]:
                    row_max(0, u)

            for par in range(2):
                normalise(par, par)
            with dve.Fori(0, ROUNDS_A - 1) as i:
                for par in range(2):
                    keep_v_and_split(i * 2 + par, par, i, True)
            keep_v_and_split(NG - 2, 0, None, False, ((0, 1), (), ()))
            keep_v_and_split(NG - 1, 1, None, False, ((2, 3, 4), (5, 6), range(7, 16)))

            def split_max(b):
                dve.wait_ge(mx_free, b * 16 + 18)
                mx_f, hi, lo = mx[:, :, :].rearrange("p h c -> p (h c)"), nm[:, 0:2 * H], nm[:, 2 * H:4 * H]
                ch.link(v.tensor_scalar(hi, mx_f, -1.0, None, ALU.mult))
                v.scalar_tensor_tensor(lo, mx_f, -1.0, hi, ALU.mult,
                                       ALU.subtract).then_inc(nm_ready, 1)

            def values(b):
                dve.wait_ge(ot_done, b + 3)
                o = bank[TR][:, 0:8 * QW].rearrange("p (h n) -> p h n", n=HD + 1)
                ch.link(v.reciprocal(rec[:, :, :].rearrange("p q h -> p (q h)"), o[:, :, HD]))
                v.tensor_tensor(vals[:, :, :].rearrange("p q (h n) -> p (q h) n", n=HD), o[:, :, 0:HD],
                                rec[:, :, :].rearrange("p q h -> p (q h)").unsqueeze(2).broadcast_to([P, 2 * H, HD]),
                                ALU.mult).then_inc(vals_ready, 1)

            def begin_high(e):
                v.tensor_copy(MINUS_T, thr[:, 0:1])
                v.tensor_copy(BASE, thr[:, 1:2])
                v.memset(L, 0.0)
                v.scalar_tensor_tensor(khi[:, :], flat(keys[:, 0, bass.ds(e, 1), :]), HALF, avail[:, :],
                                       ALU.mult, ALU.mult).then_inc(thr_ready, 1)

            def begin_low(e, k):
                v.tensor_copy(MINUS_T, thr[:, ROUNDS:ROUNDS + 1])
                v.tensor_copy(BASE, thr[:, ROUNDS + 1:ROUNDS + 2])
                ch.link(v.tensor_scalar(QUOTA, L, -1.0, -DONE[ROUNDS] * HALF, ALU.mult, ALU.add))
                v.memset(L, 0.0)
                v.scalar_tensor_tensor(key2[:, :], khi[:, :], QUOTA, flat(keys[:, 1, bass.ds(e, 1), :]),
                                       ALU.subtract, ALU.add).then_inc(thr_ready, 1)
                dve.wait_ge(thr_ready, k + 1)

            def next_digit(k, r, half):
                w = (HALF, 1.0)[half] * STEPS[r]
                ch.need()
                dve.wait_ge(cnt_sum, k + 1)
                ch.link(v.tensor_scalar(junk16[:, :], bank[CNT][:, 0:REP], ENOUGH, None, ALU.is_ge, ALU.add,
                                        accum_out=DIG))
                if r < ROUNDS - 1:
                    v.scalar_tensor_tensor(MINUS_T, DIG, -w, BASE, ALU.mult, ALU.add).then_inc(thr_ready, 1)
                ch.mark(v.scalar_tensor_tensor(L, DIG, -w, L, ALU.mult, ALU.add))

            def next_base(r, half):
                ch.need()
                if r < ROUNDS - 2:
                    col = half * ROUNDS + r + 2
                    ch.mark(v.tensor_tensor(BASE, L, thr[:, col:col + 1], ALU.add))

            def choose(e, beside=()):
                units = iter(beside)

                def unit():
                    for b, u in [next(units, (None, None))]:
                        if u is not None:
                            row_max(b, u)
                ch.link(v.tensor_scalar(T, L, -1.0, -DONE[ROUNDS], ALU.mult, ALU.add))
                v.tensor_scalar(ge[:, :], key2[:, :], T, None, ALU.is_ge, ALU.add, accum_out=cnt[:, 1:2])
                v.tensor_scalar(eq[:, :], key2[:, :], T, None, ALU.is_equal, ALU.add,
                                accum_out=cnt[:, 2:3]).then_inc(fin_ready, 1)
                unit()
                dve.wait_ge(fin_ready, e + 1)
                ch.mark(v.tensor_tensor_scan(pre[:, :], ones_h[:, :], eq[:, :], 0.0, ALU.mult, ALU.add))
                unit()
                dve.wait_ge(fin_sum, e + 1)
                ch.link(v.tensor_scalar(QUOTA, bank[CNT][:, 0:1], float(CAP), None, ALU.add))
                v.scalar_tensor_tensor(pre[:, :], pre[:, :], QUOTA, eq[:, :], ALU.is_gt, ALU.mult)
                ch.mark(v.tensor_tensor(avail[:, :], avail[:, :], ge[:, :], ALU.subtract))
                unit()
                ch.need()
                ch.mark(v.tensor_tensor(avail[:, :], avail[:, :], pre[:, :], ALU.add))
                unit()
                ch.need()
                v.tensor_tensor(eid[:, :], eid[:, :], avail[:, :], ALU.add).then_inc(eid_ready, 1)

            def make_keys():
                dve.wait_ge(score_in, 16 * 2)
                bits = key_f[:, :].bitcast(I32)
                flip = key2[:, 0:S].bitcast(I32)
                ch.link(v.tensor_scalar(flip, bits, 31, -2147483648, ALU.arith_shift_right, ALU.bitwise_or))
                ch.link(v.tensor_tensor(flip, flip, bits, ALU.bitwise_xor))
                halves = key2[:, 0:S].bitcast(U16).rearrange("p (f w) -> p w f", w=2)
                v.tensor_copy(key_h[:, 1, :], halves[:, 0, :])
                v.tensor_copy(key_h[:, 0, :], halves[:, 1, :]).then_inc(key_ready, 1)

            def batch(b, before, ahead, ahead2, half=None, e=None, beside=None):
                for h in range(H):
                    if ahead and h:
                        for u in UNITS[h]:
                            row_max(b + 1, u)
                    if half == 0 and h == 0:
                        begin_high(e)
                    if half is not None and h - SUM_AFTER - 1 in COUNT_AT[half]:
                        next_base(COUNT_AT[half].index(h - SUM_AFTER - 1), half)
                    if half is not None and h - SUM_AFTER in COUNT_AT[half]:
                        r = COUNT_AT[half].index(h - SUM_AFTER)
                        next_digit((b - 1) * ROUNDS + r, r, half)
                    if beside and h in beside:
                        beside[h]()
                    if before and h == 7:
                        values(b - 1)
                    if ahead and h == 11:
                        split_max(b + 1)
                if half == 0:
                    begin_low(e, b * ROUNDS)
                units = [(b + 2, u) for u in range(EARLY)] if ahead2 else []
                if half == 1:
                    choose(e, units)
                else:
                    for unit in units:
                        row_max(*unit)

            split_max(0)
            for u in range(EARLY):
                row_max(1, u)
            make_keys()
            batch(0, False, True, True)
            dve.wait_ge(keys_in, 16 * NG)
            with dve.Fori(0, PAIRS - 1) as i:
                ch.loop(i, SEARCH_LINKS)
                batch(i * 2 + 1, True, True, True, 0, i)
                batch(i * 2 + 2, True, True, True, 1, i)
            ch.end(PAIRS - 1)
            batch(B - 3, True, True, True, 0, PAIRS - 1)
            batch(B - 2, True, True, False, 1, PAIRS - 1)

            def experts_hot():
                dve.wait_ge(eid_tr, 1)
                ch.link(v.tensor_copy(eidT[:, :].rearrange("p (g c) -> p c g", c=GT),
                                      bank[CNT][:, :].bitcast(F16)[:, 0:GT * P].rearrange(
                                          "p (c g j) -> p c g j", c=GT, j=REP)[:, :, :, 0]))
                for e in range(E0):
                    ins = v.tensor_scalar(hot[:, e, :], eidT[:, :], float(e), None, ALU.is_equal)
                ins.then_inc(hot_ready, 1)

            def places():
                dve.wait_ge(pos_mm, 1)
                ch.link(v.tensor_copy(posa[:, :], bank[1][:, 0:E0 * NT]))
                ch.link(v.tensor_tensor_scan(tot[:, :], ones_h[:, 0:E0 * NT], posa[:, :], 0.0, ALU.mult, ALU.add))
                ch.link(v.tensor_tensor(posa[:, :], tot[:, :], posa[:, :], ALU.subtract))
                ch.link(v.tensor_tensor(posa[:, :], bank[0][:, 0:E0 * NT], posa[:, :], ALU.add))
                ch.link(v.tensor_tensor(posa[:, :], posa[:, :], hot[:, :, :].rearrange("p e t -> p (e t)"), ALU.mult))
                ch.link(v.tensor_reduce(pos_f[:, :], posa[:, :].rearrange("p (e t) -> p t e", e=E0), AX.X, ALU.add))
                ch.link(v.tensor_copy(pos[:, :], pos_f[:, :]))
                v.tensor_scalar(lo_i[:, :], pos[:, :], P - 1, None, ALU.bitwise_and)
                ch.link(v.tensor_scalar(hi_i[:, :], pos[:, :], int(np.log2(P)), None, ALU.arith_shift_right))
                v.tensor_copy(lo_f[:, :], lo_i[:, :])
                ch.link(v.tensor_copy(hi_f[:, :], hi_i[:, :]))

            def by_place():
                ch.link(v.tensor_tensor(at_high[:, :, 0, :], iota[:, 0:NT].unsqueeze(1).broadcast_to([P, NT, NT]),
                                        hi_f[:, :].unsqueeze(2).broadcast_to([P, NT, NT]), ALU.is_equal))
                v.tensor_scalar(at_high[:, :, 1, :], at_high[:, :, 0, :], token[:, 0:1], None, ALU.mult)
                v.tensor_tensor(at_high[:, :, 2, :], at_high[:, :, 0, :],
                                iota[:, 0:NT].unsqueeze(2).broadcast_to([P, NT, NT]), ALU.mult)
                for n in range(NT // LOW_TILES):
                    at = slice(n * LOW_TILES, (n + 1) * LOW_TILES)
                    v.tensor_tensor(at_low[:, at, :], iota.unsqueeze(1).broadcast_to([P, LOW_TILES, P]),
                                    lo_f[:, at].unsqueeze(2).broadcast_to([P, LOW_TILES, P]),
                                    ALU.is_equal).then_inc(low_ready, 1)

            batch(B - 1, True, False, False, beside={4: experts_hot, 5: places, 9: by_place})
            dve.wait_ge(idx_mm, 1)
            ch.link(v.tensor_copy(lo_f[:, :], bank[7][:, 0:NT]))
            v.scalar_tensor_tensor(idx[:, :], bank[7][:, NT:2 * NT], float(P), lo_f[:, :], ALU.mult,
                                   ALU.add).then_inc(idx_ready, 1)
            values(B - 1)

            dve.sem_inc(y_evac, 2)

            def expert(e, par, round_):
                dve.wait_ge(y_done, e + 1)
                if round_ is not None:
                    dve.wait_ge(spread[par], round_ * ROWS)
                v.tensor_tensor(ho[:, par], bank[3 + par][:, :].rearrange("p (t n) -> p t n", t=GT),
                                b2e[:, par].unsqueeze(1).broadcast_to([P, GT, D]), ALU.add).then_inc(y_evac, 1)

            for par in range(2):
                expert(par, par, None)
            with dve.Fori(1, E0 // 2) as i:
                for par in range(2):
                    expert(i * 2 + par, par, i)

            v.tensor_copy(bd_ag[:, P:P + E1], w_g)
            dve.wait_ge(w8_done, 1)
            v.tensor_tensor(bd_ag[:, 0:P], bank[6][:, 0:P], block_mask[:, :], ALU.mult).then_inc(w8_evac, 1)
            v.tensor_tensor(bd_v[:, :], bank[6][:, P:2 * P], block_mask[:, :], ALU.mult).then_inc(w8_evac, 1)
            dve.wait_ge(bias_done, B)
            with dve.Fori(0, ROUNDS_A) as i:
                ch.loop(i, 3)
                g = i * 2
                even, odd = bass.ds(g * GT, GT), bass.ds((g + 1) * GT, GT)
                dve.wait_ge(silu_done, g + 2)
                ch.mark(v.tensor_tensor(s_all[:, odd, :], s_all[:, odd, :], routed[:, odd, :], ALU.mult))
                dve.wait_ge(sg_ready, i + 1)
                ch.link(v.tensor_tensor(x_all[:, even, :], x_all[:, even, :], s_all[:, even, :], ALU.add))
                ch.mark(v.tensor_tensor(x_all[:, odd, :], x_all[:, odd, :], s_all[:, odd, :], ALU.add))
                for t in range(2 * GT):
                    if t == GT:
                        ch.need()
                    one = bass.ds(g * GT + t, 1)
                    ins = v.bn_stats(flat(stat6[:, one, :]), flat(x_all[:, one, :]))
            ch.end(ROUNDS_A)
            ch.link(v.memset(small[:, :], 0.0))
            statistics()
            both_scales(var1_ok, root1_ok, 1)

            dve.sem_inc(yg_evac, 2)

            def normalise_x1(g, par):
                dve.wait_ge(tr1_done, g + 1)
                for t in range(GT):
                    one = bass.ds(g * GT + t, 1)
                    ins = v.tensor_scalar(xst[:, par, t, :], flat(x_all[:, one, :]), mean[:, one], rstd[:, one],
                                          ALU.subtract, ALU.mult)
                ins.then_inc(st1_ready, 1)

            def diagonal(g, par, more):
                at = bass.ds(g * GT, GT)
                dve.wait_ge(yg_done, g + 1)
                yg = [bank[k[par]][:, 0:2 * (P + E1)].rearrange("p (t n) -> p t n", t=2) for k in (Y1, G1)]
                for k in range(2):
                    ins = v.tensor_tensor(zst[:, par, 2 * k:2 * k + 2, :], yg[k][:, :, 0:P],
                                          xst[:, par, 2 * k:2 * k + 2, :], ALU.mult)
                ch.link(ins)
                if more:
                    normalise_x1(g + 2, par)
                v.tensor_reduce(ds[:, at, :], zst[:, par].rearrange("p t (h n) -> p t h n", n=HD), AX.X, ALU.add)
                for k in range(2):
                    ins = v.tensor_copy(gl[:, bass.ds(g * GT + 2 * k, 2), :], yg[k][:, :, P:P + E1])
                ins.then_inc(yg_evac, 1)

            for par in range(2):
                normalise_x1(par, par)
            with dve.Fori(0, ROUNDS_A - 1) as i:
                ch.loop(i, 2)
                for par in range(2):
                    diagonal(i * 2 + par, par, True)
            ch.end(ROUNDS_A - 1)
            for par in range(2):
                diagonal(NG - 2 + par, par, False)
            ch.link(v.memset(small[:, :], 0.0))
            dve.wait_ge(x1_copied, NG + 2)

            row = lambda t: t[:, :].unsqueeze(2).broadcast_to([P, NT, E1])
            in_row = lambda n: key2[:, n * NT * E1 // 2:(n + 2) * NT * E1 // 2].rearrange("p (t e) -> p t e", t=NT)
            first, second, rest = in_row(0), in_row(2), khi[:, 0:NT * E1].rearrange("p (t e) -> p t e", t=NT)
            order = first_f.unsqueeze(1).broadcast_to([P, NT, E1])

            def take_largest(src, to, largest):
                ch.link(v.tensor_reduce(largest[:, :], src, AX.X, ALU.max))
                ch.link(v.tensor_tensor(to, src, row(largest), ALU.is_equal))
                ch.link(v.tensor_tensor(to, to, order, ALU.mult))
                ch.link(v.tensor_reduce(small2[:, :], to, AX.X, ALU.max))
                ch.link(v.tensor_tensor(to, order, row(small2), ALU.is_equal))

            take_largest(gl, first, small)
            ch.link(v.scalar_tensor_tensor(rest, first, -3e38, gl, ALU.mult, ALU.add))
            v.tensor_tensor(gl, gl, row(small), ALU.subtract).then_inc(lg_ready, 1)
            take_largest(rest, second, small3)
            ch.link(v.tensor_tensor(first, first, second, ALU.add))
            dve.wait_ge(exp_done, 1)
            ch.link(v.tensor_tensor(gl, gl, first, ALU.mult))
            ch.link(v.tensor_reduce(small[:, :], gl, AX.X, ALU.add))
            ch.link(v.reciprocal(small[:, :], small[:, :]))
            ch.link(v.tensor_tensor(gl, gl, row(small), ALU.mult))

            def batch_softmax():
                by_batch = ds.rearrange("p (c f) h -> p f h c", f=2)
                hm2 = hmax[:, :].rearrange("p (f h) -> p f h", f=2)
                wide = hm2.unsqueeze(1).broadcast_to([P, B, 2, H])
                ds4 = ds.rearrange("p (c f) h -> p c f h", f=2)
                ch.link(v.tensor_reduce(hm2, by_batch, AX.X, ALU.max))
                v.tensor_tensor(ds4, ds4, wide, ALU.subtract).then_inc(lg_ready, 1)
                dve.wait_ge(exp_done, 2)
                ch.link(v.tensor_reduce(hm2, by_batch, AX.X, ALU.add))
                ch.link(v.reciprocal(hmax[:, :], hmax[:, :]))
                ch.link(v.tensor_tensor(ds4, ds4, wide, ALU.mult))

            dve.sem_inc(ym_free, 2)

            def give_scores(g, par):
                v.tensor_copy(scm[:, par], gl[:, bass.ds(g * GT, GT), :]).then_inc(sct_in, 1)

            def finish(g, par):
                dve.wait_ge(stored, (g + 1) * 16)
                for c in range(2):
                    pr = ds[:, bass.ds((g * 2 + c) * 2, 2), :].unsqueeze(3).broadcast_to([P, 2, H, HD])
                    vs = vsum[:, bass.ds(g * 2 + c, 1), :].broadcast_to([P, 2, D]).rearrange(
                        "p f (h n) -> p f h n", n=HD)
                    ins = v.tensor_tensor(outs[:, par, 2 * c:2 * c + 2, :].rearrange("p f (h n) -> p f h n", n=HD),
                                          pr, vs, ALU.mult)
                ch.link(ins)
                dve.wait_ge(gate_done, g + 1)
                ch.link(v.tensor_tensor(outs[:, par], outs[:, par], gate[:, par], ALU.mult))
                v.tensor_tensor(outs[:, par], outs[:, par], x_all[:, bass.ds(g * GT, GT), :],
                                ALU.add).then_inc(out_ready, 1)

            def group(g, par, before, more):
                dve.wait_ge(b2_done, g + 1)
                ch.link(v.tensor_copy(acc[:, par].rearrange("p t n -> p (t n)"), bank[7][:, :]))
                if more:
                    give_scores(g + 1, 1 - par)
                for e in range(E1):
                    dve.wait_ge(ym_done, g * E1 + e + 3)
                    for t in range(GT):
                        ins = v.scalar_tensor_tensor(acc[:, par, t, :], bank[4 + e % 2][:, t * P:(t + 1) * P],
                                                     scm[:, par, t, e:e + 1], acc[:, par, t, :], ALU.mult, ALU.add)
                    ins.then_inc(ym_free, 1)
                    dve.wait_ge(ym_free, g * E1 + e + 3)
                    if e == 3 and before:
                        finish(g - 1, 1 - par)
                v.sem_inc(acc_ready, 1)

            give_scores(0, 0)
            batch_softmax()
            dve.wait_ge(vs_evac, B // 4)
            group(0, 0, False, True)
            with dve.Fori(0, ROUNDS_A - 1) as i:
                ch.loop(i, 6)
                for n in range(2):
                    group(i * 2 + n + 1, 1 - n, True, True)
            ch.end(ROUNDS_A - 1)
            group(NG - 1, 1, True, False)
            finish(NG - 1, 1)


_INS = ["x", "pack", "pack_h", "b_v", "b_o", "w1", "b1", "w2", "b2", "w8", "w1m", "w2m", "b2m"]


def kernel(**inputs):
    import concourse.bacc as bacc
    from concourse.bass_utils import run_bass_kernel_spmd

    a = {k: np.asarray(t) for k, t in inputs.items()}
    w = a["L0_attn_w_qkv"].reshape(H, 3, HD, D)
    bias = a["L0_attn_b_qkv"].reshape(H, 3, HD)
    rep = lambda m: np.tile(m, (1, H))
    lay = {
        "x": a["L0_attn_x"].reshape(TOK, D),
        "w_q": w[:, 0].reshape(D, D).T, "w_k": w[:, 1].reshape(D, D).T, "w_v": w[:, 2].reshape(D, D).T,
        "w_o": a["L0_attn_w_o"].T,
        "b_qk": bias[:, 0:2].transpose(0, 2, 1).reshape(D, 2), "b_v": bias[:, 2].reshape(1, D),
        "b_o": a["L0_attn_b_o"].reshape(1, D),
        "cent": a["L0_ffn_centroids"].T, "ln_gb": np.stack([a["L0_ffn_ln_g"], a["L0_ffn_ln_b"]], 1),
        "w1": a["L0_ffn_w1"].transpose(1, 0, 2),
        "b1": a["L0_ffn_b1"].reshape(E0, 4, P).transpose(2, 0, 1),
        "w2": a["L0_ffn_w2"].reshape(E0, 4, P, D).transpose(2, 0, 1, 3).reshape(P, E0, 4 * D),
        "b2": a["L0_ffn_b2"],
        "w8": np.concatenate([rep(a["L1_attn_Wq"]), rep(a["L1_attn_Wk"]), rep(a["L1_attn_Wv"]),
                              rep(np.eye(HD, dtype=np.float32))], 1),
        "w_g": a["L1_ffn_Wg"],
        "w1m": a["L1_ffn_W1"].transpose(1, 0, 2).reshape(D, E1 * H1),
        "b1m": a["L1_ffn_b1"].reshape(E1, 2, P).transpose(2, 0, 1).reshape(P, 2 * E1),
        "w2m": a["L1_ffn_W2"].reshape(E1, 2, P, D).transpose(2, 0, 1, 3).reshape(P, E1 * 2 * D),
        "b2m": a["L1_ffn_b2"],
        **host_constants(),
    }
    lay["pack"] = np.concatenate([lay[n] for n in PACK], 1)
    lay["pack_h"] = np.concatenate([lay[n] for n in PACK_H], 1)
    nc = bacc.Bacc("TRN2", target_bir_lowering=False, num_devices=1)
    arrays, aps = {}, {}
    for name in _INS:
        t = np.ascontiguousarray(lay[name])
        arrays[f"in_{name}"] = t
        aps[name] = nc.dram_tensor(f"in_{name}", t.shape, mybir.dt.from_np(t.dtype), kind="ExternalInput").ap()
    out = nc.dram_tensor("out_0", (TOK, D), F32, kind="ExternalOutput").ap()
    two_layers(nc, aps, out)
    got = run_bass_kernel_spmd(nc, [arrays], core_ids=[0])
    return got.results[0]["out_0"].reshape(B, S, D)
```
